# Optimizing a Trainium2 kernel written in Bass

```python
import numpy as np
import jax
import jax.numpy as jnp

def _softmax(x, axis=-1):
    return jax.nn.softmax(x, axis=axis)

def _gelu(x):
    return jax.nn.gelu(x, approximate=True)

def _silu(x):
    return jax.nn.silu(x)

def _sigmoid(x):
    return jax.nn.sigmoid(x)

def _layernorm(x, axis=-1, eps=1e-05):
    m = jnp.mean(x, axis=axis, keepdims=True)
    v = jnp.var(x, axis=axis, keepdims=True)
    return (x - m) / jnp.sqrt(v + eps)

def _scatter_add(tgt, idx, src, axis=0):
    return tgt.at[idx].add(src)

def _segment_sum(src, seg, n):
    return jax.ops.segment_sum(src, seg, n)
kernel_name = 'mk_gnn_resnorm_d2_gnn_r64_36027a'

def setup_inputs(seed: int=0):
    np.random.seed(seed)
    _w = jnp.asarray

    def _rec_inputs():
        import jax
        import jax.numpy as jnp
        _gk = jax.random.key(seed)
        x = -0.0003713 + 1 * jax.random.normal(jax.random.fold_in(_gk, 1), (50000, 128), jnp.float32)
        src = jax.random.randint(jax.random.fold_in(_gk, 2), (12500,), 0, 50000, jnp.int32)
        dst = jnp.minimum((50000 * jax.random.uniform(jax.random.fold_in(_gk, 3), (12500,)) ** 2.0).astype(jnp.int32), 49999)
        _o = jnp.argsort(dst, stable=True)
        src = src[_o]
        dst = dst[_o]
        edge_attr_128 = -6.47781e-05 + 0.999943 * jax.random.normal(jax.random.fold_in(_gk, 12), (12500, 128), jnp.float32)
        return (x, src, dst, edge_attr_128)
    x, src, dst, edge_attr_128 = _rec_inputs()

    def _L0_gnn_setup():
        import jax, jax.numpy as jnp
        import numpy as np
        N_NODES = 100000
        N_EDGES = 25000
        D_X = 128
        D_E = 128
        D_U = 16
        D_IN = D_X + D_E + D_U
        H = 128
        D_OUT = 128
        LN_EPS = 1e-05

        def _layer_norm(x, gamma, beta):
            mu = jnp.mean(x, axis=-1, keepdims=True)
            var = jnp.var(x, axis=-1, keepdims=True)
            return (x - mu) * jax.lax.rsqrt(var + LN_EPS) * gamma + beta
        key = jax.random.key(seed)
        ks = jax.random.split(key, 12)
        x = jax.random.normal(ks[0], (N_NODES, D_X), dtype=jnp.float32)
        edge_attr = jax.random.normal(ks[1], (N_EDGES, D_E), dtype=jnp.float32)
        u = jax.random.normal(ks[2], (1, D_U), dtype=jnp.float32)
        edge_index = jax.random.randint(ks[3], (2, N_EDGES), 0, N_NODES, dtype=jnp.int64)
        batch = jnp.zeros((N_NODES,), dtype=jnp.int64)

        def lin(k, din, dout):
            s = 1.0 / np.sqrt(din)
            kw, kb = jax.random.split(k)
            W = jax.random.uniform(kw, (din, dout), minval=-s, maxval=s, dtype=jnp.float32)
            b = jax.random.uniform(kb, (dout,), minval=-s, maxval=s, dtype=jnp.float32)
            return (W, b)
        W1, b1 = lin(ks[4], D_IN, H)
        W2, b2 = lin(ks[5], H, H)
        W3, b3 = lin(ks[6], H, D_OUT)
        g1 = jnp.ones((H,), jnp.float32)
        be1 = jnp.zeros((H,), jnp.float32)
        g2 = jnp.ones((H,), jnp.float32)
        be2 = jnp.zeros((H,), jnp.float32)
        return {'x': x, 'edge_attr': edge_attr, 'u': u, 'W1': W1, 'b1': b1, 'g1': g1, 'be1': be1, 'W2': W2, 'b2': b2, 'g2': g2, 'be2': be2, 'W3': W3, 'b3': b3, 'edge_index': edge_index, 'batch': batch}
    _L0_gnn_all = _L0_gnn_setup()
    _L0_gnn_in = {k: v for k, v in _L0_gnn_all.items() if k in ('u', 'W1', 'b1', 'g1', 'be1', 'W2', 'b2', 'g2', 'be2', 'W3', 'b3')}
    del _L0_gnn_all

    def _L1_gnn_setup():
        import jax, jax.numpy as jnp
        import numpy as np
        EPS = 1e-12

        def sage_conv(x, src, dst, num_nodes, W_l, b_l, W_r):
            msg = x[src]
            agg = jax.ops.segment_sum(msg, dst, num_segments=num_nodes)
            cnt = jax.ops.segment_sum(jnp.ones((src.shape[0],), x.dtype), dst, num_segments=num_nodes)
            mean = agg / jnp.maximum(cnt, 1.0)[:, None]
            out = mean @ W_l.T + b_l + x @ W_r.T
            norm = jnp.linalg.norm(out, axis=-1, keepdims=True)
            return out / jnp.maximum(norm, EPS)
        key = jax.random.key(seed)
        ks = jax.random.split(key, 8)
        N, E, IN, H = (50000, 12500, 128, 128)
        x = jax.random.normal(ks[0], (N, IN), dtype=jnp.float32)
        edge_index = jax.random.randint(ks[1], (2, E), 0, N, dtype=jnp.int64)

        def lin(k, fout, fin):
            bound = 1.0 / np.sqrt(fin)
            return jax.random.uniform(k, (fout, fin), jnp.float32, -bound, bound)
        W_l0 = lin(ks[2], H, IN)
        b_l0 = jnp.zeros((H,), jnp.float32)
        W_r0 = lin(ks[3], H, IN)
        W_l1 = lin(ks[4], H, H)
        b_l1 = jnp.zeros((H,), jnp.float32)
        W_r1 = lin(ks[5], H, H)
        return {'x': x, 'edge_index': edge_index, 'W_l0': W_l0, 'b_l0': b_l0, 'W_r0': W_r0, 'W_l1': W_l1, 'b_l1': b_l1, 'W_r1': W_r1}
    _L1_gnn_all = _L1_gnn_setup()
    _L1_gnn_in = {k: v for k, v in _L1_gnn_all.items() if k in ('W_l0', 'b_l0', 'W_r0', 'W_l1', 'b_l1', 'W_r1')}
    del _L1_gnn_all
    return {'x': x, 'src': src, 'dst': dst, 'edge_attr_128': edge_attr_128, 'L0_gnn_u': _L0_gnn_in['u'], 'L0_gnn_W1': _L0_gnn_in['W1'], 'L0_gnn_b1': _L0_gnn_in['b1'], 'L0_gnn_g1': _L0_gnn_in['g1'], 'L0_gnn_be1': _L0_gnn_in['be1'], 'L0_gnn_W2': _L0_gnn_in['W2'], 'L0_gnn_b2': _L0_gnn_in['b2'], 'L0_gnn_g2': _L0_gnn_in['g2'], 'L0_gnn_be2': _L0_gnn_in['be2'], 'L0_gnn_W3': _L0_gnn_in['W3'], 'L0_gnn_b3': _L0_gnn_in['b3'], 'L1_gnn_W_l0': _L1_gnn_in['W_l0'], 'L1_gnn_b_l0': _L1_gnn_in['b_l0'], 'L1_gnn_W_r0': _L1_gnn_in['W_r0'], 'L1_gnn_W_l1': _L1_gnn_in['W_l1'], 'L1_gnn_b_l1': _L1_gnn_in['b_l1'], 'L1_gnn_W_r1': _L1_gnn_in['W_r1']}

def reference(x, src, dst, edge_attr_128, L0_gnn_u, L0_gnn_W1, L0_gnn_b1, L0_gnn_g1, L0_gnn_be1, L0_gnn_W2, L0_gnn_b2, L0_gnn_g2, L0_gnn_be2, L0_gnn_W3, L0_gnn_b3, L1_gnn_W_l0, L1_gnn_b_l0, L1_gnn_W_r0, L1_gnn_W_l1, L1_gnn_b_l1, L1_gnn_W_r1):
    import jax
    import jax.numpy as jnp

    def _L0_gnn_ref(x, edge_attr, u, W1, b1, g1, be1, W2, b2, g2, be2, W3, b3, edge_index, batch):
        import jax, jax.numpy as jnp
        import numpy as np
        N_NODES = 100000
        N_EDGES = 25000
        D_X = 128
        D_E = 128
        D_U = 16
        D_IN = D_X + D_E + D_U
        H = 128
        D_OUT = 128
        LN_EPS = 1e-05

        def _layer_norm(x, gamma, beta):
            mu = jnp.mean(x, axis=-1, keepdims=True)
            var = jnp.var(x, axis=-1, keepdims=True)
            return (x - mu) * jax.lax.rsqrt(var + LN_EPS) * gamma + beta
        edge_dst = edge_index[1]
        agg = jax.ops.segment_sum(edge_attr, edge_dst, num_segments=x.shape[0])
        u_exp = jnp.broadcast_to(u, (x.shape[0], u.shape[1]))
        h = jnp.concatenate([x, agg, u_exp], axis=1)
        h = _layer_norm(jax.nn.relu(h @ W1 + b1), g1, be1)
        h = _layer_norm(jax.nn.relu(h @ W2 + b2), g2, be2)
        return h @ W3 + b3

    def _L1_gnn_ref(x, edge_index, W_l0, b_l0, W_r0, W_l1, b_l1, W_r1):
        import jax, jax.numpy as jnp
        import numpy as np
        EPS = 1e-12

        def sage_conv(x, src, dst, num_nodes, W_l, b_l, W_r):
            msg = x[src]
            agg = jax.ops.segment_sum(msg, dst, num_segments=num_nodes)
            cnt = jax.ops.segment_sum(jnp.ones((src.shape[0],), x.dtype), dst, num_segments=num_nodes)
            mean = agg / jnp.maximum(cnt, 1.0)[:, None]
            out = mean @ W_l.T + b_l + x @ W_r.T
            norm = jnp.linalg.norm(out, axis=-1, keepdims=True)
            return out / jnp.maximum(norm, EPS)
        N = x.shape[0]
        src, dst = (edge_index[0], edge_index[1])
        h = sage_conv(x, src, dst, N, W_l0, b_l0, W_r0)
        h = jax.nn.relu(h)
        h = sage_conv(h, src, dst, N, W_l1, b_l1, W_r1)
        h = jax.nn.relu(h)
        return h
    edge_index = jnp.stack([src, dst])
    batch0 = jnp.zeros((50000,), jnp.int32)
    x = _layernorm(x + _L0_gnn_ref(x, edge_attr_128, L0_gnn_u, L0_gnn_W1, L0_gnn_b1, L0_gnn_g1, L0_gnn_be1, L0_gnn_W2, L0_gnn_b2, L0_gnn_g2, L0_gnn_be2, L0_gnn_W3, L0_gnn_b3, edge_index, batch0), axis=-1)
    x = _layernorm(x + _L1_gnn_ref(x, edge_index, L1_gnn_W_l0, L1_gnn_b_l0, L1_gnn_W_r0, L1_gnn_W_l1, L1_gnn_b_l1, L1_gnn_W_r1), axis=-1)
    return x

_drawn_inputs = setup_inputs


def setup_inputs(seed=0):
    import zlib

    import numpy as np

    out = dict(_drawn_inputs(seed))
    spreads = {'L0_gnn_g1': (1.0, 0.2),
     'L0_gnn_be1': (0.0, 0.1),
     'L0_gnn_g2': (1.0, 0.2),
     'L0_gnn_be2': (0.0, 0.1),
     'L1_gnn_b_l0': (0.0, 2.0),
     'L1_gnn_b_l1': (0.0, 0.1)}
    factors = {'L1_gnn_W_l0': 43.755, 'L1_gnn_W_r0': 3.357, 'L1_gnn_W_l1': 19.495, 'L1_gnn_W_r1': 2.842}
    for name, (base, spread) in spreads.items():
        noise = np.random.default_rng([zlib.crc32(name.encode()), seed]).standard_normal(out[name].shape)
        drawn = base * np.exp(spread * noise) if base else spread * noise
        out[name] = jnp.asarray(drawn.astype(out[name].dtype))
    for name, factor in factors.items():
        out[name] = (out[name] * factor).astype(out[name].dtype)
    return out
```

```python
from contextlib import ExitStack

import concourse.bass as bass
from concourse import mybir

F32 = mybir.dt.float32
BF16 = mybir.dt.bfloat16
I32 = mybir.dt.int32
ALU = mybir.AluOpType
ACT = mybir.ActivationFunctionType

P = 128
J = 4
G = P * J
F = 128
U = 6
LN_EPS = 1e-5
NORM_EPS = 1e-12


class Schedule:

    def __init__(self, kinds):
        self.kinds = kinds

    def kind(self, n):
        return self.kinds[n] if 0 <= n < len(self.kinds) else None

    def upto(self, n, *which):
        which = which or ("node", "tail", "edge")
        return sum(k in which for k in self.kinds[:max(n + 1, 0)])


class Place:

    APART = (mybir.EngineType.Pool, mybir.EngineType.SP)
    passed = None

    def __init__(self, i, turns=1, reg=None):
        self.i, self.turns, self.reg = i, turns, reg

    def value(self, f):
        a = f(self.i)
        if self.reg is None:
            return a
        step = f(self.i + U) - a
        assert all(f(self.i + U * t) == a + step * t for t in range(self.turns))
        return a + self.reg * step if step else a

    def wait(self, eng, sem, f, apart=False):
        if f(self.i) > 0:
            eng.wait_ge(sem, self.value(f))
            if self.reg is not None and (apart or eng.engine in self.APART):
                eng.sem_inc(self.passed, 1)
        else:
            assert f(self.i + U * (self.turns - 1)) <= 0

    def idle(self, eng):
        if self.reg is not None:
            eng.sem_inc(self.passed, 1)
        return eng.drain()


def run_phase(eng, sched, depth, body):
    length = len(sched.kinds) + depth
    blocks = -(-length // U)

    def pattern(b):
        return [sched.kind(n) for n in range(b * U - depth, b * U + U)]

    b = 0
    while b < blocks:
        e = b + 1
        if b * U - depth >= U:
            while e < blocks and pattern(e) == pattern(b) and (e + 1) * U <= len(sched.kinds):
                e += 1
        if e - b >= 2:
            with eng.Fori(0, e - b) as turn:
                for u in range(U):
                    body(Place(b * U + u, e - b, turn))
        else:
            e = b + 1
            for i in range(b * U, min(e * U, length)):
                body(Place(i))
        b = e


def build(nc, A, out, debug=None):
    N = A["x"].shape[0]
    E = A["src"].shape[0]
    NG = N // G
    TAIL = (N - NG * G) // J
    assert (N - NG * G) % J == 0 and E % J == 0
    EG = -(-E // G)
    SLOTS = EG * G
    ETAIL = (E - (EG - 1) * G) // J
    H = -(-N // P)
    ROWS = N + SLOTS
    D_U = A["L0_gnn_u"].shape[1]

    half = 2 * EG
    rest = NG + 1 - half
    phase1 = Schedule((["node", "node", "edge"] * EG + ["node"] * rest)[:-1] + ["tail"])
    phase2 = Schedule(["node", "node", "edge"] * EG)
    third = ["node"] * (rest - 1) + ["tail"] + ["none"] * (2 * EG - rest)
    phase3 = Schedule([k for d in range(EG) for k in (third[2 * d], third[2 * d + 1], "edge")])
    DEPTH1, DEPTH2 = 8, 5

    with ExitStack() as ctx:
        def sb(name, shape, dt=F32):
            return ctx.enter_context(nc.sbuf_tensor(name, shape, dt))

        def ps(name, shape):
            return ctx.enter_context(nc.psum_tensor(name, shape, F32))

        def sem(name):
            return ctx.enter_context(nc.semaphore(name))

        x1_table = nc.dram_tensor("x1_table", [ROWS, F], F32, kind="Internal").ap()
        h1_table = nc.dram_tensor("h1_table", [ROWS, F], F32, kind="Internal").ap()

        def node_rows(table, k):
            return table[0:NG * G].rearrange("(g p j) f -> g p (j f)", p=P, j=J)[k]

        def tail_rows(table):
            return table[NG * G:N].rearrange("(p j) f -> p (j f)", j=J)

        def edge_rows(table, k):
            return table[N:ROWS].rearrange("(g p j) f -> g p (j f)", p=P, j=J)[k]

        wbuf = sb("wbuf", [P, 8, F])
        w1x, w1e, w2c, w3c, wr0, wl0, wr1, wl1 = [wbuf[:, i, :] for i in range(8)]
        raw = sb("raw", [P, 6, F])
        w1u = sb("w1u", [D_U, F])
        u_col = sb("u_col", [D_U, 1])
        cols = sb("cols", [P, 6])
        c1 = cols[:, 5:6]
        be_wide = sb("be_wide", [P, 2, F])
        brow = sb("brow", [P, 2, F])
        bias2 = sb("bias2", [P, F])
        bias3 = sb("bias3", [P, J, F])
        identity = sb("identity", [P, P])
        centre = sb("centre", [P, P])
        avg = sb("avg", [P, 2])
        scaled = sb("scaled", [P, 2, F])
        bl_wide = sb("bl_wide", [96, 2, F])
        bl_tmp = sb("bl_tmp", [96, 2, F])
        bl_part = sb("bl_part", [96, 3, 2, F], BF16)
        bl_rows = sb("bl_rows", [96, 2, F], BF16)
        ones3 = sb("ones3", [96, P], BF16)

        src_c = sb("src_c", [P, EG, J], I32)
        dst_c = sb("dst_c", [P, EG, J], I32)
        next_c = sb("next_c", [P, EG, J], I32)
        x_idx = sb("x_idx", [P, EG, J], I32)
        row_idx = sb("row_idx", [P, EG, J], I32)
        out_idx = sb("out_idx", [P, EG, J], I32)
        same = sb("same", [P, SLOTS], BF16)
        inv_count = sb("inv_count", [P, SLOTS])
        int_c = sb("int_c", [P, EG, J], I32)
        fc = sb("fc", [P, 8, EG, J])
        dst_f, is_last, e_high, e_low, src_f, src_hi, dst_hi, dst_lo = [fc[:, i] for i in range(8)]
        idx_now = sb("idx_now", [P, 2, J], I32)
        found = sb("found", [P, EG, J])
        fsel = sb("fsel", [P, 2, EG, J])
        iota_hi = sb("iota_hi", [P, H])
        iota_lo = sb("iota_lo", [P, P], BF16)
        iota_p = sb("iota_p", [P, 1])
        hot_hi = sb("hot_hi", [P, 2, H], BF16)
        hot_lo = sb("hot_lo", [P, 2, 2, P], BF16)
        slot_table = sb("slot_table", [P, 2, H], BF16)
        hot_src = inv_count[:, :].bitcast(BF16)[:, 0:SLOTS]
        junk_hi = sb("junk_hi", [P, 2, H])
        wide = sb("wide", [P, SLOTS], I32)

        results = wide[:, :].bitcast(F32).rearrange("p (g j f) -> p g j f", g=EG, j=J)

        xg = sb("xg", [P, 6, J, F])
        ea = sb("ea", [P, 2, J, F])
        aggT = sb("aggT", [P, 2, G])
        r2 = sb("r2", [P, 2, G])
        v3 = sb("v3", [P, 2, J, F])
        x1 = sb("x1", [P, 3, J, F])
        x1T = sb("x1T", [P, 2, G])
        rows = sb("rows", [P, 3, J, F])
        early = wide[:, 0:12 * G].bitcast(F32).rearrange("p (b r n) -> p b r n", b=6, r=2)
        xT, r1, sq1, sq2 = [early[:, b] for b in range(4)]
        z2, h1 = [early[:, b].rearrange("p r (j f) -> p r j f", j=J) for b in (4, 5)]
        junk = sb("junk", [P, 2, F])
        ssq = sb("ssq", [P, 2, J])
        stats = sb("stats", [P, 2, 2, J])
        stats_m2 = sb("stats_m2", [P, 2, J])
        stats_v = sb("stats_v", [P, 2, J])
        bn6 = sb("bn6", [P, 2, J, 6])
        bn2 = sb("bn2", [P, 2, J, 2])
        nmean = sb("nmean", [P, 2, J])
        var = sb("var", [P, 2, 16])
        std = sb("std", [P, 2, 16])
        inv = sb("inv", [P, 2, 16])

        bank = [ps(f"bank{i}", [P, G]) for i in range(8)]

        Place.passed = sem("passed")

        w_in = [sem(f"w_in{i}") for i in range(3)]
        consts = sem("consts")
        prep_v = sem("prep_v")
        prep_p = sem("prep_p")
        rows_in = sem("rows_in")
        dst_in = sem("dst_in")
        wide_in = sem("wide_in")
        wide_free = sem("wide_free")
        hot_ready = sem("hot_ready")
        hot_used = sem("hot_used")
        table_done = sem("table_done")
        table_copied = sem("table_copied")
        looked_up = sem("looked_up")
        selected = sem("selected")
        prologue_done = sem("prologue_done")
        chain = sem("chain")

        with nc.Block() as block:
            @block.sync
            def _(sp):
                sp.dma_start(raw[:, 0, :], A["L0_gnn_W2"]).then_inc(w_in[0], 16)
                sp.dma_start(raw[:, 1, :], A["L0_gnn_W3"]).then_inc(w_in[0], 16)
                for i, name in enumerate(["L1_gnn_W_r0", "L1_gnn_W_l0", "L1_gnn_W_r1", "L1_gnn_W_l1"]):
                    sp.dma_start(raw[:, 2 + i, :], A[name]).then_inc(w_in[0], 16)
                sp.dma_start(w1x, A["L0_gnn_W1"][0:F, :]).then_inc(w_in[0], 16)
                sp.dma_start(w1e, A["L0_gnn_W1"][F:2 * F, :]).then_inc(w_in[0], 16)
                sp.dma_start(w1u[:, :], A["L0_gnn_W1"][2 * F:2 * F + D_U, :]).then_inc(w_in[0], 16)
                sp.dma_start(u_col[:, :], A["L0_gnn_u"].rearrange("a d -> d a")).then_inc(w_in[0], 16)
                for i, name in enumerate(["b1", "g1", "be1", "g2", "be2"]):
                    sp.dma_start(cols[:, i:i + 1], A["L0_gnn_" + name].rearrange("(d a) -> d a", a=1)).then_inc(w_in[0], 16)
                for i, name in enumerate(["b2", "b3"]):
                    row = A["L0_gnn_" + name].rearrange("(a d) -> a d", a=1)
                    sp.dma_start(brow[:, i, :], row.to_broadcast([P, F])).then_inc(w_in[0], 16)
                for i, name in enumerate(["b_l0", "b_l1"]):
                    row = A["L1_gnn_" + name].rearrange("(a d) -> a d", a=1)
                    sp.dma_start(bl_wide[:, i, :], row.to_broadcast([96, F])).then_inc(w_in[0], 16)
                sp.wait_ge(consts, 1)
                whole = (EG - 1) * G
                for sbuf, name in ((src_c, "src"), (dst_c, "dst")):
                    sp.dma_start(sbuf[:, 0:EG - 1, :], A[name][0:whole].rearrange("(g p j) -> p g j", p=P, j=J)).then_inc(dst_in, 16)
                    sp.dma_start(sbuf[0:ETAIL, EG - 1, :], A[name][whole:E].rearrange("(p j) -> p j", j=J)).then_inc(dst_in, 16)
                sp.dma_start(next_c[:, 0:EG - 1, :], A["dst"][1:whole + 1].rearrange("(g p j) -> p g j", p=P, j=J)).then_inc(dst_in, 16)
                sp.dma_start(next_c[0:ETAIL - 1, EG - 1, :], A["dst"][whole + 1:E - J + 1].rearrange("(p j) -> p j", j=J)).then_inc(dst_in, 16)
                sp.dma_start(next_c[ETAIL - 1:ETAIL, EG - 1, 0:J - 1], A["dst"][E - J + 1:E].rearrange("(p j) -> p j", p=1)).then_inc(dst_in, 16)
                sp.dma_start(wide[:, 0:E], A["src"].rearrange("(a e) -> a e", a=1).to_broadcast([P, E])).then_inc(wide_in, 16)
                sp.wait_ge(wide_free, 1)
                sp.dma_start(wide[:, 0:E], A["dst"].rearrange("(a e) -> a e", a=1).to_broadcast([P, E])).then_inc(wide_in, 16)

            W_LOADS = 16 * (6 + 4 + 5 + 2 + 2)

            @block.gpsimd
            def _(pool):
                nc.gpsimd.memset(src_c[:, :, :], 0)
                nc.gpsimd.memset(dst_c[:, :, :], -1)
                nc.gpsimd.memset(wide[:, :], 0)
                nc.gpsimd.memset(next_c[:, :, :], -1).then_inc(prep_p, 1)
                pool.wait_ge(prep_p, 1)
                nc.gpsimd.iota(int_c[:, :, :], pattern=[[G, EG], [1, J]], base=1, channel_multiplier=J).then_inc(consts, 1)
                nc.gpsimd.memset(identity[:, :], 0.0).then_inc(prep_p, 1)
                nc.gpsimd.memset(centre[:, :], -1.0 / F).then_inc(prep_p, 1)
                pool.wait_ge(prep_p, 3)
                nc.gpsimd.affine_select(out=identity[:, :], in_=identity[:, :], compare_op=ALU.not_equal, fill=1.0,
                                        base=0, pattern=[[-1, P]], channel_multiplier=1).then_inc(consts, 1)
                nc.gpsimd.affine_select(out=centre[:, :], in_=centre[:, :], compare_op=ALU.not_equal, fill=1.0 - 1.0 / F,
                                        base=0, pattern=[[-1, P]], channel_multiplier=1).then_inc(consts, 1)
                nc.gpsimd.iota(iota_hi[:, :], pattern=[[1, H]], base=0, channel_multiplier=0,
                               allow_small_or_imprecise_dtypes=True).then_inc(consts, 1)
                nc.gpsimd.iota(iota_lo[:, :], pattern=[[1, P]], base=0, channel_multiplier=0,
                               allow_small_or_imprecise_dtypes=True).then_inc(consts, 1)
                nc.gpsimd.iota(iota_p[:, :], pattern=[[0, 1]], base=0, channel_multiplier=1,
                               allow_small_or_imprecise_dtypes=True).then_inc(consts, 1)
                nc.gpsimd.memset(ones3[:, :], 1.0).then_inc(consts, 1)
                nc.gpsimd.memset(avg[:, :], 1.0 / F).then_inc(consts, 1)
                nc.gpsimd.memset(bl_rows[:, :, :], 0.0).then_inc(consts, 1)
            CONSTS = 9

            @block.tensor
            def _(pe):
                pe.wait_ge(consts, CONSTS)
                pe.wait_ge(w_in[0], W_LOADS)
                for i in range(4):
                    pe.transpose(bank[0][:, i * F:(i + 1) * F], raw[:, 2 + i, :], identity[:, :])
                pe.matmul(bank[1][:, 0:1], w1u[:, :], u_col[:, :], start=True, stop=True)
                pe.wait_ge(prep_v, 2)
                pe.matmul(bank[2][:, 0:F], centre[:, :], scaled[:, 0, :], start=True, stop=True)
                pe.matmul(bank[2][:, F:2 * F], centre[:, :], scaled[:, 1, :], start=True, stop=True)
                pe.matmul(bank[3][:, 0:F], be_wide[:, 0, :], raw[:, 0, :], start=True, stop=True)
                pe.matmul(bank[3][:, F:2 * F], be_wide[:, 1, :], raw[:, 1, :], start=True, stop=True).then_inc(prep_p, 1)
                for t in range(SLOTS // P):
                    pe.wait_ge(hot_ready, t + 1)
                    for half_ in range(2):
                        mm = pe.matmul(bank[4 + half_][:, 0:H], hot_lo[:, t % 2, half_, :], hot_hi[:, t % 2, :],
                                       start=(t == 0), stop=(t == SLOTS // P - 1))
                    mm.then_inc(hot_used, 1)
                pe.wait_ge(table_copied, 1)
                for t in range(SLOTS // P):
                    g, j = divmod(t, J)
                    if t >= 2:
                        pe.wait_ge(selected, t - 1)
                    q = hot_src[:, g * G:(g + 1) * G].rearrange("p (i j) -> p j i", j=J)[:, j, :]
                    pe.matmul(bank[6 + t % 2][:, 0:H], q, slot_table[:, 0, :], start=True, stop=False)
                    pe.matmul(bank[6 + t % 2][:, 0:H], q, slot_table[:, 1, :], start=False, stop=True).then_inc(looked_up, 1)

            @block.vector
            def _(dve):
                links = [0]

                def link(ins):
                    links[0] += 1
                    ins.then_inc(chain, 1)
                    dve.wait_ge(chain, links[0])

                V = nc.vector
                dve.wait_ge(w_in[0], W_LOADS)
                dve.wait_ge(consts, CONSTS)
                V.memset(be_wide[:, :, :], 0.0).then_inc(prep_v, 1)
                V.memset(var[:, :, :], 1.0)
                dve.wait_ge(prep_v, 1)
                for i in range(2):
                    V.tensor_scalar(scaled[:, i, :], raw[:, i, :], cols[:, 1 + 2 * i:2 + 2 * i], None, ALU.mult)
                    last = V.tensor_scalar(be_wide[:, i, :], be_wide[:, i, :], cols[:, 2 + 2 * i:3 + 2 * i], None, ALU.add)
                last.then_inc(prep_v, 1)
                link(V.tensor_copy(bl_part[:, 0], bl_wide[:, :, :]))
                link(V.tensor_tensor(bl_tmp[:, :, :], bl_wide[:, :, :], bl_part[:, 0], ALU.subtract))
                link(V.tensor_copy(bl_part[:, 1], bl_tmp[:, :, :]))
                link(V.tensor_tensor(bl_tmp[:, :, :], bl_tmp[:, :, :], bl_part[:, 1], ALU.subtract))
                link(V.tensor_copy(bl_part[:, 2], bl_tmp[:, :, :]))
                for part in range(3):
                    r = slice(32 * part, 32 * part + 1)
                    link(V.tensor_copy(bl_rows[r], bl_part[r, part]))
                dve.wait_ge(prep_p, 4)
                V.tensor_copy(wbuf[:, 4:8, :], bank[0][:, :].rearrange("p (w f) -> p w f", w=4))
                V.tensor_tensor(c1, bank[1][:, 0:1], cols[:, 0:1], ALU.add)
                V.tensor_copy(wbuf[:, 2:4, :], bank[2][:, 0:2 * F].rearrange("p (w f) -> p w f", w=2))
                V.tensor_tensor(bias2[:, :], bank[3][:, 0:F], brow[:, 0, :], ALU.add)
                for j in range(J):
                    link(V.tensor_tensor(bias3[:, j, :], bank[3][:, F:2 * F], brow[:, 1, :], ALU.add))

                dve.wait_ge(dst_in, 16 * 7)
                next_f = fsel[:, 0]
                V.tensor_copy(src_f, src_c[:, :, :])
                V.tensor_copy(dst_f, dst_c[:, :, :])
                link(V.tensor_copy(next_f, next_c[:, :, :]))
                link(V.tensor_tensor(is_last, dst_f, next_f, ALU.not_equal))
                link(V.tensor_scalar(x_idx[:, :, :], dst_f, 0.0, None, ALU.max))
                link(V.tensor_scalar(fsel[:, 1], is_last, -float(N + P), float(N + P), ALU.mult, ALU.add))
                link(V.tensor_tensor(fsel[:, 1], fsel[:, 1], x_idx[:, :, :], ALU.add))
                link(V.tensor_copy(out_idx[:, :, :], fsel[:, 1]))
                tmp = row_idx
                for of, op, by, to in ((int_c, ALU.bitwise_and, P - 1, e_low), (int_c, ALU.bitwise_and, -P, e_high),
                                       (src_c, ALU.logical_shift_right, 7, src_hi), (x_idx, ALU.bitwise_and, P - 1, dst_lo),
                                       (x_idx, ALU.logical_shift_right, 7, dst_hi)):
                    link(V.tensor_scalar(tmp[:, :, :], of[:, :, :], by, None, op))
                    link(V.tensor_copy(to, tmp[:, :, :]))
                link(V.tensor_tensor(e_low, e_low, is_last, ALU.mult))
                link(V.tensor_tensor(e_high, e_high, is_last, ALU.mult))
                for t in range(SLOTS // P):
                    g, j = divmod(t, J)
                    if t >= 2:
                        dve.wait_ge(hot_used, t - 1)
                    V.tensor_scalar(hot_hi[:, t % 2, :], iota_hi[:, :], dst_hi[:, g, j:j + 1], None, ALU.is_equal)
                    V.tensor_scalar(hot_lo[:, t % 2, 0, :], iota_lo[:, :], dst_lo[:, g, j:j + 1], e_high[:, g, j:j + 1],
                                    ALU.is_equal, ALU.mult)
                    V.tensor_scalar(hot_lo[:, t % 2, 1, :], iota_lo[:, :], dst_lo[:, g, j:j + 1], e_low[:, g, j:j + 1],
                                    ALU.is_equal, ALU.mult).then_inc(hot_ready, 1)
                dve.wait_ge(wide_in, 16)
                link(V.tensor_scalar(wide[:, :], wide[:, :], P - 1, None, ALU.bitwise_and))
                V.tensor_scalar(hot_src, wide[:, :], iota_p[:, 0:1], None, ALU.is_equal).then_inc(wide_free, 1)
                dve.wait_ge(wide_free, 1)
                dve.wait_ge(hot_used, SLOTS // P)
                for half_ in range(2):
                    last = V.tensor_copy(slot_table[:, half_, :], bank[4 + half_][:, 0:H])
                last.then_inc(table_copied, 1)
                for t in range(SLOTS // P):
                    g, j = divmod(t, J)
                    dve.wait_ge(looked_up, t + 1)
                    V.scalar_tensor_tensor(out=junk_hi[:, t % 2, :], in0=iota_hi[:, :], scalar=src_hi[:, g, j:j + 1],
                                           in1=bank[6 + t % 2][:, 0:H], op0=ALU.is_equal, op1=ALU.mult,
                                           accum_out=found[:, g, j:j + 1]).then_inc(selected, 1)
                dve.wait_ge(selected, SLOTS // P)
                link(V.tensor_scalar(fsel[:, 0], found[:, :, :], 0.0, None, ALU.is_gt))
                link(V.tensor_tensor(fsel[:, 1], found[:, :, :], src_f, ALU.subtract))
                link(V.tensor_scalar(fsel[:, 1], fsel[:, 1], float(N - 1), None, ALU.add))
                link(V.tensor_tensor(fsel[:, 1], fsel[:, 1], fsel[:, 0], ALU.mult))
                link(V.tensor_tensor(fsel[:, 1], fsel[:, 1], src_f, ALU.add))
                link(V.tensor_copy(row_idx[:, :, :], fsel[:, 1]))
                dve.wait_ge(wide_in, 32)
                V.memset(same[:, 0:1], 0.0)
                if SLOTS > E:
                    V.memset(same[:, E:SLOTS], 0.0)
                link(V.tensor_tensor(same[:, 1:E], wide[:, 1:E], wide[:, 0:E - 1], ALU.is_equal))
                link(V.memset(wide[:, :].bitcast(F32), 1.0))
                link(V.tensor_tensor_scan(inv_count[:, :], same[:, :], wide[:, :].bitcast(F32), 0.0, ALU.mult, ALU.add))
                link(V.reciprocal(inv_count[:, :], inv_count[:, :]))

        S = phase1
        x_in = [sem(f"x_in{s}") for s in range(6)]
        xd_in = [sem(f"xd_in{s}") for s in range(2)]
        ea_in = [sem(f"ea_in{s}") for s in range(2)]
        pe_a, pe_ea, pe_b, pe_c, pe_d, pe_e, pe_f, pe_g = [sem("pe_" + c) for c in ("x_turned", "ea_turned", "y1", "y2_stats", "z2_turned", "y3_stats", "x1_turned", "z_sage")]
        xT_done, r1_done, r2_done, x1T_done, std_done, ssq_done = [sem(c) for c in ("xT_done", "r1_done", "r2_done", "x1T_done", "std_done", "ssq_done")]
        stats_read, stats_sq, stats_sub, var_done, inv_done = [sem(c) for c in ("stats_read", "stats_sq", "stats_sub", "var_done", "inv_done")]
        agg_done, z2_done, v3_done, bn6_done, bn2_done, h1_done = [sem(c) for c in ("agg_done", "z2_done", "v3_done", "bn6_done", "bn2_done", "h1_done")]
        sq1_done, sq2_done, xb_done, x1_done = [sem(c) for c in ("sq1_done", "sq2_done", "xb_done", "x1_done")]
        x_idx_now = sem("x_idx_now")
        x1_out = [sem(f"x1_out{s}") for s in range(3)]
        h1_out = [sem(f"h1_out{s}") for s in range(2)]

        NODES = ("node", "tail")
        L1 = len(S.kinds)

        def loaded1(n):
            return 16 * sum(S.kind(m) in NODES for m in range(n % 6, n + 1, 6))

        def rounds1(i):
            return i - 1

        def stat_rounds1(i):
            return min(i, L1 + 3) - 1

        def stored1(n, ring, kinds=("node", "tail", "edge")):
            return 16 * sum(S.kind(m) in kinds for m in range(n % ring, n + 1, ring)) if n >= 0 else 0

        with nc.Block() as block:
            @block.sync
            def _(sp):
                def body(at):
                    n = at.i
                    if S.kind(n) is not None:
                        if S.kind(n) == "edge":
                            e = (n % 6) // 3
                            k = at.value(lambda i: S.upto(i, "edge") - 1)
                            at.wait(sp, pe_ea, lambda i: S.upto(i, "edge") - 2)
                            if n == 3 * EG - 1:
                                sp.dma_start(ea[0:ETAIL, e].rearrange("p j f -> p (j f)"),
                                             A["edge_attr_128"][(EG - 1) * G:E].rearrange("(p j) f -> p (j f)", j=J)).then_inc(ea_in[e], 16)
                            else:
                                sp.dma_start(ea[:, e].rearrange("p j f -> p (j f)"),
                                             A["edge_attr_128"][0:(EG - 1) * G].rearrange("(g p j) f -> g p (j f)", p=P, j=J)[k]).then_inc(ea_in[e], 16)
                        else:
                            at.wait(sp, v3_done, lambda i: i - 5)
                            dst = xg[:, n % 6].rearrange("p j f -> p (j f)")
                            if S.kind(n) == "tail":
                                sp.dma_start(dst[0:TAIL], tail_rows(A["x"])).then_inc(x_in[n % 6], 16)
                            else:
                                k = at.value(lambda i: S.upto(i, "node") - 1)
                                sp.dma_start(dst, node_rows(A["x"], k)).then_inc(x_in[n % 6], 16)
                    n = at.i - 6
                    if S.kind(n) is not None:
                        at.wait(sp, x1_done, lambda i: i - 5)
                        of = x1[:, n % 3].rearrange("p j f -> p (j f)")
                        if S.kind(n) == "tail":
                            sp.dma_start(tail_rows(x1_table), of[0:TAIL]).then_inc(x1_out[n % 3], 16)
                        elif S.kind(n) == "edge":
                            k = at.value(lambda i: S.upto(i - 6, "edge") - 1)
                            sp.dma_start(edge_rows(x1_table, k), of).then_inc(x1_out[n % 3], 16)
                        else:
                            k = at.value(lambda i: S.upto(i - 6, "node") - 1)
                            sp.dma_start(node_rows(x1_table, k), of).then_inc(x1_out[n % 3], 16)
                    n = at.i - 9
                    if S.kind(n) in NODES:
                        at.wait(sp, h1_done, lambda i: S.upto(i - 9, *NODES))
                        of = h1[:, n % 2].rearrange("p j f -> p (j f)")
                        if S.kind(n) == "tail":
                            sp.dma_start(tail_rows(h1_table), of[0:TAIL]).then_inc(h1_out[n % 2], 16)
                        else:
                            k = at.value(lambda i: S.upto(i - 9, "node") - 1)
                            sp.dma_start(node_rows(h1_table, k), of).then_inc(h1_out[n % 2], 16)
                run_phase(sp, S, DEPTH1 + 1, body)
                for s in range(3):
                    last = max(n for n in range(L1) if n % 3 == s)
                    sp.wait_ge(x1_out[s], stored1(last, 3))
                for s in range(2):
                    last = max(n for n in range(L1) if n % 2 == s)
                    sp.wait_ge(h1_out[s], stored1(last, 2, NODES))

            @block.tensor
            def _(pe):
                def body(at):
                    n = at.i - 2
                    if S.kind(n) is not None:
                        at.wait(pe, r1_done, lambda i: i - 1)
                        at.wait(pe, sq1_done, lambda i: i - 1)
                        at.wait(pe, z2_done, lambda i: i - 2)
                        at.wait(pe, stats_read, lambda i: stat_rounds1(i - 1))
                        for j in range(J):
                            pe.matmul(bank[2][:, j * F:(j + 1) * F], r1[:, n % 2, j * F:(j + 1) * F], w2c, start=True, stop=True)
                            pe.matmul(bank[7][:, j:j + 1], r1[:, n % 2, j * F:(j + 1) * F], avg[:, 0:1], start=True, stop=True)
                        for j in range(J):
                            mm = pe.matmul(bank[7][:, 4 + j:5 + j], sq1[:, n % 2, j * F:(j + 1) * F], avg[:, 0:1], start=True, stop=True)
                        mm.then_inc(pe_c, 1)
                    n = at.i - 4
                    if S.kind(n) is not None:
                        at.wait(pe, r2_done, lambda i: i - 3)
                        at.wait(pe, sq2_done, lambda i: i - 3)
                        at.wait(pe, v3_done, lambda i: i - 4)
                        at.wait(pe, stats_read, lambda i: stat_rounds1(i - 1))
                        for j in range(J):
                            pe.matmul(bank[4][:, j * F:(j + 1) * F], r2[:, n % 2, j * F:(j + 1) * F], w3c, start=True, stop=True)
                            pe.matmul(bank[7][:, 8 + j:9 + j], r2[:, n % 2, j * F:(j + 1) * F], avg[:, 0:1], start=True, stop=True)
                        for j in range(J):
                            mm = pe.matmul(bank[7][:, 12 + j:13 + j], sq2[:, n % 2, j * F:(j + 1) * F], avg[:, 0:1], start=True, stop=True)
                        mm.then_inc(pe_e, 1)
                    n = at.i
                    if S.kind(n) is not None:
                        if S.kind(n) == "edge":
                            at.wait(pe, xd_in[(n % 6) // 3], lambda i: 16 * J * ((S.upto(i, "edge") + 1) // 2))
                        else:
                            at.wait(pe, x_in[n % 6], loaded1)
                        at.wait(pe, xT_done, lambda i: i)
                        for j in range(J):
                            mm = pe.transpose(bank[0][:, j * F:(j + 1) * F], xg[:, n % 6, j, :], identity[:, :])
                        mm.then_inc(pe_a, 1)
                        if S.kind(n) == "edge":
                            at.wait(pe, ea_in[(n % 6) // 3], lambda i: 16 * ((S.upto(i, "edge") + 1) // 2))
                            at.wait(pe, agg_done, lambda i: S.upto(i, "edge") - 1)
                            at.wait(pe, x1T_done, lambda i: S.upto(i - 7, *NODES))
                            for j in range(J):
                                mm = pe.transpose(bank[5][:, :].rearrange("p (i j) -> p j i", j=J)[:, j, :],
                                                  ea[:, (n % 6) // 3, j, :], identity[:, :])
                            mm.then_inc(pe_ea, 1)
                    n = at.i - 1
                    if S.kind(n) is not None:
                        at.wait(pe, xT_done, lambda i: i)
                        at.wait(pe, r1_done, lambda i: i - 1)
                        edge = S.kind(n) == "edge"
                        mm = pe.matmul(bank[1][:, :], w1x, xT[:, n % 2, :], start=True, stop=not edge)
                        if edge:
                            at.wait(pe, agg_done, lambda i: S.upto(i - 1, "edge"))
                            mm = pe.matmul(bank[1][:, :], w1e, aggT[:, (n % 6) // 3, :].rearrange("p (i j) -> p j i", j=J),
                                           start=False, stop=True)
                        mm.then_inc(pe_b, 1)
                    n = at.i - 3
                    if S.kind(n) is not None:
                        at.wait(pe, z2_done, lambda i: i - 2)
                        at.wait(pe, r2_done, lambda i: i - 3)
                        for j in range(J):
                            mm = pe.transpose(bank[3][:, j * F:(j + 1) * F], z2[:, n % 2, j, :], identity[:, :])
                        mm.then_inc(pe_d, 1)
                    n = at.i - 6
                    if S.kind(n) in NODES:
                        at.wait(pe, x1_done, lambda i: i - 5)
                        at.wait(pe, x1T_done, lambda i: S.upto(i - 7, *NODES))
                        at.wait(pe, agg_done, lambda i: S.upto(i, "edge"))
                        for j in range(J):
                            mm = pe.transpose(bank[5][:, j * F:(j + 1) * F], x1[:, n % 3, j, :], identity[:, :])
                        mm.then_inc(pe_f, 1)
                    n = at.i - 7
                    if S.kind(n) in NODES:
                        at.wait(pe, x1T_done, lambda i: S.upto(i - 7, *NODES))
                        at.wait(pe, h1_done, lambda i: S.upto(i - 8, *NODES))
                        for j in range(J):
                            pe.matmul(bank[6][:, j * F:(j + 1) * F], ones3[:, :], bl_rows[:, 0], start=True, stop=False)
                            mm = pe.matmul(bank[6][:, j * F:(j + 1) * F], x1T[:, n % 2, j * F:(j + 1) * F], wr0,
                                           start=False, stop=True)
                        mm.then_inc(pe_g, 1)
                run_phase(pe, S, DEPTH1, body)

            @block.scalar
            def _(act):
                def body(at):
                    if at.i >= 2:
                        at.wait(act, var_done, rounds1)
                        nc.scalar.activation(std[:, at.i % 2, :], var[:, at.i % 2, :], ACT.Sqrt).then_inc(std_done, 1)
                    n = at.i - 1
                    if S.kind(n) is not None:
                        at.wait(act, pe_b, lambda i: i)
                        at.wait(act, pe_c, lambda i: i - 2)
                        nc.scalar.activation(r1[:, n % 2, :], bank[1][:, :], ACT.Relu, bias=c1).then_inc(r1_done, 1)
                    n = at.i - 3
                    if S.kind(n) is not None:
                        at.wait(act, pe_d, lambda i: i - 2)
                        at.wait(act, pe_e, lambda i: i - 4)
                        nc.scalar.activation(r2[:, n % 2, :], bank[3][:, :], ACT.Relu).then_inc(r2_done, 1)
                    n = at.i
                    if S.kind(n) is not None:
                        at.wait(act, pe_a, lambda i: i + 1)
                        at.wait(act, pe_b, lambda i: i - 1)
                        nc.scalar.copy(xT[:, n % 2, :], bank[0][:, :]).then_inc(xT_done, 1)
                    n = at.i - 6
                    if S.kind(n) in NODES:
                        at.wait(act, pe_f, lambda i: S.upto(i - 6, *NODES))
                        at.wait(act, pe_g, lambda i: S.upto(i - 8, *NODES))
                        nc.scalar.copy(x1T[:, n % 2, :], bank[5][:, :]).then_inc(x1T_done, 1)
                    n = at.i - 7
                    if S.kind(n) in NODES:
                        at.wait(act, pe_g, lambda i: S.upto(i - 7, *NODES))
                        at.wait(act, ssq_done, lambda i: J * S.upto(i - 8, *NODES))
                        at.wait(act, var_done, lambda i: rounds1(i - 1))
                        for j in range(J):
                            nc.scalar.activation(junk[:, j % 2, :], bank[6][:, j * F:(j + 1) * F], ACT.Square,
                                                 accum_out=ssq[:, n % 2, j:j + 1]).then_inc(ssq_done, 1)
                            if j < J - 1:
                                act.wait_ge(ssq_done, at.value(lambda i: J * S.upto(i - 8, *NODES) + j + 1))
                run_phase(act, S, DEPTH1, body)

            @block.vector
            def _(dve):
                V = nc.vector

                def body(at):
                    par = at.i % 2
                    ln1, ln2 = S.kind(at.i - 2) is not None, S.kind(at.i - 4) is not None
                    if ln1 or ln2:
                        r = slice(0 if ln1 else 1, 2 if ln2 else 1)
                        if ln1:
                            at.wait(dve, pe_c, lambda i: i - 1)
                        if ln2:
                            at.wait(dve, pe_e, lambda i: i - 3)
                        V.tensor_copy(stats[:, r], bank[7][:, 0:16].rearrange("p (l s j) -> p l s j", l=2, s=2)[:, r]).then_inc(stats_read, 1)
                        at.wait(dve, stats_read, stat_rounds1)
                        V.tensor_tensor(stats_m2[:, r], stats[:, r, 0, :], stats[:, r, 0, :], ALU.mult).then_inc(stats_sq, 1)
                        at.wait(dve, stats_sq, stat_rounds1)
                        V.tensor_tensor(stats_v[:, r], stats[:, r, 1, :], stats_m2[:, r], ALU.subtract).then_inc(stats_sub, 1)
                    if S.kind(at.i - 5) is not None:
                        at.wait(dve, bn2_done, lambda i: i - 4)
                        V.tensor_scalar(var[:, par, 8:12], bn2[:, (at.i - 5) % 2, :, 1], LN_EPS, None, ALU.add)
                    if S.kind(at.i - 8) in NODES:
                        at.wait(dve, ssq_done, lambda i: J * S.upto(i - 8, *NODES))
                        V.tensor_scalar(var[:, par, 12:16], ssq[:, (at.i - 8) % 2, :], NORM_EPS * NORM_EPS, None, ALU.max)
                    if at.i >= 2:
                        if ln1 or ln2:
                            at.wait(dve, stats_sub, stat_rounds1)
                            V.tensor_scalar(var[:, par, 0:8].rearrange("p (l j) -> p l j", l=2)[:, r], stats_v[:, r], 0.0, LN_EPS,
                                            ALU.max, ALU.add).then_inc(var_done, 1)
                        else:
                            at.idle(dve).then_inc(var_done, 1)
                    if S.kind(at.i) == "edge":
                        e = (at.i % 6) // 3
                        at.wait(dve, pe_ea, lambda i: S.upto(i, "edge"))
                        at.wait(dve, pe_b, lambda i: i - 5)
                        at.wait(dve, agg_done, lambda i: S.upto(i, "edge") - 1)
                        first = at.value(lambda i: (S.upto(i, "edge") - 1) * G)
                        V.tensor_tensor_scan(aggT[:, e, :], same[:, bass.ds(first, G)], bank[5][:, :],
                                             0.0 if at.i < 3 else aggT[:, 1 - e, G - 1:G], ALU.mult, ALU.add).then_inc(agg_done, 1)
                    if at.i >= 2:
                        at.wait(dve, std_done, rounds1)
                        V.reciprocal(inv[:, par, :], std[:, par, :]).then_inc(inv_done, 1)
                        at.wait(dve, inv_done, rounds1)
                    n = at.i - 2
                    if S.kind(n) is not None:
                        at.wait(dve, pe_d, lambda i: i - 3)
                        for j in range(J):
                            ins = V.scalar_tensor_tensor(out=z2[:, n % 2, j, :], in0=bank[2][:, j * F:(j + 1) * F],
                                                         scalar=inv[:, par, j:j + 1], in1=bias2[:, :], op0=ALU.mult, op1=ALU.add)
                        ins.then_inc(z2_done, 1)
                    n = at.i - 4
                    if S.kind(n) is not None:
                        at.wait(dve, xb_done, lambda i: i - 3)
                        at.wait(dve, x1_done, lambda i: i - 5)
                        for j in range(J):
                            ins = V.scalar_tensor_tensor(out=v3[:, n % 2, j, :], in0=bank[4][:, j * F:(j + 1) * F],
                                                         scalar=inv[:, par, 4 + j:5 + j], in1=xg[:, n % 6, j, :], op0=ALU.mult, op1=ALU.add)
                        ins.then_inc(v3_done, 1)
                    n = at.i - 8
                    if S.kind(n) in NODES:
                        at.wait(dve, h1_out[n % 2], lambda i: stored1(i - 10, 2, NODES))
                        for j in range(J):
                            ins = V.tensor_scalar(h1[:, n % 2, j, :], bank[6][:, j * F:(j + 1) * F], 0.0, inv[:, par, 12 + j:13 + j],
                                                  ALU.max, ALU.mult)
                        ins.then_inc(h1_done, 1)
                    n = at.i - 4
                    if S.kind(n) is not None:
                        at.wait(dve, v3_done, lambda i: i - 3)
                        for j in range(J):
                            ins = V.bn_stats(bn6[:, n % 2, j, :], v3[:, n % 2, j, :])
                        ins.then_inc(bn6_done, 1)
                        at.wait(dve, bn6_done, lambda i: i - 3, apart=True)
                        for j in range(J):
                            ins = V.bn_aggr(bn2[:, n % 2, j, :], bn6[:, n % 2, j, :])
                        ins.then_inc(bn2_done, 1)
                run_phase(dve, S, DEPTH1, body)

            @block.gpsimd
            def _(pool):
                Q = nc.gpsimd

                def body(at):
                    n = at.i
                    if S.kind(n) == "edge":
                        at.wait(pool, v3_done, lambda i: i - 5)
                        k = at.value(lambda i: S.upto(i, "edge") - 1)
                        e = (n % 6) // 3
                        Q.tensor_copy(idx_now[:, e, :], x_idx[:, k, :]).then_inc(x_idx_now, 1)
                        at.wait(pool, x_idx_now, lambda i: S.upto(i, "edge"))
                        for j in range(J):
                            Q.indirect_dma_start(out=xg[:, n % 6, j, :], out_offset=None, in_=A["x"],
                                                 in_offset=bass.IndirectOffsetOnAxis(ap=idx_now[:, e, j:j + 1], axis=0),
                                                 bounds_check=N - 1, oob_is_err=False).then_inc(xd_in[e], 16)
                    n = at.i - 5
                    if S.kind(n) is not None:
                        at.wait(pool, inv_done, rounds1)
                        at.wait(pool, pe_f, lambda i: S.upto(i - 8, *NODES))
                        at.wait(pool, x1_out[n % 3], lambda i: stored1(i - 8, 3))
                        for j in range(J):
                            ins = Q.tensor_scalar(x1[:, n % 3, j, :], v3[:, n % 2, j, :], bn2[:, n % 2, j, 0:1],
                                                  inv[:, at.i % 2, 8 + j:9 + j], ALU.subtract, ALU.mult)
                        ins.then_inc(x1_done, 1)
                    n = at.i - 1
                    if S.kind(n) is not None:
                        at.wait(pool, r1_done, lambda i: i)
                        at.wait(pool, pe_c, lambda i: i - 2)
                        Q.tensor_tensor(sq1[:, n % 2, :], r1[:, n % 2, :], r1[:, n % 2, :], ALU.mult).then_inc(sq1_done, 1)
                    n = at.i - 3
                    if S.kind(n) is not None:
                        at.wait(pool, r2_done, lambda i: i - 2)
                        at.wait(pool, pe_e, lambda i: i - 4)
                        Q.tensor_tensor(sq2[:, n % 2, :], r2[:, n % 2, :], r2[:, n % 2, :], ALU.mult).then_inc(sq2_done, 1)
                    n = at.i - 1
                    if S.kind(n) is not None:
                        at.wait(pool, pe_a, lambda i: i)
                        Q.tensor_tensor(xg[:, n % 6], xg[:, n % 6], bias3[:, :, :], ALU.add).then_inc(xb_done, 1)
                run_phase(pool, S, DEPTH1, body)

        scattered = sem("scattered")

        def sage_phase(S, name, first_node, wr_e, wl_e, bias_e, res_e):
            LS = len(S.kinds)
            table = x1_table if not res_e else h1_table
            rin = [sem(f"{name}_rows_in{s}") for s in range(3)]
            xin = [sem(f"{name}_x1_in{s}") for s in range(6)]
            msg_in = [sem(f"{name}_messages_in{s}") for s in range(2)]
            turned, msg_turned, z_ready = sem(f"{name}_turned"), sem(f"{name}_messages_turned"), sem(f"{name}_z")
            rT_done, ss_done, sd_done = sem(f"{name}_rT"), sem(f"{name}_ssq"), sem(f"{name}_std")
            vr_done, iv_done, ag_done, mean_done = sem(f"{name}_var"), sem(f"{name}_inv"), sem(f"{name}_agg"), sem(f"{name}_mean")
            u_done, b6, b2, sum_done, fin_done = sem(f"{name}_u"), sem(f"{name}_bn6"), sem(f"{name}_bn2"), sem(f"{name}_sum"), sem(f"{name}_fin")
            idx_copied = sem(f"{name}_idx_copied")
            stored = [sem(f"{name}_stored{s}") for s in range(3)]
            ALL = ("node", "tail", "edge")
            FULL = ALL if res_e else NODES

            def up(n, *k):
                return S.upto(n, *k)

            def in_slot(n, ring, kinds, w=lambda k: 16):
                return sum(w(S.kind(m)) for m in range(n % ring, n + 1, ring) if S.kind(m) in kinds) if n >= 0 else 0

            STORED = NODES if res_e else ALL

            with nc.Block() as block:
                @block.sync
                def _(sp):
                    def body(at):
                        n = at.i
                        k = S.kind(n)
                        if k in ALL:
                            at.wait(sp, turned, lambda i: up(i - 3))
                            dst = rows[:, n % 3].rearrange("p j f -> p (j f)")
                            dst2 = xg[:, n % 6].rearrange("p j f -> p (j f)")
                            if k in FULL:
                                at.wait(sp, sum_done, lambda i: up(i - 6, *FULL))
                            if k == "edge":
                                g = at.value(lambda i: up(i, "edge") - 1)
                                sp.dma_start(dst, edge_rows(table, g)).then_inc(rin[n % 3], 16)
                                if res_e:
                                    sp.dma_start(dst2, edge_rows(x1_table, g)).then_inc(xin[n % 6], 16)
                            elif k == "tail":
                                sp.dma_start(dst[0:TAIL], tail_rows(h1_table)).then_inc(rin[n % 3], 16)
                                sp.dma_start(dst2[0:TAIL], tail_rows(x1_table)).then_inc(xin[n % 6], 16)
                            else:
                                g = at.value(lambda i: first_node + up(i, "node") - 1)
                                sp.dma_start(dst, node_rows(h1_table, g)).then_inc(rin[n % 3], 16)
                                sp.dma_start(dst2, node_rows(x1_table, g)).then_inc(xin[n % 6], 16)
                        n = at.i - 5
                        k = S.kind(n)
                        if k in NODES:
                            at.wait(sp, fin_done, lambda i: up(i - 5, *FULL))
                            of = x1[:, n % 3].rearrange("p j f -> p (j f)")
                            if k == "tail":
                                sp.dma_start(tail_rows(out), of[0:TAIL]).then_inc(stored[n % 3], 16)
                            else:
                                g = at.value(lambda i: first_node + up(i - 5, "node") - 1)
                                sp.dma_start(node_rows(out, g), of).then_inc(stored[n % 3], 16)
                        elif k == "edge" and not res_e:
                            at.wait(sp, u_done, lambda i: up(i - 5))
                            g = at.value(lambda i: up(i - 5, "edge") - 1)
                            sp.dma_start(edge_rows(h1_table, g), z2[:, (n % 6) // 3].rearrange("p j f -> p (j f)")).then_inc(stored[n % 3], 16)
                    run_phase(sp, S, DEPTH2, body)
                    for s in range(3):
                        last = max(n for n in range(LS) if n % 3 == s)
                        sp.wait_ge(stored[s], in_slot(last, 3, STORED))

                @block.tensor
                def _(pe):
                    def body(at):
                        n = at.i
                        k = S.kind(n)
                        if k in ALL:
                            at.wait(pe, rin[n % 3], lambda i: in_slot(i, 3, ALL))
                            at.wait(pe, rT_done, lambda i: up(i - 2))
                            for j in range(J):
                                mm = pe.transpose(bank[n % 2][:, j * F:(j + 1) * F], rows[:, n % 3, j, :], identity[:, :])
                            mm.then_inc(turned, 1)
                        if k == "edge":
                            e = (n % 6) // 3
                            at.wait(pe, msg_in[e], lambda i: 16 * J * ((up(i, "edge") + 1) // 2))
                            at.wait(pe, ag_done, lambda i: up(i, "edge") - 1)
                            for j in range(J):
                                mm = pe.transpose(bank[2][:, :].rearrange("p (i j) -> p j i", j=J)[:, j, :], ea[:, e, j, :], identity[:, :])
                            mm.then_inc(msg_turned, 1)
                        n = at.i - 1
                        k = S.kind(n)
                        if k in ALL:
                            edge = k == "edge"
                            zb = bank[4 + n % 2]
                            at.wait(pe, rT_done, lambda i: up(i - 1))
                            at.wait(pe, u_done, lambda i: up(i - 3))
                            if edge:
                                at.wait(pe, mean_done, lambda i: up(i - 1, "edge"))
                            b = bias_e if edge else 1
                            for j in range(J):
                                pe.matmul(zb[:, j * F:(j + 1) * F], ones3[:, :], bl_rows[:, b], start=True, stop=False)
                                mm = pe.matmul(zb[:, j * F:(j + 1) * F], x1T[:, n % 2, j * F:(j + 1) * F], wr_e if edge else wr1,
                                               start=False, stop=not edge)
                                if edge:
                                    mm = pe.matmul(zb[:, j * F:(j + 1) * F], r2[:, (n % 6) // 3, j * F:(j + 1) * F], wl_e,
                                                   start=False, stop=True)
                            mm.then_inc(z_ready, 1)
                    run_phase(pe, S, DEPTH2, body)

                @block.scalar
                def _(act):
                    def body(at):
                        if at.i >= 2:
                            at.wait(act, vr_done, rounds1)
                            nc.scalar.activation(std[:, at.i % 2, 0:8], var[:, at.i % 2, 0:8], ACT.Sqrt).then_inc(sd_done, 1)
                        n = at.i
                        if S.kind(n) in ALL:
                            at.wait(act, turned, lambda i: up(i))
                            at.wait(act, z_ready, lambda i: up(i - 2))
                            nc.scalar.copy(x1T[:, n % 2, :], bank[n % 2][:, :]).then_inc(rT_done, 1)
                        n = at.i - 1
                        if S.kind(n) in ALL:
                            at.wait(act, z_ready, lambda i: up(i - 1))
                            at.wait(act, ss_done, lambda i: J * up(i - 2))
                            at.wait(act, vr_done, lambda i: rounds1(i - 1))
                            for j in range(J):
                                nc.scalar.activation(junk[:, j % 2, :], bank[4 + n % 2][:, j * F:(j + 1) * F], ACT.Square,
                                                     accum_out=ssq[:, n % 2, j:j + 1]).then_inc(ss_done, 1)
                                if j < J - 1:
                                    act.wait_ge(ss_done, at.value(lambda i: J * up(i - 2) + j + 1))
                        n = at.i - 4
                        if S.kind(n) in FULL:
                            at.wait(act, iv_done, rounds1)
                            at.wait(act, stored[n % 3], lambda i: in_slot(i - 7, 3, STORED))
                            to = x1[:, n % 3]
                            if S.kind(n) == "edge":
                                to = results[:, at.value(lambda i: up(i - 4, "edge") - 1)]
                            for j in range(J):
                                ins = nc.scalar.activation(to[:, j, :], v3[:, n % 2, j, :], ACT.Identity,
                                                           bias=nmean[:, at.i % 2, j:j + 1], scale=inv[:, at.i % 2, 4 + j:5 + j])
                            ins.then_inc(fin_done, 1)
                    run_phase(act, S, DEPTH2, body)

                @block.vector
                def _(dve):
                    V = nc.vector

                    def body(at):
                        par = at.i % 2
                        if at.i >= 2:
                            if S.kind(at.i - 4) in FULL:
                                at.wait(dve, b2, lambda i: up(i - 4, *FULL))
                                V.tensor_scalar(var[:, par, 4:8], bn2[:, (at.i - 4) % 2, :, 1], LN_EPS, None, ALU.add)
                            if S.kind(at.i - 2) in ALL:
                                at.wait(dve, ss_done, lambda i: J * up(i - 2))
                                V.tensor_scalar(var[:, par, 0:4], ssq[:, (at.i - 2) % 2, :], NORM_EPS * NORM_EPS, None,
                                                ALU.max).then_inc(vr_done, 1)
                            else:
                                at.idle(dve).then_inc(vr_done, 1)
                        if S.kind(at.i) == "edge":
                            e = (at.i % 6) // 3
                            at.wait(dve, msg_turned, lambda i: up(i, "edge"))
                            at.wait(dve, mean_done, lambda i: up(i, "edge") - 1)
                            first = at.value(lambda i: (up(i, "edge") - 1) * G)
                            V.tensor_tensor_scan(aggT[:, e, :], same[:, bass.ds(first, G)], bank[2][:, :],
                                                 0.0 if at.i < 3 else aggT[:, 1 - e, G - 1:G], ALU.mult, ALU.add).then_inc(ag_done, 1)
                            at.wait(dve, z_ready, lambda i: up(i - 6))
                            at.wait(dve, ag_done, lambda i: up(i, "edge"))
                            V.tensor_tensor(r2[:, e, :].rearrange("p (j i) -> p j i", j=J),
                                            aggT[:, e, :].rearrange("p (i j) -> p j i", j=J),
                                            inv_count[:, bass.ds(first, G)].rearrange("p (i j) -> p j i", j=J), ALU.mult).then_inc(mean_done, 1)
                        if at.i >= 2:
                            at.wait(dve, sd_done, rounds1)
                            V.reciprocal(inv[:, par, 0:8], std[:, par, 0:8]).then_inc(iv_half, 1)
                            dve.wait_ge(iv_half, at.value(lambda i: i - 1 + iv_base[name]))
                            if S.kind(at.i - 4) in FULL:
                                V.scalar_tensor_tensor(out=nmean[:, par, :], in0=bn2[:, (at.i - 4) % 2, :, 0], scalar=-1.0,
                                                       in1=inv[:, par, 4:8], op0=ALU.mult, op1=ALU.mult).then_inc(iv_done, 1)
                            else:
                                at.idle(dve).then_inc(iv_done, 1)
                        n = at.i - 2
                        if S.kind(n) in ALL:
                            full = S.kind(n) in FULL
                            u = v3[:, n % 2] if full else z2[:, (n % 6) // 3]
                            if full:
                                at.wait(dve, fin_done, lambda i: up(i - 4, *FULL))
                            else:
                                at.wait(dve, stored[n % 3], lambda i: in_slot(i - 8, 3, STORED))
                            for j in range(J):
                                ins = V.tensor_scalar(u[:, j, :], bank[4 + n % 2][:, j * F:(j + 1) * F], 0.0,
                                                      inv[:, par, j:j + 1], ALU.max, ALU.mult)
                            ins.then_inc(u_done, 1)
                        n = at.i - 3
                        if S.kind(n) in FULL:
                            at.wait(dve, sum_done, lambda i: up(i - 3, *FULL))
                            for j in range(J):
                                ins = V.bn_stats(bn6[:, n % 2, j, :], v3[:, n % 2, j, :])
                            ins.then_inc(b6, 1)
                            at.wait(dve, b6, lambda i: up(i - 3, *FULL), apart=True)
                            for j in range(J):
                                ins = V.bn_aggr(bn2[:, n % 2, j, :], bn6[:, n % 2, j, :])
                            ins.then_inc(b2, 1)
                    run_phase(dve, S, DEPTH2, body)

                @block.gpsimd
                def _(pool):
                    Q = nc.gpsimd

                    def body(at):
                        n = at.i
                        if S.kind(n) == "edge":
                            e = (n % 6) // 3
                            g = at.value(lambda i: up(i, "edge") - 1)
                            at.wait(pool, msg_turned, lambda i: up(i, "edge") - 2)
                            Q.tensor_copy(idx_now[:, e, :], row_idx[:, g, :]).then_inc(idx_copied, 1)
                            at.wait(pool, idx_copied, lambda i: up(i, "edge"))
                            for j in range(J):
                                Q.indirect_dma_start(out=ea[:, e, j, :], out_offset=None, in_=table,
                                                     in_offset=bass.IndirectOffsetOnAxis(ap=idx_now[:, e, j:j + 1], axis=0),
                                                     bounds_check=ROWS - 1, oob_is_err=False).then_inc(msg_in[e], 16)
                        n = at.i - 2
                        if S.kind(n) in FULL:
                            at.wait(pool, u_done, lambda i: up(i - 2))
                            at.wait(pool, xin[n % 6], lambda i: in_slot(i - 2, 6, FULL))
                            Q.tensor_tensor(v3[:, n % 2], v3[:, n % 2], xg[:, n % 6], ALU.add).then_inc(sum_done, 1)
                    run_phase(pool, S, DEPTH2, body)
                    if res_e:
                        pool.wait_ge(fin_done, up(LS, *FULL))
                        for s in range(3):
                            last = max(n for n in range(LS) if n % 3 == s)
                            pool.wait_ge(stored[s], in_slot(last, 3, STORED))
                        for g in range(EG):
                            for j in range(J):
                                Q.indirect_dma_start(out=out, out_offset=bass.IndirectOffsetOnAxis(ap=out_idx[:, g, j:j + 1], axis=0),
                                                     in_=results[:, g, j, :], in_offset=None,
                                                     bounds_check=N - 1, oob_is_err=False).then_inc(scattered, 16)
                        pool.wait_ge(scattered, 16 * J * EG)

        iv_half = sem("inv_half")
        iv_base = {"p2": 0, "p3": len(phase2.kinds) + DEPTH2 - 2}
        sage_phase(phase2, "p2", 0, wr0, wl0, 0, False)
        sage_phase(phase3, "p3", half, wr1, wl1, 1, True)


_INS = ['x', 'src', 'dst', 'edge_attr_128', 'L0_gnn_u', 'L0_gnn_W1', 'L0_gnn_b1', 'L0_gnn_g1', 'L0_gnn_be1', 'L0_gnn_W2',
        'L0_gnn_b2', 'L0_gnn_g2', 'L0_gnn_be2', 'L0_gnn_W3', 'L0_gnn_b3', 'L1_gnn_W_l0', 'L1_gnn_b_l0', 'L1_gnn_W_r0',
        'L1_gnn_W_l1', 'L1_gnn_b_l1', 'L1_gnn_W_r1']


def kernel(**inputs):
    import numpy as _np
    import concourse.bacc as _bacc
    from concourse import mybir as _mybir
    from concourse.bass_utils import run_bass_kernel_spmd as _run

    nc = _bacc.Bacc("TRN2", target_bir_lowering=False, num_devices=1)
    arrays, args = {}, {}
    for name in _INS:
        a = _np.ascontiguousarray(inputs[name])
        arrays[f"in_{name}_dram"] = a
        args[name] = nc.dram_tensor(f"in_{name}_dram", a.shape, _mybir.dt.from_np(a.dtype), kind="ExternalInput").ap()
    out = nc.dram_tensor("out_0_dram", arrays["in_x_dram"].shape, _mybir.dt.float32, kind="ExternalOutput").ap()
    build(nc, args, out)
    r = _run(nc, [arrays], core_ids=[0])
    return r.results[0]["out_0_dram"]
```

```python
from contextlib import ExitStack

import concourse.bass as bass
from concourse import mybir

F32 = mybir.dt.float32
BF16 = mybir.dt.bfloat16
I32 = mybir.dt.int32
ALU = mybir.AluOpType
ACT = mybir.ActivationFunctionType

P = 128
J = 4
G = P * J
F = 128
U = 6
LN_EPS = 1e-5
NORM_EPS = 1e-12


class Schedule:

    def __init__(self, kinds):
        self.kinds = kinds

    def kind(self, n):
        return self.kinds[n] if 0 <= n < len(self.kinds) else None

    def upto(self, n, *which):
        which = which or ("node", "tail", "edge")
        return sum(k in which for k in self.kinds[:max(n + 1, 0)])


class Place:

    APART = (mybir.EngineType.Pool, mybir.EngineType.SP)
    passed = None

    def __init__(self, i, turns=1, reg=None):
        self.i, self.turns, self.reg = i, turns, reg

    def value(self, f):
        a = f(self.i)
        if self.reg is None:
            return a
        step = f(self.i + U) - a
        assert all(f(self.i + U * t) == a + step * t for t in range(self.turns))
        return a + self.reg * step if step else a

    def wait(self, eng, sem, f, apart=False):
        if f(self.i) > 0:
            eng.wait_ge(sem, self.value(f))
            if self.reg is not None and (apart or eng.engine in self.APART):
                eng.sem_inc(self.passed, 1)
        else:
            assert f(self.i + U * (self.turns - 1)) <= 0

    def idle(self, eng):
        if self.reg is not None:
            eng.sem_inc(self.passed, 1)
        return eng.drain()


def run_phase(eng, sched, depth, body):
    length = len(sched.kinds) + depth
    blocks = -(-length // U)

    def pattern(b):
        return [sched.kind(n) for n in range(b * U - depth, b * U + U)]

    b = 0
    while b < blocks:
        e = b + 1
        if b * U - depth >= U:
            while e < blocks and pattern(e) == pattern(b) and (e + 1) * U <= len(sched.kinds):
                e += 1
        if e - b >= 2:
            with eng.Fori(0, e - b) as turn:
                for u in range(U):
                    body(Place(b * U + u, e - b, turn))
        else:
            e = b + 1
            for i in range(b * U, min(e * U, length)):
                body(Place(i))
        b = e


def build(nc, A, out, debug=None):
    N = A["x"].shape[0]
    E = A["src"].shape[0]
    NG = N // G
    TAIL = (N - NG * G) // J
    assert (N - NG * G) % J == 0 and E % J == 0
    EG = -(-E // G)
    SLOTS = EG * G
    ETAIL = (E - (EG - 1) * G) // J
    H = -(-N // P)
    ROWS = N + SLOTS
    D_U = A["L0_gnn_u"].shape[1]

    half = 2 * EG
    rest = NG + 1 - half
    phase1 = Schedule((["node", "node", "edge"] * EG + ["node"] * rest)[:-1] + ["tail"])
    phase2 = Schedule(["node", "node", "edge"] * EG)
    third = ["node"] * (rest - 1) + ["tail"] + ["none"] * (2 * EG - rest)
    phase3 = Schedule([k for d in range(EG) for k in (third[2 * d], third[2 * d + 1], "edge")])
    DEPTH1, DEPTH2 = 8, 5

    with ExitStack() as ctx:
        def sb(name, shape, dt=F32):
            return ctx.enter_context(nc.sbuf_tensor(name, shape, dt))

        def ps(name, shape):
            return ctx.enter_context(nc.psum_tensor(name, shape, F32))

        def sem(name):
            return ctx.enter_context(nc.semaphore(name))

        x1_table = nc.dram_tensor("x1_table", [ROWS, F], F32, kind="Internal").ap()
        h1_table = nc.dram_tensor("h1_table", [ROWS, F], F32, kind="Internal").ap()

        def node_rows(table, k):
            return table[0:NG * G].rearrange("(g p j) f -> g p (j f)", p=P, j=J)[k]

        def tail_rows(table):
            return table[NG * G:N].rearrange("(p j) f -> p (j f)", j=J)

        def edge_rows(table, k):
            return table[N:ROWS].rearrange("(g p j) f -> g p (j f)", p=P, j=J)[k]

        wbuf = sb("wbuf", [P, 8, F])
        w1x, w1e, w2c, w3c, wr0, wl0, wr1, wl1 = [wbuf[:, i, :] for i in range(8)]
        xg = sb("xg", [P, 6, J, F])
        spare = xg[:, :, :, :].rearrange("p s j f -> p (s j f)")
        raw = spare[:, 0:6 * F].rearrange("p (w f) -> p w f", w=6)
        be_wide, brow, scaled, bl_wide, bl_tmp = [spare[:, (6 + 2 * i) * F:(8 + 2 * i) * F].rearrange("p (w f) -> p w f", w=2)
                                                  for i in range(5)]
        centre = spare[:, 16 * F:17 * F]
        bl_part = spare[:, 17 * F:20 * F].bitcast(BF16).rearrange("p (a w f) -> p a w f", a=3, w=2)
        w1u = sb("w1u", [D_U, F])
        u_col = sb("u_col", [D_U, 1])
        cols = sb("cols", [P, 6])
        c1 = cols[:, 5:6]
        bias2 = sb("bias2", [P, F])
        bias3 = sb("bias3", [P, J, F])
        identity = sb("identity", [P, P])
        avg = sb("avg", [P, 2])
        bl_rows = sb("bl_rows", [96, 2, F], BF16)
        ones3 = sb("ones3", [96, P], BF16)

        src_c = sb("src_c", [P, EG, J], I32)
        dst_c = sb("dst_c", [P, EG, J], I32)
        next_c = sb("next_c", [P, EG, J], I32)
        x_idx = sb("x_idx", [P, EG, J], I32)
        row_idx = sb("row_idx", [P, EG, J], I32)
        out_idx = sb("out_idx", [P, EG, J], I32)
        same = sb("same", [P, SLOTS], BF16)
        inv_count = sb("inv_count", [P, SLOTS])
        int_c = sb("int_c", [P, EG, J], I32)
        fc = sb("fc", [P, 8, EG, J])
        dst_f, is_last, e_high, e_low, src_f, src_hi, dst_hi, dst_lo = [fc[:, i] for i in range(8)]
        idx_now = sb("idx_now", [P, 2, J], I32)
        found = sb("found", [P, EG, J])
        fsel = sb("fsel", [P, 2, EG, J])
        iota_hi = sb("iota_hi", [P, H])
        iota_lo = sb("iota_lo", [P, P], BF16)
        iota_p = sb("iota_p", [P, 1])
        ones = sb("ones", [P, G], BF16)
        dst_row = sb("dst_row", [P, 2, G + 1], I32)
        src_row = sb("src_row", [P, 2, G], I32)
        src_low = sb("src_low", [P, G], I32)
        count = sb("count", [P, 2, G])
        slot_sum = sb("slot_sum", [P, H])
        slot_table = sb("slot_table", [P, 2, H], BF16)
        results = sb("results", [P, EG, J, F])
        wide = results[:, :, :, :].rearrange("p g j f -> p (g j f)")
        hot_src = wide[:, 12 * G:12 * G + SLOTS // 2].bitcast(BF16)

        ea = sb("ea", [P, 2, J, F])
        aggT = sb("aggT", [P, 2, G])
        r2 = sb("r2", [P, 2, G])
        v3 = sb("v3", [P, 2, J, F])
        x1 = sb("x1", [P, 3, J, F])
        x1T = sb("x1T", [P, 2, G])
        rows = sb("rows", [P, 3, J, F])
        hot_words = rows[:, :, :, :].rearrange("p s j f -> p (s j f)").bitcast(BF16)
        hot_hi = hot_words[:, 0:J * H].rearrange("p (j h) -> p j h", j=J)
        hot_lo = hot_words[:, 2048:2048 + 2 * J * P].rearrange("p (j a l) -> p j a l", j=J, a=2)
        slot_int = v3[:, :, :, :].rearrange("p s j f -> p (s j f)").bitcast(I32)[:, 0:2 * H].rearrange("p (a h) -> p a h", a=2)
        entries = r2[:, :, :].rearrange("p s n -> p (s n)")[:, 0:2 * H].rearrange("p (a h) -> p a h", a=2)
        early = wide[:, 0:12 * G].rearrange("p (b r n) -> p b r n", b=6, r=2)
        xT, r1, sq1, sq2 = [early[:, b] for b in range(4)]
        z2, h1 = [early[:, b].rearrange("p r (j f) -> p r j f", j=J) for b in (4, 5)]
        junk = sb("junk", [P, 4, F])
        ssq = sb("ssq", [P, 2, J])
        stats = sb("stats", [P, 2, 2, J])
        stats_m2 = sb("stats_m2", [P, 2, J])
        stats_v = sb("stats_v", [P, 2, J])
        bn6 = sb("bn6", [P, 2, J, 6])
        bn2 = sb("bn2", [P, 2, J, 2])
        nmean = sb("nmean", [P, 2, J])
        var = sb("var", [P, 2, 16])
        std = sb("std", [P, 2, 16])
        inv = sb("inv", [P, 2, 16])

        bank = [ps(f"bank{i}", [P, G]) for i in range(8)]

        Place.passed = sem("passed")

        w_in = [sem(f"w_in{i}") for i in range(3)]
        consts = sem("consts")
        prep_v = sem("prep_v")
        prep_p = sem("prep_p")
        rows_in = sem("rows_in")
        dst_in = sem("dst_in")
        table_copied = sem("table_copied")
        looked_up = sem("looked_up")
        selected = sem("selected")
        prologue_done = sem("prologue_done")
        chain = sem("chain")

        with nc.Block() as block:
            @block.sync
            def _(sp):
                sp.dma_start(raw[:, 0, :], A["L0_gnn_W2"]).then_inc(w_in[0], 16)
                sp.dma_start(raw[:, 1, :], A["L0_gnn_W3"]).then_inc(w_in[0], 16)
                for i, name in enumerate(["L1_gnn_W_r0", "L1_gnn_W_l0", "L1_gnn_W_r1", "L1_gnn_W_l1"]):
                    sp.dma_start(raw[:, 2 + i, :], A[name]).then_inc(w_in[0], 16)
                sp.dma_start(w1x, A["L0_gnn_W1"][0:F, :]).then_inc(w_in[0], 16)
                sp.dma_start(w1e, A["L0_gnn_W1"][F:2 * F, :]).then_inc(w_in[0], 16)
                sp.dma_start(w1u[:, :], A["L0_gnn_W1"][2 * F:2 * F + D_U, :]).then_inc(w_in[0], 16)
                sp.dma_start(u_col[:, :], A["L0_gnn_u"].rearrange("a d -> d a")).then_inc(w_in[0], 16)
                for i, name in enumerate(["b1", "g1", "be1", "g2", "be2"]):
                    sp.dma_start(cols[:, i:i + 1], A["L0_gnn_" + name].rearrange("(d a) -> d a", a=1)).then_inc(w_in[0], 16)
                for i, name in enumerate(["b2", "b3"]):
                    row = A["L0_gnn_" + name].rearrange("(a d) -> a d", a=1)
                    sp.dma_start(brow[:, i, :], row.to_broadcast([P, F])).then_inc(w_in[0], 16)
                for i, name in enumerate(["b_l0", "b_l1"]):
                    row = A["L1_gnn_" + name].rearrange("(a d) -> a d", a=1)
                    sp.dma_start(bl_wide[0:96, i, :], row.to_broadcast([96, F])).then_inc(w_in[0], 16)
                sp.wait_ge(consts, 1)
                whole = (EG - 1) * G
                for sbuf, name in ((src_c, "src"), (dst_c, "dst")):
                    sp.dma_start(sbuf[:, 0:EG - 1, :], A[name][0:whole].rearrange("(g p j) -> p g j", p=P, j=J)).then_inc(dst_in, 16)
                    sp.dma_start(sbuf[0:ETAIL, EG - 1, :], A[name][whole:E].rearrange("(p j) -> p j", j=J)).then_inc(dst_in, 16)
                sp.dma_start(next_c[:, 0:EG - 1, :], A["dst"][1:whole + 1].rearrange("(g p j) -> p g j", p=P, j=J)).then_inc(dst_in, 16)
                sp.dma_start(next_c[0:ETAIL - 1, EG - 1, :], A["dst"][whole + 1:E - J + 1].rearrange("(p j) -> p j", j=J)).then_inc(dst_in, 16)
                sp.dma_start(next_c[ETAIL - 1:ETAIL, EG - 1, 0:J - 1], A["dst"][E - J + 1:E].rearrange("(p j) -> p j", p=1)).then_inc(dst_in, 16)

            W_LOADS = 16 * (6 + 4 + 5 + 2 + 2)

            @block.gpsimd
            def _(pool):
                nc.gpsimd.memset(src_c[:, :, :], 0)
                nc.gpsimd.memset(dst_c[:, :, :], -1)
                nc.gpsimd.memset(dst_row[:, 0, 0:1], -2)
                nc.gpsimd.memset(next_c[:, :, :], -1).then_inc(prep_p, 1)
                pool.wait_ge(prep_p, 1)
                nc.gpsimd.iota(int_c[:, :, :], pattern=[[G, EG], [1, J]], base=1, channel_multiplier=J).then_inc(consts, 1)
                nc.gpsimd.memset(identity[:, :], 0.0).then_inc(prep_p, 1)
                nc.gpsimd.memset(centre[:, :], -1.0 / F).then_inc(prep_p, 1)
                pool.wait_ge(prep_p, 3)
                nc.gpsimd.affine_select(out=identity[:, :], in_=identity[:, :], compare_op=ALU.not_equal, fill=1.0,
                                        base=0, pattern=[[-1, P]], channel_multiplier=1).then_inc(consts, 1)
                nc.gpsimd.affine_select(out=centre[:, :], in_=centre[:, :], compare_op=ALU.not_equal, fill=1.0 - 1.0 / F,
                                        base=0, pattern=[[-1, P]], channel_multiplier=1).then_inc(consts, 1)
                nc.gpsimd.iota(iota_hi[:, :], pattern=[[1, H]], base=0, channel_multiplier=0,
                               allow_small_or_imprecise_dtypes=True).then_inc(consts, 1)
                nc.gpsimd.iota(iota_lo[:, :], pattern=[[1, P]], base=0, channel_multiplier=0,
                               allow_small_or_imprecise_dtypes=True).then_inc(consts, 1)
                nc.gpsimd.iota(iota_p[:, :], pattern=[[0, 1]], base=0, channel_multiplier=1,
                               allow_small_or_imprecise_dtypes=True).then_inc(consts, 1)
                nc.gpsimd.memset(ones3[:, :], 1.0).then_inc(consts, 1)
                nc.gpsimd.memset(avg[:, :], 1.0 / F).then_inc(consts, 1)
                nc.gpsimd.memset(bl_rows[:, :, :], 0.0).then_inc(consts, 1)
            CONSTS = 9

            @block.tensor
            def _(pe):
                pe.wait_ge(consts, CONSTS)
                pe.wait_ge(w_in[0], W_LOADS)
                for i in range(4):
                    pe.transpose(bank[0][:, i * F:(i + 1) * F], raw[:, 2 + i, :], identity[:, :])
                pe.matmul(bank[1][:, 0:1], w1u[:, :], u_col[:, :], start=True, stop=True)
                pe.wait_ge(prep_v, 2)
                pe.matmul(bank[2][:, 0:F], centre[:, :], scaled[:, 0, :], start=True, stop=True)
                pe.matmul(bank[2][:, F:2 * F], centre[:, :], scaled[:, 1, :], start=True, stop=True)
                pe.matmul(bank[3][:, 0:F], be_wide[:, 0, :], raw[:, 0, :], start=True, stop=True)
                pe.matmul(bank[3][:, F:2 * F], be_wide[:, 1, :], raw[:, 1, :], start=True, stop=True).then_inc(prep_p, 1)

            @block.vector
            def _(dve):
                links = [0]

                def link(ins):
                    links[0] += 1
                    ins.then_inc(chain, 1)
                    dve.wait_ge(chain, links[0])

                V = nc.vector
                dve.wait_ge(w_in[0], W_LOADS)
                dve.wait_ge(consts, CONSTS)
                V.memset(slot_sum[:, :], 0.0)
                V.memset(ones[:, :], 1.0)
                V.memset(be_wide[:, :, :], 0.0).then_inc(prep_v, 1)
                V.memset(var[:, :, :], 1.0)
                dve.wait_ge(prep_v, 1)
                for i in range(2):
                    V.tensor_scalar(scaled[:, i, :], raw[:, i, :], cols[:, 1 + 2 * i:2 + 2 * i], None, ALU.mult)
                    last = V.tensor_scalar(be_wide[:, i, :], be_wide[:, i, :], cols[:, 2 + 2 * i:3 + 2 * i], None, ALU.add)
                last.then_inc(prep_v, 1)
                link(V.tensor_copy(bl_part[0:96, 0], bl_wide[0:96]))
                link(V.tensor_tensor(bl_tmp[0:96], bl_wide[0:96], bl_part[0:96, 0], ALU.subtract))
                link(V.tensor_copy(bl_part[0:96, 1], bl_tmp[0:96]))
                link(V.tensor_tensor(bl_tmp[0:96], bl_tmp[0:96], bl_part[0:96, 1], ALU.subtract))
                link(V.tensor_copy(bl_part[0:96, 2], bl_tmp[0:96]))
                for part in range(3):
                    r = slice(32 * part, 32 * part + 1)
                    link(V.tensor_copy(bl_rows[r], bl_part[r, part]))
                dve.wait_ge(prep_p, 4)
                V.tensor_copy(wbuf[:, 4:8, :], bank[0][:, :].rearrange("p (w f) -> p w f", w=4))
                V.tensor_tensor(c1, bank[1][:, 0:1], cols[:, 0:1], ALU.add)
                V.tensor_copy(wbuf[:, 2:4, :], bank[2][:, 0:2 * F].rearrange("p (w f) -> p w f", w=2))
                V.tensor_tensor(bias2[:, :], bank[3][:, 0:F], brow[:, 0, :], ALU.add)
                for j in range(J):
                    link(V.tensor_tensor(bias3[:, j, :], bank[3][:, F:2 * F], brow[:, 1, :], ALU.add))

                dve.wait_ge(dst_in, 16 * 7)
                next_f = fsel[:, 0]
                V.tensor_copy(src_f, src_c[:, :, :])
                V.tensor_copy(dst_f, dst_c[:, :, :])
                link(V.tensor_copy(next_f, next_c[:, :, :]))
                link(V.tensor_tensor(is_last, dst_f, next_f, ALU.not_equal))
                link(V.tensor_scalar(x_idx[:, :, :], dst_f, 0.0, None, ALU.max))
                link(V.tensor_scalar(fsel[:, 1], is_last, -float(N + P), float(N + P), ALU.mult, ALU.add))
                link(V.tensor_tensor(fsel[:, 1], fsel[:, 1], x_idx[:, :, :], ALU.add))
                link(V.tensor_copy(out_idx[:, :, :], fsel[:, 1]))
                tmp = row_idx
                for of, op, by, to in ((int_c, ALU.bitwise_and, P - 1, e_low), (int_c, ALU.bitwise_and, -P, e_high),
                                       (src_c, ALU.logical_shift_right, 7, src_hi), (x_idx, ALU.bitwise_and, P - 1, dst_lo),
                                       (x_idx, ALU.logical_shift_right, 7, dst_hi)):
                    link(V.tensor_scalar(tmp[:, :, :], of[:, :, :], by, None, op))
                    link(V.tensor_copy(to, tmp[:, :, :]))
                link(V.tensor_tensor(e_low, e_low, is_last, ALU.mult))
                link(V.tensor_tensor(e_high, e_high, is_last, ALU.mult))

        S = phase1
        x_in = [sem(f"x_in{s}") for s in range(6)]
        xd_in = [sem(f"xd_in{s}") for s in range(2)]
        ea_in = [sem(f"ea_in{s}") for s in range(2)]
        pe_a, pe_ea, pe_b, pe_c, pe_d, pe_e, pe_f, pe_g = [sem("pe_" + c) for c in ("x_turned", "ea_turned", "y1", "y2_stats", "z2_turned", "y3_stats", "x1_turned", "z_sage")]
        xT_done, r1_done, r2_done, x1T_done, std_done, ssq_done = [sem(c) for c in ("xT_done", "r1_done", "r2_done", "x1T_done", "std_done", "ssq_done")]
        stats_read, stats_sq, stats_sub, var_done, inv_done = [sem(c) for c in ("stats_read", "stats_sq", "stats_sub", "var_done", "inv_done")]
        agg_done, z2_done, v3_done, bn6_done, bn2_done, h1_done = [sem(c) for c in ("agg_done", "z2_done", "v3_done", "bn6_done", "bn2_done", "h1_done")]
        sq1_done, sq2_done, xb_done, x1_done = [sem(c) for c in ("sq1_done", "sq2_done", "xb_done", "x1_done")]
        x_idx_now = sem("x_idx_now")
        dst_row_in = [sem(f"dst_row_in{s}") for s in range(2)]
        src_row_in = [sem(f"src_row_in{s}") for s in range(2)]
        same_done, count_done, inv_count_done, low_done = sem("same_done"), sem("count_done"), sem("inv_count_done"), sem("low_done")
        hot_ready, hot_src_done, table_part, table_added = sem("hot_ready"), sem("hot_src_done"), sem("table_part"), sem("table_added")
        x1_out = [sem(f"x1_out{s}") for s in range(3)]
        h1_out = [sem(f"h1_out{s}") for s in range(2)]

        NODES = ("node", "tail")
        TABLE = 64
        L1 = len(S.kinds)

        def loaded1(n):
            return 16 * sum(S.kind(m) in NODES for m in range(n % 6, n + 1, 6))

        def rounds1(i):
            return i - 1

        def stat_rounds1(i):
            return min(i, L1 + 3) - 1

        def stored1(n, ring, kinds=("node", "tail", "edge")):
            return 16 * sum(S.kind(m) in kinds for m in range(n % ring, n + 1, ring)) if n >= 0 else 0

        def row_of(list_, first, size):
            return list_.rearrange("(a e) -> a e", a=1)[:, bass.ds(first, size)].to_broadcast([P, size])

        with nc.Block() as block:
            @block.sync
            def _(sp):
                def body(at):
                    n = at.i
                    if S.kind(n) is not None:
                        if S.kind(n) == "edge":
                            e = (n % 6) // 3
                            k = at.value(lambda i: S.upto(i, "edge") - 1)
                            at.wait(sp, same_done, lambda i: S.upto(i, "edge") - 2)
                            if n == 2:
                                sp.dma_start(dst_row[:, e, 1:G + 1], row_of(A["dst"], 0, G)).then_inc(dst_row_in[e], 16)
                            elif n == 3 * EG - 1:
                                size = E - (EG - 1) * G + 1
                                sp.dma_start(dst_row[:, e, 0:size], row_of(A["dst"], E - size, size)).then_inc(dst_row_in[e], 16)
                            else:
                                first = at.value(lambda i: (S.upto(i, "edge") - 1) * G - 1)
                                sp.dma_start(dst_row[:, e, :], row_of(A["dst"], first, G + 1)).then_inc(dst_row_in[e], 16)
                            at.wait(sp, low_done, lambda i: S.upto(i, "edge") - 2)
                            size = E - (EG - 1) * G if n == 3 * EG - 1 else G
                            first = at.value(lambda i: (S.upto(i, "edge") - 1) * G)
                            sp.dma_start(src_row[:, e, 0:size], row_of(A["src"], first, size)).then_inc(src_row_in[e], 16)
                            at.wait(sp, pe_ea, lambda i: S.upto(i, "edge") - 2)
                            if n == 3 * EG - 1:
                                sp.dma_start(ea[0:ETAIL, e].rearrange("p j f -> p (j f)"),
                                             A["edge_attr_128"][(EG - 1) * G:E].rearrange("(p j) f -> p (j f)", j=J)).then_inc(ea_in[e], 16)
                            else:
                                sp.dma_start(ea[:, e].rearrange("p j f -> p (j f)"),
                                             A["edge_attr_128"][0:(EG - 1) * G].rearrange("(g p j) f -> g p (j f)", p=P, j=J)[k]).then_inc(ea_in[e], 16)
                        else:
                            at.wait(sp, v3_done, lambda i: i - 5)
                            dst = xg[:, n % 6].rearrange("p j f -> p (j f)")
                            if S.kind(n) == "tail":
                                sp.dma_start(dst[0:TAIL], tail_rows(A["x"])).then_inc(x_in[n % 6], 16)
                            else:
                                k = at.value(lambda i: S.upto(i, "node") - 1)
                                sp.dma_start(dst, node_rows(A["x"], k)).then_inc(x_in[n % 6], 16)
                    n = at.i - 6
                    if S.kind(n) is not None:
                        at.wait(sp, x1_done, lambda i: i - 5)
                        of = x1[:, n % 3].rearrange("p j f -> p (j f)")
                        if S.kind(n) == "tail":
                            sp.dma_start(tail_rows(x1_table), of[0:TAIL]).then_inc(x1_out[n % 3], 16)
                        elif S.kind(n) == "edge":
                            k = at.value(lambda i: S.upto(i - 6, "edge") - 1)
                            sp.dma_start(edge_rows(x1_table, k), of).then_inc(x1_out[n % 3], 16)
                        else:
                            k = at.value(lambda i: S.upto(i - 6, "node") - 1)
                            sp.dma_start(node_rows(x1_table, k), of).then_inc(x1_out[n % 3], 16)
                    n = at.i - 9
                    if S.kind(n) in NODES:
                        at.wait(sp, h1_done, lambda i: S.upto(i - 9, *NODES))
                        of = h1[:, n % 2].rearrange("p j f -> p (j f)")
                        if S.kind(n) == "tail":
                            sp.dma_start(tail_rows(h1_table), of[0:TAIL]).then_inc(h1_out[n % 2], 16)
                        else:
                            k = at.value(lambda i: S.upto(i - 9, "node") - 1)
                            sp.dma_start(node_rows(h1_table, k), of).then_inc(h1_out[n % 2], 16)
                run_phase(sp, S, DEPTH1 + 1, body)
                for s in range(3):
                    last = max(n for n in range(L1) if n % 3 == s)
                    sp.wait_ge(x1_out[s], stored1(last, 3))
                for s in range(2):
                    last = max(n for n in range(L1) if n % 2 == s)
                    sp.wait_ge(h1_out[s], stored1(last, 2, NODES))

            @block.tensor
            def _(pe):
                def body(at):
                    n = at.i - 2
                    if S.kind(n) is not None:
                        at.wait(pe, r1_done, lambda i: i - 1)
                        at.wait(pe, sq1_done, lambda i: i - 1)
                        at.wait(pe, z2_done, lambda i: i - 2)
                        at.wait(pe, stats_read, lambda i: stat_rounds1(i - 1))
                        for j in range(J):
                            pe.matmul(bank[2][:, j * F:(j + 1) * F], r1[:, n % 2, j * F:(j + 1) * F], w2c, start=True, stop=True)
                            pe.matmul(bank[7][:, j:j + 1], r1[:, n % 2, j * F:(j + 1) * F], avg[:, 0:1], start=True, stop=True)
                        for j in range(J):
                            mm = pe.matmul(bank[7][:, 4 + j:5 + j], sq1[:, n % 2, j * F:(j + 1) * F], avg[:, 0:1], start=True, stop=True)
                        mm.then_inc(pe_c, 1)
                    n = at.i - 4
                    if S.kind(n) is not None:
                        at.wait(pe, r2_done, lambda i: i - 3)
                        at.wait(pe, sq2_done, lambda i: i - 3)
                        at.wait(pe, v3_done, lambda i: i - 4)
                        at.wait(pe, stats_read, lambda i: stat_rounds1(i - 1))
                        for j in range(J):
                            pe.matmul(bank[4][:, j * F:(j + 1) * F], r2[:, n % 2, j * F:(j + 1) * F], w3c, start=True, stop=True)
                            pe.matmul(bank[7][:, 8 + j:9 + j], r2[:, n % 2, j * F:(j + 1) * F], avg[:, 0:1], start=True, stop=True)
                        for j in range(J):
                            mm = pe.matmul(bank[7][:, 12 + j:13 + j], sq2[:, n % 2, j * F:(j + 1) * F], avg[:, 0:1], start=True, stop=True)
                        mm.then_inc(pe_e, 1)
                    n = at.i
                    if S.kind(n) is not None:
                        if S.kind(n) == "edge":
                            at.wait(pe, xd_in[(n % 6) // 3], lambda i: 16 * J * ((S.upto(i, "edge") + 1) // 2))
                        else:
                            at.wait(pe, x_in[n % 6], loaded1)
                        at.wait(pe, xT_done, lambda i: i)
                        for j in range(J):
                            mm = pe.transpose(bank[0][:, j * F:(j + 1) * F], xg[:, n % 6, j, :], identity[:, :])
                        mm.then_inc(pe_a, 1)
                        if S.kind(n) == "edge":
                            at.wait(pe, ea_in[(n % 6) // 3], lambda i: 16 * ((S.upto(i, "edge") + 1) // 2))
                            at.wait(pe, agg_done, lambda i: S.upto(i, "edge") - 1)
                            at.wait(pe, x1T_done, lambda i: S.upto(i - 7, *NODES))
                            for j in range(J):
                                mm = pe.transpose(bank[5][:, :].rearrange("p (i j) -> p j i", j=J)[:, j, :],
                                                  ea[:, (n % 6) // 3, j, :], identity[:, :])
                            mm.then_inc(pe_ea, 1)
                    n = at.i - 1
                    if S.kind(n) is not None:
                        at.wait(pe, xT_done, lambda i: i)
                        at.wait(pe, r1_done, lambda i: i - 1)
                        edge = S.kind(n) == "edge"
                        mm = pe.matmul(bank[1][:, :], w1x, xT[:, n % 2, :], start=True, stop=not edge)
                        if edge:
                            at.wait(pe, agg_done, lambda i: S.upto(i - 1, "edge"))
                            mm = pe.matmul(bank[1][:, :], w1e, aggT[:, (n % 6) // 3, :].rearrange("p (i j) -> p j i", j=J),
                                           start=False, stop=True)
                        mm.then_inc(pe_b, 1)
                    n = at.i - 3
                    if S.kind(n) is not None:
                        at.wait(pe, z2_done, lambda i: i - 2)
                        at.wait(pe, r2_done, lambda i: i - 3)
                        for j in range(J):
                            mm = pe.transpose(bank[3][:, j * F:(j + 1) * F], z2[:, n % 2, j, :], identity[:, :])
                        mm.then_inc(pe_d, 1)
                    n = at.i - 6
                    if S.kind(n) in NODES:
                        at.wait(pe, x1_done, lambda i: i - 5)
                        at.wait(pe, x1T_done, lambda i: S.upto(i - 7, *NODES))
                        at.wait(pe, agg_done, lambda i: S.upto(i, "edge"))
                        for j in range(J):
                            mm = pe.transpose(bank[5][:, j * F:(j + 1) * F], x1[:, n % 3, j, :], identity[:, :])
                        mm.then_inc(pe_f, 1)
                    n = at.i - 7
                    if S.kind(n) in NODES:
                        at.wait(pe, x1T_done, lambda i: S.upto(i - 7, *NODES))
                        at.wait(pe, h1_done, lambda i: S.upto(i - 8, *NODES))
                        for j in range(J):
                            pe.matmul(bank[6][:, j * F:(j + 1) * F], ones3[:, :], bl_rows[:, 0], start=True, stop=False)
                            mm = pe.matmul(bank[6][:, j * F:(j + 1) * F], x1T[:, n % 2, j * F:(j + 1) * F], wr0,
                                           start=False, stop=True)
                        mm.then_inc(pe_g, 1)
                    if S.kind(at.i - 1) == "edge":
                        at.wait(pe, hot_ready, lambda i: S.upto(i - 1, "edge"))
                        at.wait(pe, stats_read, stat_rounds1)
                        for j in range(J):
                            for part in range(2):
                                mm = pe.matmul(bank[7][:, TABLE:TABLE + H], hot_lo[:, j, part, :], hot_hi[:, j, :],
                                               start=(j + part == 0), stop=(j + part == J))
                        mm.then_inc(table_part, 1)
                run_phase(pe, S, DEPTH1, body)

            @block.scalar
            def _(act):
                def body(at):
                    if at.i >= 2:
                        at.wait(act, var_done, rounds1)
                        nc.scalar.activation(std[:, at.i % 2, :], var[:, at.i % 2, :], ACT.Sqrt).then_inc(std_done, 1)
                    n = at.i - 1
                    if S.kind(n) is not None:
                        at.wait(act, pe_b, lambda i: i)
                        at.wait(act, pe_c, lambda i: i - 2)
                        nc.scalar.activation(r1[:, n % 2, :], bank[1][:, :], ACT.Relu, bias=c1).then_inc(r1_done, 1)
                    n = at.i - 3
                    if S.kind(n) is not None:
                        at.wait(act, pe_d, lambda i: i - 2)
                        at.wait(act, pe_e, lambda i: i - 4)
                        nc.scalar.activation(r2[:, n % 2, :], bank[3][:, :], ACT.Relu).then_inc(r2_done, 1)
                    n = at.i
                    if S.kind(n) is not None:
                        at.wait(act, pe_a, lambda i: i + 1)
                        at.wait(act, pe_b, lambda i: i - 1)
                        nc.scalar.copy(xT[:, n % 2, :], bank[0][:, :]).then_inc(xT_done, 1)
                    n = at.i - 6
                    if S.kind(n) in NODES:
                        at.wait(act, pe_f, lambda i: S.upto(i - 6, *NODES))
                        at.wait(act, pe_g, lambda i: S.upto(i - 8, *NODES))
                        nc.scalar.copy(x1T[:, n % 2, :], bank[5][:, :]).then_inc(x1T_done, 1)
                    n = at.i - 7
                    if S.kind(n) in NODES:
                        at.wait(act, pe_g, lambda i: S.upto(i - 7, *NODES))
                        at.wait(act, ssq_done, lambda i: J * S.upto(i - 8, *NODES))
                        at.wait(act, var_done, lambda i: rounds1(i - 1))
                        for j in range(J):
                            nc.scalar.activation(junk[:, j, :], bank[6][:, j * F:(j + 1) * F], ACT.Square,
                                                 accum_out=ssq[:, n % 2, j:j + 1]).then_inc(ssq_done, 1)
                run_phase(act, S, DEPTH1, body)

            @block.vector
            def _(dve):
                V = nc.vector

                def body(at):
                    par = at.i % 2
                    ln1, ln2 = S.kind(at.i - 2) is not None, S.kind(at.i - 4) is not None
                    if ln1 or ln2:
                        r = slice(0 if ln1 else 1, 2 if ln2 else 1)
                        if ln1:
                            at.wait(dve, pe_c, lambda i: i - 1)
                        if ln2:
                            at.wait(dve, pe_e, lambda i: i - 3)
                        if S.kind(at.i - 2) == "edge":
                            at.wait(dve, table_part, lambda i: S.upto(i - 2, "edge"))
                            at.wait(dve, table_added, lambda i: S.upto(i - 3, "edge"))
                            V.tensor_tensor(slot_sum[:, :], slot_sum[:, :], bank[7][:, TABLE:TABLE + H], ALU.add).then_inc(table_added, 1)
                        V.tensor_copy(stats[:, r], bank[7][:, 0:16].rearrange("p (l s j) -> p l s j", l=2, s=2)[:, r]).then_inc(stats_read, 1)
                        at.wait(dve, stats_read, stat_rounds1)
                        V.tensor_tensor(stats_m2[:, r], stats[:, r, 0, :], stats[:, r, 0, :], ALU.mult).then_inc(stats_sq, 1)
                        at.wait(dve, stats_sq, stat_rounds1)
                        V.tensor_tensor(stats_v[:, r], stats[:, r, 1, :], stats_m2[:, r], ALU.subtract).then_inc(stats_sub, 1)
                    if S.kind(at.i - 5) is not None:
                        at.wait(dve, bn2_done, lambda i: i - 4)
                        V.tensor_scalar(var[:, par, 8:12], bn2[:, (at.i - 5) % 2, :, 1], LN_EPS, None, ALU.add)
                    if S.kind(at.i - 8) in NODES:
                        at.wait(dve, ssq_done, lambda i: J * S.upto(i - 8, *NODES))
                        V.tensor_scalar(var[:, par, 12:16], ssq[:, (at.i - 8) % 2, :], NORM_EPS * NORM_EPS, None, ALU.max)
                    if at.i >= 2:
                        if ln1 or ln2:
                            at.wait(dve, stats_sub, stat_rounds1)
                            V.tensor_scalar(var[:, par, 0:8].rearrange("p (l j) -> p l j", l=2)[:, r], stats_v[:, r], 0.0, LN_EPS,
                                            ALU.max, ALU.add).then_inc(var_done, 1)
                        else:
                            at.idle(dve).then_inc(var_done, 1)
                    if S.kind(at.i) == "edge":
                        e = (at.i % 6) // 3
                        at.wait(dve, dst_row_in[e], lambda i: 16 * ((S.upto(i, "edge") + 1) // 2))
                        first = at.value(lambda i: (S.upto(i, "edge") - 1) * G)
                        V.tensor_tensor(same[:, bass.ds(first, G)], dst_row[:, e, 1:G + 1], dst_row[:, e, 0:G],
                                        ALU.is_equal).then_inc(same_done, 1)
                        at.wait(dve, same_done, lambda i: S.upto(i, "edge"))
                        at.wait(dve, pe_ea, lambda i: S.upto(i, "edge"))
                        at.wait(dve, pe_b, lambda i: i - 5)
                        at.wait(dve, agg_done, lambda i: S.upto(i, "edge") - 1)
                        first = at.value(lambda i: (S.upto(i, "edge") - 1) * G)
                        V.tensor_tensor_scan(aggT[:, e, :], same[:, bass.ds(first, G)], bank[5][:, :],
                                             0.0 if at.i < 3 else aggT[:, 1 - e, G - 1:G], ALU.mult, ALU.add).then_inc(agg_done, 1)
                    if at.i >= 2:
                        at.wait(dve, std_done, rounds1)
                        V.reciprocal(inv[:, par, :], std[:, par, :]).then_inc(inv_done, 1)
                        at.wait(dve, inv_done, rounds1)
                    n = at.i - 2
                    if S.kind(n) is not None:
                        at.wait(dve, pe_d, lambda i: i - 3)
                        for j in range(J):
                            ins = V.scalar_tensor_tensor(out=z2[:, n % 2, j, :], in0=bank[2][:, j * F:(j + 1) * F],
                                                         scalar=inv[:, par, j:j + 1], in1=bias2[:, :], op0=ALU.mult, op1=ALU.add)
                        ins.then_inc(z2_done, 1)
                    n = at.i - 4
                    if S.kind(n) is not None:
                        at.wait(dve, xb_done, lambda i: i - 3)
                        at.wait(dve, x1_done, lambda i: i - 5)
                        for j in range(J):
                            ins = V.scalar_tensor_tensor(out=v3[:, n % 2, j, :], in0=bank[4][:, j * F:(j + 1) * F],
                                                         scalar=inv[:, par, 4 + j:5 + j], in1=xg[:, n % 6, j, :], op0=ALU.mult, op1=ALU.add)
                        ins.then_inc(v3_done, 1)
                    n = at.i - 8
                    if S.kind(n) in NODES:
                        at.wait(dve, h1_out[n % 2], lambda i: stored1(i - 10, 2, NODES))
                        for j in range(J):
                            ins = V.tensor_scalar(h1[:, n % 2, j, :], bank[6][:, j * F:(j + 1) * F], 0.0, inv[:, par, 12 + j:13 + j],
                                                  ALU.max, ALU.mult)
                        ins.then_inc(h1_done, 1)
                    n = at.i - 5
                    if S.kind(n) is not None:
                        at.wait(dve, pe_f, lambda i: S.upto(i - 8, *NODES))
                        at.wait(dve, x1_out[n % 3], lambda i: stored1(i - 8, 3))
                        for j in range(J):
                            ins = V.tensor_scalar(x1[:, n % 3, j, :], v3[:, n % 2, j, :], bn2[:, n % 2, j, 0:1],
                                                  inv[:, par, 8 + j:9 + j], ALU.subtract, ALU.mult)
                        ins.then_inc(x1_done, 1)
                    n = at.i - 4
                    if S.kind(n) is not None:
                        at.wait(dve, v3_done, lambda i: i - 3)
                        for j in range(J):
                            ins = V.bn_stats(bn6[:, n % 2, j, :], v3[:, n % 2, j, :])
                        ins.then_inc(bn6_done, 1)
                        at.wait(dve, bn6_done, lambda i: i - 3, apart=True)
                        for j in range(J):
                            ins = V.bn_aggr(bn2[:, n % 2, j, :], bn6[:, n % 2, j, :])
                        ins.then_inc(bn2_done, 1)
                    if S.kind(at.i) == "edge":
                        g = at.value(lambda i: S.upto(i, "edge") - 1)
                        first = at.value(lambda i: (S.upto(i, "edge") - 1) * G)
                        at.wait(dve, inv_count_done, lambda i: S.upto(i, "edge") - 2)
                        V.tensor_tensor_scan(count[:, e, :], same[:, bass.ds(first, G)], ones[:, :],
                                             0.0 if at.i < 3 else count[:, 1 - e, G - 1:G], ALU.mult, ALU.add).then_inc(count_done, 1)
                        at.wait(dve, src_row_in[e], lambda i: 16 * ((S.upto(i, "edge") + 1) // 2))
                        at.wait(dve, hot_src_done, lambda i: S.upto(i, "edge") - 1)
                        V.tensor_scalar(src_low[:, :], src_row[:, e, :], P - 1, None, ALU.bitwise_and).then_inc(low_done, 1)
                        at.wait(dve, count_done, lambda i: S.upto(i, "edge"))
                        V.reciprocal(inv_count[:, bass.ds(first, G)], count[:, e, :]).then_inc(inv_count_done, 1)
                        at.wait(dve, low_done, lambda i: S.upto(i, "edge"))
                        V.tensor_scalar(hot_src[:, bass.ds(first, G)], src_low[:, :], iota_p[:, 0:1], None, ALU.is_equal).then_inc(hot_src_done, 1)
                        at.wait(dve, table_part, lambda i: S.upto(i, "edge") - 1)
                        for j in range(J):
                            V.tensor_scalar(hot_hi[:, j, :], iota_hi[:, :], dst_hi[:, g, j:j + 1], None, ALU.is_equal)
                            V.tensor_scalar(hot_lo[:, j, 0, :], iota_lo[:, :], dst_lo[:, g, j:j + 1], e_high[:, g, j:j + 1],
                                            ALU.is_equal, ALU.mult)
                            ins = V.tensor_scalar(hot_lo[:, j, 1, :], iota_lo[:, :], dst_lo[:, g, j:j + 1], e_low[:, g, j:j + 1],
                                                  ALU.is_equal, ALU.mult)
                        ins.then_inc(hot_ready, 1)
                run_phase(dve, S, DEPTH1, body)

            @block.gpsimd
            def _(pool):
                Q = nc.gpsimd

                def body(at):
                    n = at.i - 1
                    if S.kind(n) is not None:
                        at.wait(pool, r1_done, lambda i: i)
                        at.wait(pool, pe_c, lambda i: i - 2)
                        Q.tensor_tensor(sq1[:, n % 2, :], r1[:, n % 2, :], r1[:, n % 2, :], ALU.mult).then_inc(sq1_done, 1)
                    n = at.i - 3
                    if S.kind(n) is not None:
                        at.wait(pool, r2_done, lambda i: i - 2)
                        at.wait(pool, pe_e, lambda i: i - 4)
                        Q.tensor_tensor(sq2[:, n % 2, :], r2[:, n % 2, :], r2[:, n % 2, :], ALU.mult).then_inc(sq2_done, 1)
                    n = at.i - 1
                    if S.kind(n) is not None:
                        at.wait(pool, pe_a, lambda i: i)
                        Q.tensor_tensor(xg[:, n % 6], xg[:, n % 6], bias3[:, :, :], ALU.add).then_inc(xb_done, 1)
                    n = at.i + 1
                    if S.kind(n) == "edge":
                        at.wait(pool, v3_done, lambda i: i - 4)
                        k = at.value(lambda i: S.upto(i + 1, "edge") - 1)
                        e = (n % 6) // 3
                        Q.tensor_copy(idx_now[:, e, :], x_idx[:, k, :]).then_inc(x_idx_now, 1)
                        at.wait(pool, x_idx_now, lambda i: S.upto(i + 1, "edge"))
                        for j in range(J):
                            Q.indirect_dma_start(out=xg[:, n % 6, j, :], out_offset=None, in_=A["x"],
                                                 in_offset=bass.IndirectOffsetOnAxis(ap=idx_now[:, e, j:j + 1], axis=0),
                                                 bounds_check=N - 1, oob_is_err=False).then_inc(xd_in[e], 16)
                run_phase(pool, S, DEPTH1, body)

        link_s = sem("link_s")
        RING = 4
        with nc.Block() as block:
            @block.tensor
            def _(pe):
                pe.wait_ge(table_copied, 1)
                for t in range(SLOTS // P):
                    g, j = divmod(t, J)
                    if t >= RING:
                        pe.wait_ge(selected, t - RING + 1)
                    q = hot_src[:, g * G:(g + 1) * G].rearrange("p (i j) -> p j i", j=J)[:, j, :]
                    for part in range(2):
                        mm = pe.matmul(bank[t % RING][:, 0:H], q, slot_table[:, part, :], start=(part == 0), stop=(part == 1))
                    mm.then_inc(looked_up, 1)

            @block.vector
            def _(dve):
                V = nc.vector
                links = [0]

                def link(ins):
                    links[0] += 1
                    ins.then_inc(link_s, 1)
                    dve.wait_ge(link_s, links[0])

                link(V.tensor_copy(slot_int[:, 0, :], slot_sum[:, :]))
                link(V.tensor_scalar(slot_int[:, 1, :], slot_int[:, 0, :], P - 1, None, ALU.bitwise_and))
                link(V.tensor_scalar(slot_int[:, 0, :], slot_int[:, 0, :], -P, None, ALU.bitwise_and))
                V.tensor_copy(slot_table[:, :, :], slot_int[:, :, :]).then_inc(table_copied, 1)
                for t in range(SLOTS // P):
                    g, j = divmod(t, J)
                    dve.wait_ge(looked_up, t + 1)
                    if t >= 2:
                        dve.wait_ge(selected, t - 1)
                    V.scalar_tensor_tensor(out=entries[:, t % 2, :], in0=iota_hi[:, :], scalar=src_hi[:, g, j:j + 1],
                                           in1=bank[t % RING][:, 0:H], op0=ALU.is_equal, op1=ALU.mult,
                                           accum_out=found[:, g, j:j + 1]).then_inc(selected, 1)
                dve.wait_ge(selected, SLOTS // P)
                link(V.tensor_scalar(fsel[:, 0], found[:, :, :], 0.0, None, ALU.is_gt))
                link(V.tensor_tensor(fsel[:, 1], found[:, :, :], src_f, ALU.subtract))
                link(V.tensor_scalar(fsel[:, 1], fsel[:, 1], float(N - 1), None, ALU.add))
                link(V.tensor_tensor(fsel[:, 1], fsel[:, 1], fsel[:, 0], ALU.mult))
                link(V.tensor_tensor(fsel[:, 1], fsel[:, 1], src_f, ALU.add))
                link(V.tensor_copy(row_idx[:, :, :], fsel[:, 1]))

        scattered = sem("scattered")

        def sage_phase(S, name, first_node, wr_e, wl_e, bias_e, res_e):
            LS = len(S.kinds)
            table = x1_table if not res_e else h1_table
            rin = [sem(f"{name}_rows_in{s}") for s in range(3)]
            xin = [sem(f"{name}_x1_in{s}") for s in range(6)]
            msg_in = [sem(f"{name}_messages_in{s}") for s in range(2)]
            turned, msg_turned, z_ready = sem(f"{name}_turned"), sem(f"{name}_messages_turned"), sem(f"{name}_z")
            rT_done, ss_done, sd_done = sem(f"{name}_rT"), sem(f"{name}_ssq"), sem(f"{name}_std")
            vr_done, iv_done, ag_done, mean_done = sem(f"{name}_var"), sem(f"{name}_inv"), sem(f"{name}_agg"), sem(f"{name}_mean")
            u_done, b6, b2, sum_done, fin_done = sem(f"{name}_u"), sem(f"{name}_bn6"), sem(f"{name}_bn2"), sem(f"{name}_sum"), sem(f"{name}_fin")
            idx_copied = sem(f"{name}_idx_copied")
            stored = [sem(f"{name}_stored{s}") for s in range(3)]
            ALL = ("node", "tail", "edge")
            FULL = ALL if res_e else NODES

            def up(n, *k):
                return S.upto(n, *k)

            def in_slot(n, ring, kinds, w=lambda k: 16):
                return sum(w(S.kind(m)) for m in range(n % ring, n + 1, ring) if S.kind(m) in kinds) if n >= 0 else 0

            STORED = NODES if res_e else ALL
            STORE = 6

            with nc.Block() as block:
                @block.sync
                def _(sp):
                    def body(at):
                        n = at.i
                        k = S.kind(n)
                        if k in ALL:
                            at.wait(sp, turned, lambda i: up(i - 3))
                            dst = rows[:, n % 3].rearrange("p j f -> p (j f)")
                            dst2 = xg[:, n % 6].rearrange("p j f -> p (j f)")
                            if k in FULL:
                                at.wait(sp, fin_done, lambda i: up(i - 6, *FULL))
                            if k == "edge":
                                g = at.value(lambda i: up(i, "edge") - 1)
                                sp.dma_start(dst, edge_rows(table, g)).then_inc(rin[n % 3], 16)
                                if res_e:
                                    sp.dma_start(dst2, edge_rows(x1_table, g)).then_inc(xin[n % 6], 16)
                            elif k == "tail":
                                sp.dma_start(dst[0:TAIL], tail_rows(h1_table)).then_inc(rin[n % 3], 16)
                                sp.dma_start(dst2[0:TAIL], tail_rows(x1_table)).then_inc(xin[n % 6], 16)
                            else:
                                g = at.value(lambda i: first_node + up(i, "node") - 1)
                                sp.dma_start(dst, node_rows(h1_table, g)).then_inc(rin[n % 3], 16)
                                sp.dma_start(dst2, node_rows(x1_table, g)).then_inc(xin[n % 6], 16)
                        n = at.i - STORE
                        k = S.kind(n)
                        if k in NODES:
                            at.wait(sp, fin_done, lambda i: up(i - STORE, *FULL))
                            at.wait(sp, stored[n % 3], lambda i: in_slot(i - STORE - 3, 3, STORED))
                            of = x1[:, n % 3].rearrange("p j f -> p (j f)")
                            if k == "tail":
                                sp.dma_start(tail_rows(out), of[0:TAIL]).then_inc(stored[n % 3], 16)
                            else:
                                g = at.value(lambda i: first_node + up(i - STORE, "node") - 1)
                                sp.dma_start(node_rows(out, g), of).then_inc(stored[n % 3], 16)
                        elif k == "edge" and not res_e:
                            at.wait(sp, u_done, lambda i: up(i - STORE))
                            at.wait(sp, stored[n % 3], lambda i: in_slot(i - STORE - 3, 3, STORED))
                            g = at.value(lambda i: up(i - STORE, "edge") - 1)
                            sp.dma_start(edge_rows(h1_table, g), z2[:, (n % 6) // 3].rearrange("p j f -> p (j f)")).then_inc(stored[n % 3], 16)
                    run_phase(sp, S, DEPTH2 + 1, body)
                    for s in range(3):
                        last = max(n for n in range(LS) if n % 3 == s)
                        sp.wait_ge(stored[s], in_slot(last, 3, STORED))

                @block.tensor
                def _(pe):
                    def body(at):
                        n = at.i - 1
                        k = S.kind(n)
                        if k in ALL:
                            edge = k == "edge"
                            zb = bank[4 + n % 2]
                            at.wait(pe, rT_done, lambda i: up(i - 1))
                            at.wait(pe, u_done, lambda i: up(i - 3))
                            if edge:
                                at.wait(pe, mean_done, lambda i: up(i - 1, "edge"))
                            b = bias_e if edge else 1
                            for j in range(J):
                                pe.matmul(zb[:, j * F:(j + 1) * F], ones3[:, :], bl_rows[:, b], start=True, stop=False)
                                mm = pe.matmul(zb[:, j * F:(j + 1) * F], x1T[:, n % 2, j * F:(j + 1) * F], wr_e if edge else wr1,
                                               start=False, stop=not edge)
                                if edge:
                                    mm = pe.matmul(zb[:, j * F:(j + 1) * F], r2[:, (n % 6) // 3, j * F:(j + 1) * F], wl_e,
                                                   start=False, stop=True)
                            mm.then_inc(z_ready, 1)
                        n = at.i
                        k = S.kind(n)
                        if k in ALL:
                            at.wait(pe, rin[n % 3], lambda i: in_slot(i, 3, ALL))
                            at.wait(pe, rT_done, lambda i: up(i - 2))
                            for j in range(J):
                                mm = pe.transpose(bank[n % 2][:, j * F:(j + 1) * F], rows[:, n % 3, j, :], identity[:, :])
                            mm.then_inc(turned, 1)
                        if k == "edge":
                            e = (n % 6) // 3
                            at.wait(pe, msg_in[e], lambda i: 16 * J * ((up(i, "edge") + 1) // 2))
                            at.wait(pe, ag_done, lambda i: up(i, "edge") - 1)
                            for j in range(J):
                                mm = pe.transpose(bank[2][:, :].rearrange("p (i j) -> p j i", j=J)[:, j, :], ea[:, e, j, :], identity[:, :])
                            mm.then_inc(msg_turned, 1)
                    run_phase(pe, S, DEPTH2, body)

                @block.scalar
                def _(act):
                    def body(at):
                        if at.i >= 2:
                            at.wait(act, vr_done, rounds1)
                            nc.scalar.activation(std[:, at.i % 2, 0:8], var[:, at.i % 2, 0:8], ACT.Sqrt).then_inc(sd_done, 1)
                        n = at.i - 1
                        if S.kind(n) in ALL:
                            at.wait(act, z_ready, lambda i: up(i - 1))
                            at.wait(act, ss_done, lambda i: J * up(i - 2))
                            at.wait(act, vr_done, lambda i: rounds1(i - 1))
                            for j in range(J):
                                nc.scalar.activation(junk[:, j, :], bank[4 + n % 2][:, j * F:(j + 1) * F], ACT.Square,
                                                     accum_out=ssq[:, n % 2, j:j + 1]).then_inc(ss_done, 1)
                        n = at.i
                        if S.kind(n) in ALL:
                            at.wait(act, turned, lambda i: up(i))
                            at.wait(act, z_ready, lambda i: up(i - 2))
                            nc.scalar.copy(x1T[:, n % 2, :], bank[n % 2][:, :]).then_inc(rT_done, 1)
                        n = at.i - 4
                        if S.kind(n) in FULL:
                            at.wait(act, iv_done, rounds1)
                            at.wait(act, stored[n % 3], lambda i: in_slot(i - 7, 3, STORED))
                            to = x1[:, n % 3]
                            if S.kind(n) == "edge":
                                to = results[:, at.value(lambda i: up(i - 4, "edge") - 1)]
                            for j in range(J):
                                ins = nc.scalar.activation(to[:, j, :], xg[:, n % 6, j, :], ACT.Identity,
                                                           bias=nmean[:, at.i % 2, j:j + 1], scale=inv[:, at.i % 2, 4 + j:5 + j])
                            ins.then_inc(fin_done, 1)
                    run_phase(act, S, DEPTH2, body)

                @block.vector
                def _(dve):
                    V = nc.vector

                    def body(at):
                        par = at.i % 2
                        if at.i >= 2:
                            if S.kind(at.i - 4) in FULL:
                                at.wait(dve, b2, lambda i: up(i - 4, *FULL))
                                V.tensor_scalar(var[:, par, 4:8], bn2[:, (at.i - 4) % 2, :, 1], LN_EPS, None, ALU.add)
                            if S.kind(at.i - 2) in ALL:
                                at.wait(dve, ss_done, lambda i: J * up(i - 2))
                                V.tensor_scalar(var[:, par, 0:4], ssq[:, (at.i - 2) % 2, :], NORM_EPS * NORM_EPS, None,
                                                ALU.max).then_inc(vr_done, 1)
                            else:
                                at.idle(dve).then_inc(vr_done, 1)
                        n = at.i - 3
                        if S.kind(n) in FULL:
                            at.wait(dve, sum_done, lambda i: up(i - 3, *FULL))
                            for j in range(J):
                                ins = V.bn_stats(bn6[:, n % 2, j, :], xg[:, n % 6, j, :])
                            ins.then_inc(b6, 1)
                            at.wait(dve, b6, lambda i: up(i - 3, *FULL), apart=True)
                            for j in range(J):
                                ins = V.bn_aggr(bn2[:, n % 2, j, :], bn6[:, n % 2, j, :])
                            ins.then_inc(b2, 1)
                        if at.i >= 2:
                            at.wait(dve, sd_done, rounds1)
                            V.reciprocal(inv[:, par, 0:8], std[:, par, 0:8]).then_inc(iv_half, 1)
                            dve.wait_ge(iv_half, at.value(lambda i: i - 1 + iv_base[name]))
                            if S.kind(at.i - 4) in FULL:
                                V.scalar_tensor_tensor(out=nmean[:, par, :], in0=bn2[:, (at.i - 4) % 2, :, 0], scalar=-1.0,
                                                       in1=inv[:, par, 4:8], op0=ALU.mult, op1=ALU.mult).then_inc(iv_done, 1)
                            else:
                                at.idle(dve).then_inc(iv_done, 1)
                        n = at.i - 2
                        if S.kind(n) in ALL:
                            full = S.kind(n) in FULL
                            u = v3[:, n % 2] if full else z2[:, (n % 6) // 3]
                            if full:
                                at.wait(dve, sum_done, lambda i: up(i - 4, *FULL))
                            else:
                                at.wait(dve, stored[n % 3], lambda i: in_slot(i - 8, 3, STORED))
                            for j in range(J):
                                ins = V.tensor_scalar(u[:, j, :], bank[4 + n % 2][:, j * F:(j + 1) * F], 0.0,
                                                      inv[:, par, j:j + 1], ALU.max, ALU.mult)
                            ins.then_inc(u_done, 1)
                        if S.kind(at.i) == "edge":
                            e = (at.i % 6) // 3
                            at.wait(dve, msg_turned, lambda i: up(i, "edge"))
                            at.wait(dve, mean_done, lambda i: up(i, "edge") - 1)
                            first = at.value(lambda i: (up(i, "edge") - 1) * G)
                            V.tensor_tensor_scan(aggT[:, e, :], same[:, bass.ds(first, G)], bank[2][:, :],
                                                 0.0 if at.i < 3 else aggT[:, 1 - e, G - 1:G], ALU.mult, ALU.add).then_inc(ag_done, 1)
                            at.wait(dve, z_ready, lambda i: up(i - 6))
                            at.wait(dve, ag_done, lambda i: up(i, "edge"))
                            V.tensor_tensor(r2[:, e, :].rearrange("p (j i) -> p j i", j=J),
                                            aggT[:, e, :].rearrange("p (i j) -> p j i", j=J),
                                            inv_count[:, bass.ds(first, G)].rearrange("p (i j) -> p j i", j=J), ALU.mult).then_inc(mean_done, 1)
                    run_phase(dve, S, DEPTH2, body)

                @block.gpsimd
                def _(pool):
                    Q = nc.gpsimd

                    def indices(at, ahead):
                        e = ((at.i + ahead) % 6) // 3
                        g = at.value(lambda i: up(i + ahead, "edge") - 1)
                        at.wait(pool, msg_turned, lambda i: up(i + ahead, "edge") - 2)
                        Q.tensor_copy(idx_now[:, e, :], row_idx[:, g, :]).then_inc(idx_copied, 1)
                        at.wait(pool, idx_copied, lambda i: up(i + ahead, "edge"))

                    def gather(n, part):
                        e = (n % 6) // 3
                        for j in (2 * part, 2 * part + 1):
                            Q.indirect_dma_start(out=ea[:, e, j, :], out_offset=None, in_=table,
                                                 in_offset=bass.IndirectOffsetOnAxis(ap=idx_now[:, e, j:j + 1], axis=0),
                                                 bounds_check=ROWS - 1, oob_is_err=False).then_inc(msg_in[e], 16)

                    def body(at):
                        n = at.i - 2
                        if S.kind(n) in FULL:
                            at.wait(pool, u_done, lambda i: up(i - 2))
                            at.wait(pool, xin[n % 6], lambda i: in_slot(i - 2, 6, FULL))
                            Q.tensor_tensor(xg[:, n % 6], v3[:, n % 2], xg[:, n % 6], ALU.add).then_inc(sum_done, 1)
                        if at.i % 3 == 0 and S.kind(at.i + 5) == "edge":
                            indices(at, 5)
                            gather(at.i + 5, 0)
                        if at.i % 3 == 1 and S.kind(at.i + 4) == "edge":
                            gather(at.i + 4, 1)
                    indices(Place(0), 2)
                    gather(2, 0)
                    gather(2, 1)
                    run_phase(pool, S, DEPTH2, body)
                    if res_e:
                        pool.wait_ge(fin_done, up(LS, *FULL))
                        for s in range(3):
                            last = max(n for n in range(LS) if n % 3 == s)
                            pool.wait_ge(stored[s], in_slot(last, 3, STORED))
                        for g in range(EG):
                            for j in range(J):
                                Q.indirect_dma_start(out=out, out_offset=bass.IndirectOffsetOnAxis(ap=out_idx[:, g, j:j + 1], axis=0),
                                                     in_=results[:, g, j, :], in_offset=None,
                                                     bounds_check=N - 1, oob_is_err=False).then_inc(scattered, 16)
                        pool.wait_ge(scattered, 16 * J * EG)

        iv_half = sem("inv_half")
        iv_base = {"p2": 0, "p3": len(phase2.kinds) + DEPTH2 - 2}
        sage_phase(phase2, "p2", 0, wr0, wl0, 0, False)
        sage_phase(phase3, "p3", half, wr1, wl1, 1, True)


_INS = ['x', 'src', 'dst', 'edge_attr_128', 'L0_gnn_u', 'L0_gnn_W1', 'L0_gnn_b1', 'L0_gnn_g1', 'L0_gnn_be1', 'L0_gnn_W2',
        'L0_gnn_b2', 'L0_gnn_g2', 'L0_gnn_be2', 'L0_gnn_W3', 'L0_gnn_b3', 'L1_gnn_W_l0', 'L1_gnn_b_l0', 'L1_gnn_W_r0',
        'L1_gnn_W_l1', 'L1_gnn_b_l1', 'L1_gnn_W_r1']


def kernel(**inputs):
    import numpy as _np
    import concourse.bacc as _bacc
    from concourse import mybir as _mybir
    from concourse.bass_utils import run_bass_kernel_spmd as _run

    nc = _bacc.Bacc("TRN2", target_bir_lowering=False, num_devices=1)
    arrays, args = {}, {}
    for name in _INS:
        a = _np.ascontiguousarray(inputs[name])
        arrays[f"in_{name}_dram"] = a
        args[name] = nc.dram_tensor(f"in_{name}_dram", a.shape, _mybir.dt.from_np(a.dtype), kind="ExternalInput").ap()
    out = nc.dram_tensor("out_0_dram", arrays["in_x_dram"].shape, _mybir.dt.float32, kind="ExternalOutput").ap()
    build(nc, args, out)
    r = _run(nc, [arrays], core_ids=[0])
    return r.results[0]["out_0_dram"]
```

```python
from contextlib import ExitStack

import concourse.bass as bass
from concourse import mybir

F32 = mybir.dt.float32
BF16 = mybir.dt.bfloat16
I32 = mybir.dt.int32
ALU = mybir.AluOpType
ACT = mybir.ActivationFunctionType

P = 128
J = 4
G = P * J
F = 128
U = 6
LN_EPS = 1e-5
NORM_EPS = 1e-12


class Schedule:

    def __init__(self, kinds):
        self.kinds = kinds

    def kind(self, n):
        return self.kinds[n] if 0 <= n < len(self.kinds) else None

    def upto(self, n, *which):
        which = which or ("node", "tail", "edge")
        return sum(k in which for k in self.kinds[:max(n + 1, 0)])


class Place:

    APART = (mybir.EngineType.Pool, mybir.EngineType.SP)
    passed = None

    def __init__(self, i, turns=1, reg=None):
        self.i, self.turns, self.reg = i, turns, reg

    def value(self, f):
        a = f(self.i)
        if self.reg is None:
            return a
        step = f(self.i + U) - a
        assert all(f(self.i + U * t) == a + step * t for t in range(self.turns))
        return a + self.reg * step if step else a

    def wait(self, eng, sem, f, apart=False):
        if f(self.i) > 0:
            eng.wait_ge(sem, self.value(f))
            if self.reg is not None and (apart or eng.engine in self.APART):
                eng.sem_inc(self.passed, 1)
        else:
            assert f(self.i + U * (self.turns - 1)) <= 0

    def idle(self, eng):
        if self.reg is not None:
            eng.sem_inc(self.passed, 1)
        return eng.drain()


def run_phase(eng, sched, depth, body):
    length = len(sched.kinds) + depth
    blocks = -(-length // U)

    def pattern(b):
        return [sched.kind(n) for n in range(b * U - depth, b * U + U)]

    b = 0
    while b < blocks:
        e = b + 1
        if b * U - depth >= U:
            while e < blocks and pattern(e) == pattern(b) and (e + 1) * U <= len(sched.kinds):
                e += 1
        if e - b >= 2:
            with eng.Fori(0, e - b) as turn:
                for u in range(U):
                    body(Place(b * U + u, e - b, turn))
        else:
            e = b + 1
            for i in range(b * U, min(e * U, length)):
                body(Place(i))
        b = e


def build(nc, A, out):
    N = A["x"].shape[0]
    E = A["src"].shape[0]
    NG = N // G
    TAIL = (N - NG * G) // J
    assert (N - NG * G) % J == 0 and E % J == 0
    EG = -(-E // G)
    SLOTS = EG * G
    ETAIL = (E - (EG - 1) * G) // J
    H = -(-N // P)
    ROWS = N + SLOTS
    D_U = A["L0_gnn_u"].shape[1]

    half = 2 * EG
    rest = NG + 1 - half
    phase1 = Schedule((["node", "node", "edge"] * EG + ["node"] * rest)[:-1] + ["tail"])
    phase2 = Schedule(["node", "node", "edge"] * EG)
    third = ["node"] * (rest - 1) + ["tail"] + ["none"] * (2 * EG - rest)
    phase3 = Schedule([k for d in range(EG) for k in (third[2 * d], third[2 * d + 1], "edge")])
    DEPTH1, DEPTH2 = 9, 6

    with ExitStack() as ctx:
        def sb(name, shape, dt=F32):
            return ctx.enter_context(nc.sbuf_tensor(name, shape, dt))

        def ps(name, shape):
            return ctx.enter_context(nc.psum_tensor(name, shape, F32))

        def sem(name):
            return ctx.enter_context(nc.semaphore(name))

        x1_table = nc.dram_tensor("x1_table", [ROWS, F], F32, kind="Internal").ap()
        h1_table = nc.dram_tensor("h1_table", [ROWS, F], F32, kind="Internal").ap()

        count_line = nc.dram_tensor("count_line", [EG, G], F32, kind="Internal").ap()
        inv_line = nc.dram_tensor("inv_line", [EG, G], F32, kind="Internal").ap()

        def node_rows(table, k):
            return table[0:NG * G].rearrange("(g p j) f -> g p (j f)", p=P, j=J)[k]

        def tail_rows(table):
            return table[NG * G:N].rearrange("(p j) f -> p (j f)", j=J)

        def edge_rows(table, k):
            return table[N:ROWS].rearrange("(g p j) f -> g p (j f)", p=P, j=J)[k]

        wbuf = sb("wbuf", [P, 8, F])
        w1x, w1e, w2c, w3c, wr0, wl0, wr1, wl1 = [wbuf[:, i, :] for i in range(8)]
        xg = sb("xg", [P, 6, J, F])
        spare = xg[:, :, :, :].rearrange("p s j f -> p (s j f)")
        raw = spare[:, 0:6 * F].rearrange("p (w f) -> p w f", w=6)
        be_wide, brow, scaled = [spare[:, (6 + 2 * i) * F:(8 + 2 * i) * F].rearrange("p (w f) -> p w f", w=2)
                                 for i in range(3)]
        bias_wide, bias_tmp = [spare[:, (12 + 3 * i) * F:(15 + 3 * i) * F].rearrange("p (w f) -> p w f", w=3) for i in range(2)]
        centre = spare[:, 18 * F:19 * F]
        bias_part = spare[:, 19 * F:19 * F + 9 * F // 2].bitcast(BF16).rearrange("p (a w f) -> p a w f", a=3, w=3)
        w1u = sb("w1u", [D_U, F])
        u_col = sb("u_col", [D_U, 1])
        u_wide = sb("u_wide", [D_U, P])
        cols = sb("cols", [P, 4])
        bias2 = sb("bias2", [P, F])
        bias3 = sb("bias3", [P, J, F])
        identity = sb("identity", [P, P])
        bias_rows = sb("bias_rows", [96, 3, F], BF16)
        ones3 = sb("ones3", [96, P], BF16)

        src_c = sb("src_c", [P, EG, J], I32)
        dst_c = sb("dst_c", [P, EG, J], I32)
        next_c = sb("next_c", [P, EG, J], I32)
        x_idx = sb("x_idx", [P, EG, J], I32)
        row_idx = sb("row_idx", [P, EG, J], I32)
        out_idx = sb("out_idx", [P, EG, J], I32)
        same = sb("same", [P, SLOTS], BF16)
        count = sb("count", [P, 2, G])
        inv_count = sb("inv_count", [P, 2, G])
        count_c = sb("count_c", [P, EG, J])
        int_c = sb("int_c", [P, EG, J], I32)
        fc = sb("fc", [P, 8, EG, J])
        dst_f, is_last, e_high, e_low, src_f, src_hi, dst_hi, dst_lo = [fc[:, i] for i in range(8)]
        hot_low = sb("hot_low", [P, J, P], BF16)
        idx_now = sb("idx_now", [P, 2, J], I32)
        found = sb("found", [P, EG, J])
        fsel = sb("fsel", [P, 2, EG, J])
        iota_hi = sb("iota_hi", [P, H])
        iota_lo = sb("iota_lo", [P, P], BF16)
        iota_p = sb("iota_p", [P, 1])
        ones = sb("ones", [P, G], BF16)
        dst_row = sb("dst_row", [P, 2, G + 1], I32)
        src_row = sb("src_row", [P, 2, G], I32)
        src_low = sb("src_low", [P, G], I32)
        slot_table = sb("slot_table", [P, 2, H], BF16)
        results = sb("results", [P, EG, J, F])
        wide = results[:, :, :, :].rearrange("p g j f -> p (g j f)")
        hot_src = wide[:, 10 * G:10 * G + SLOTS // 2].bitcast(BF16)

        ea = sb("ea", [P, 2, J, F])
        aggT = sb("aggT", [P, 2, G])
        r2 = sb("r2", [P, 2, G])
        v3 = sb("v3", [P, 2, J, F])
        x1 = sb("x1", [P, 3, J, F])
        xb = sb("xb", [P, 3, J, F])
        x1T = sb("x1T", [P, 2, G])
        rows = sb("rows", [P, 3, J, F])
        hot_words = rows[:, :, :, :].rearrange("p s j f -> p (s j f)").bitcast(BF16)
        hot_hi = hot_words[:, 0:J * H].rearrange("p (j h) -> p j h", j=J)
        hot_lo = hot_words[:, 2048:2048 + 2 * J * P].rearrange("p (j a l) -> p j a l", j=J, a=2)
        entries = rows[:, :, :, :].rearrange("p s j f -> p (s j f)")[:, 0:2 * H].rearrange("p (a h) -> p a h", a=2)
        slot_int = entries.bitcast(I32)
        early = wide[:, 0:10 * G].rearrange("p (b r n) -> p b r n", b=5, r=2)
        xT, r1T = [early[:, b] for b in range(2)]
        r1, z2, h1 = [early[:, b].rearrange("p r (j f) -> p r j f", j=J) for b in (2, 3, 4)]
        junk = sb("junk", [P, 4, F])
        ssq = sb("ssq", [P, 2, J])
        ln_raw = sb("ln_raw", [P, 2, 3, J, 6])
        ln_sum, ln_diff, ln_diff2, ln_within = [sb(c, [P, 2, 3, J]) for c in ("ln_sum", "ln_diff", "ln_diff2", "ln_within")]
        ln_mean = sb("ln_mean", [P, 2, J])
        eps = sb("eps", [P, 1])
        bn6 = sb("bn6", [P, 2, J, 6])
        bn2 = sb("bn2", [P, 2, J, 2])
        nmean = sb("nmean", [P, 2, J])
        var = sb("var", [P, 2, 16])
        std = sb("std", [P, 2, 16])
        inv = sb("inv", [P, 2, 16])

        def on_all(row):
            return row.rearrange("p (a f) -> p a f", a=1).to_broadcast([96, J, F])

        bank = [ps(f"bank{i}", [P, G]) for i in range(8)]

        Place.passed = sem("passed")

        weights_in = sem("weights_in")
        consts = sem("consts")
        prep_v = sem("prep_v")
        prep_p = sem("prep_p")
        dst_in = sem("dst_in")
        table_copied = sem("table_copied")
        looked_up = sem("looked_up")
        selected = sem("selected")
        chain = sem("chain")

        with nc.Block() as block:
            @block.sync
            def _(sp):
                sp.dma_start(raw[:, 0, :], A["L0_gnn_W2"]).then_inc(weights_in, 16)
                sp.dma_start(raw[:, 1, :], A["L0_gnn_W3"]).then_inc(weights_in, 16)
                for i, name in enumerate(["L1_gnn_W_r0", "L1_gnn_W_l0", "L1_gnn_W_r1", "L1_gnn_W_l1"]):
                    sp.dma_start(raw[:, 2 + i, :], A[name]).then_inc(weights_in, 16)
                sp.dma_start(w1x, A["L0_gnn_W1"][0:F, :]).then_inc(weights_in, 16)
                sp.dma_start(w1e, A["L0_gnn_W1"][F:2 * F, :]).then_inc(weights_in, 16)
                sp.dma_start(w1u[:, :], A["L0_gnn_W1"][2 * F:2 * F + D_U, :]).then_inc(weights_in, 16)
                sp.dma_start(u_col[:, :], A["L0_gnn_u"].rearrange("a d -> d a")).then_inc(weights_in, 16)
                for i, name in enumerate(["g1", "be1", "g2", "be2"]):
                    sp.dma_start(cols[:, i:i + 1], A["L0_gnn_" + name].rearrange("(d a) -> d a", a=1)).then_inc(weights_in, 16)
                for i, name in enumerate(["b2", "b3"]):
                    row = A["L0_gnn_" + name].rearrange("(a d) -> a d", a=1)
                    sp.dma_start(brow[:, i, :], row.to_broadcast([P, F])).then_inc(weights_in, 16)
                for i, name in enumerate(["L1_gnn_b_l0", "L1_gnn_b_l1", "L0_gnn_b1"]):
                    row = A[name].rearrange("(a d) -> a d", a=1)
                    sp.dma_start(bias_wide[0:96, i, :], row.to_broadcast([96, F])).then_inc(weights_in, 16)
                sp.wait_ge(consts, 1)
                whole = (EG - 1) * G
                for sbuf, name in ((src_c, "src"), (dst_c, "dst")):
                    sp.dma_start(sbuf[:, 0:EG - 1, :], A[name][0:whole].rearrange("(g p j) -> p g j", p=P, j=J)).then_inc(dst_in, 16)
                    sp.dma_start(sbuf[0:ETAIL, EG - 1, :], A[name][whole:E].rearrange("(p j) -> p j", j=J)).then_inc(dst_in, 16)
                sp.dma_start(next_c[:, 0:EG - 1, :], A["dst"][1:whole + 1].rearrange("(g p j) -> p g j", p=P, j=J)).then_inc(dst_in, 16)
                sp.dma_start(next_c[0:ETAIL - 1, EG - 1, :], A["dst"][whole + 1:E - J + 1].rearrange("(p j) -> p j", j=J)).then_inc(dst_in, 16)
                sp.dma_start(next_c[ETAIL - 1:ETAIL, EG - 1, 0:J - 1], A["dst"][E - J + 1:E].rearrange("(p j) -> p j", p=1)).then_inc(dst_in, 16)

            W_LOADS = 16 * (6 + 4 + 5 + 2 + 2)

            @block.gpsimd
            def _(pool):
                nc.gpsimd.memset(src_c[:, :, :], 0)
                nc.gpsimd.memset(dst_c[:, :, :], -1)
                nc.gpsimd.memset(dst_row[:, 0, 0:1], -2)
                nc.gpsimd.memset(next_c[:, :, :], -1).then_inc(prep_p, 1)
                pool.wait_ge(prep_p, 1)
                nc.gpsimd.iota(int_c[:, :, :], pattern=[[G, EG], [1, J]], base=1, channel_multiplier=J).then_inc(consts, 1)
                nc.gpsimd.memset(identity[:, :], 0.0).then_inc(prep_p, 1)
                nc.gpsimd.memset(centre[:, :], -1.0 / F).then_inc(prep_p, 1)
                pool.wait_ge(prep_p, 3)
                nc.gpsimd.affine_select(out=identity[:, :], in_=identity[:, :], compare_op=ALU.not_equal, fill=1.0,
                                        base=0, pattern=[[-1, P]], channel_multiplier=1).then_inc(consts, 1)
                nc.gpsimd.affine_select(out=centre[:, :], in_=centre[:, :], compare_op=ALU.not_equal, fill=1.0 - 1.0 / F,
                                        base=0, pattern=[[-1, P]], channel_multiplier=1).then_inc(consts, 1)
                nc.gpsimd.iota(iota_hi[:, :], pattern=[[1, H]], base=0, channel_multiplier=0,
                               allow_small_or_imprecise_dtypes=True).then_inc(consts, 1)
                nc.gpsimd.iota(iota_lo[:, :], pattern=[[1, P]], base=0, channel_multiplier=0,
                               allow_small_or_imprecise_dtypes=True).then_inc(consts, 1)
                nc.gpsimd.iota(iota_p[:, :], pattern=[[0, 1]], base=0, channel_multiplier=1,
                               allow_small_or_imprecise_dtypes=True).then_inc(consts, 1)
                nc.gpsimd.memset(ones3[:, :], 1.0).then_inc(consts, 1)
                nc.gpsimd.memset(bias_rows[:, :, :], 0.0).then_inc(consts, 1)
            CONSTS = 8

            @block.tensor
            def _(pe):
                pe.wait_ge(consts, CONSTS)
                pe.wait_ge(weights_in, W_LOADS)
                for i in range(4):
                    pe.transpose(bank[0][:, i * F:(i + 1) * F], raw[:, 2 + i, :], identity[:, :])
                pe.wait_ge(prep_v, 2)
                pe.matmul(bank[1][:, 0:F], u_wide[:, :], w1u[:, :], start=True, stop=True)
                pe.matmul(bank[2][:, 0:F], centre[:, :], scaled[:, 0, :], start=True, stop=True)
                pe.matmul(bank[2][:, F:2 * F], centre[:, :], scaled[:, 1, :], start=True, stop=True)
                pe.matmul(bank[3][:, 0:F], be_wide[:, 0, :], raw[:, 0, :], start=True, stop=True)
                pe.matmul(bank[3][:, F:2 * F], be_wide[:, 1, :], raw[:, 1, :], start=True, stop=True).then_inc(prep_p, 1)

            @block.vector
            def _(dve):
                links = [0]

                def link(ins):
                    links[0] += 1
                    ins.then_inc(chain, 1)
                    dve.wait_ge(chain, links[0])

                V = nc.vector
                dve.wait_ge(weights_in, W_LOADS)
                dve.wait_ge(consts, CONSTS)
                V.memset(ones[:, :], 1.0)
                V.memset(eps[:, :], LN_EPS)
                V.memset(u_wide[:, :], 0.0)
                V.memset(be_wide[:, :, :], 0.0).then_inc(prep_v, 1)
                V.memset(var[:, :, :], 1.0)
                dve.wait_ge(prep_v, 1)
                V.tensor_scalar(u_wide[:, :], u_wide[:, :], u_col[:, 0:1], None, ALU.add)
                for i in range(2):
                    V.tensor_scalar(scaled[:, i, :], raw[:, i, :], cols[:, 2 * i:1 + 2 * i], None, ALU.mult)
                    last = V.tensor_scalar(be_wide[:, i, :], be_wide[:, i, :], cols[:, 1 + 2 * i:2 + 2 * i], None, ALU.add)
                last.then_inc(prep_v, 1)
                dve.wait_ge(prep_p, 4)
                V.tensor_copy(wbuf[:, 4:8, :], bank[0][:, :].rearrange("p (w f) -> p w f", w=4))
                link(V.tensor_tensor(bias_wide[0:96, 2], bank[1][0:96, 0:F], bias_wide[0:96, 2], ALU.add))
                link(V.tensor_copy(bias_part[0:96, 0], bias_wide[0:96]))
                link(V.tensor_tensor(bias_tmp[0:96], bias_wide[0:96], bias_part[0:96, 0], ALU.subtract))
                link(V.tensor_copy(bias_part[0:96, 1], bias_tmp[0:96]))
                link(V.tensor_tensor(bias_tmp[0:96], bias_tmp[0:96], bias_part[0:96, 1], ALU.subtract))
                link(V.tensor_copy(bias_part[0:96, 2], bias_tmp[0:96]))
                for part in range(3):
                    r = slice(32 * part, 32 * part + 1)
                    link(V.tensor_copy(bias_rows[r], bias_part[r, part]))
                V.tensor_copy(wbuf[:, 2:4, :], bank[2][:, 0:2 * F].rearrange("p (w f) -> p w f", w=2))
                V.tensor_tensor(bias2[:, :], bank[3][:, 0:F], brow[:, 0, :], ALU.add)
                for j in range(J):
                    link(V.tensor_tensor(bias3[:, j, :], bank[3][:, F:2 * F], brow[:, 1, :], ALU.add))

                dve.wait_ge(dst_in, 16 * 7)
                next_f = fsel[:, 0]
                V.tensor_copy(src_f, src_c[:, :, :])
                V.tensor_copy(dst_f, dst_c[:, :, :])
                link(V.tensor_copy(next_f, next_c[:, :, :]))
                link(V.tensor_tensor(is_last, dst_f, next_f, ALU.not_equal))
                link(V.tensor_scalar(x_idx[:, :, :], dst_f, 0.0, None, ALU.max))
                link(V.tensor_scalar(fsel[:, 1], is_last, -float(N + P), float(N + P), ALU.mult, ALU.add))
                link(V.tensor_tensor(fsel[:, 1], fsel[:, 1], x_idx[:, :, :], ALU.add))
                link(V.tensor_copy(out_idx[:, :, :], fsel[:, 1]))
                tmp = row_idx
                for of, op, by, to in ((int_c, ALU.bitwise_and, P - 1, e_low), (int_c, ALU.bitwise_and, -P, e_high),
                                       (src_c, ALU.logical_shift_right, 7, src_hi), (x_idx, ALU.bitwise_and, P - 1, dst_lo),
                                       (x_idx, ALU.logical_shift_right, 7, dst_hi)):
                    link(V.tensor_scalar(tmp[:, :, :], of[:, :, :], by, None, op))
                    link(V.tensor_copy(to, tmp[:, :, :]))
                link(V.tensor_tensor(e_low, e_low, is_last, ALU.mult))
                link(V.tensor_tensor(e_high, e_high, is_last, ALU.mult))

        S = phase1
        x_in = [sem(f"x_in{s}") for s in range(6)]
        xd_in = [sem(f"xd_in{s}") for s in range(2)]
        ea_in = [sem(f"ea_in{s}") for s in range(2)]
        x_turned, y1_ready, r1_turned, y2_ready, z2_turned, y3_ready, x1_turned, z_ready, ea_turned = [sem(c) for c in (
            "x_turned", "y1_ready", "r1_turned", "y2_ready", "z2_turned", "y3_ready", "x1_turned", "z_ready", "ea_turned")]
        xT_done, r1_done, r1T_done, r2_done, r2T_done, x1T_done, std_done, ssq_done = [sem(c) for c in (
            "xT_done", "r1_done", "r1T_done", "r2_done", "r2T_done", "x1T_done", "std_done", "ssq_done")]
        ln1_raw, ln2_raw, ln3_raw, ln_added, ln_combined, var_done, inv_done = [sem(c) for c in (
            "ln1_raw", "ln2_raw", "ln3_raw", "ln_added", "ln_combined", "var_done", "inv_done")]
        agg_done, z2_done, v3_done, h1_done, xb_done, x1_centred, x1_done = [sem(c) for c in (
            "agg_done", "z2_done", "v3_done", "h1_done", "xb_done", "x1_centred", "x1_done")]
        x_idx_now = sem("x_idx_now")
        dst_row_in = [sem(f"dst_row_in{s}") for s in range(2)]
        src_row_in = [sem(f"src_row_in{s}") for s in range(2)]
        same_done, count_done, low_done = sem("same_done"), sem("count_done"), sem("low_done")
        count_out = [sem(f"count_out{s}") for s in range(2)]
        slots_split = sem("slots_split")
        hot_one, hot_low_ready = sem("hot_low_onehot"), sem("hot_low_ready")
        hot_ready, hot_src_done, table_part = sem("hot_ready"), sem("hot_src_done"), sem("table_part")
        x1_out = [sem(f"x1_out{s}") for s in range(3)]
        h1_out = [sem(f"h1_out{s}") for s in range(2)]

        NODES = ("node", "tail")
        L1 = len(S.kinds)
        link_s = sem("link_s")
        counts_moved, counts_inverted = sem("counts_moved"), sem("counts_inverted")
        by_column = "g (p j) -> p g j"
        LOOKS = 2
        LOOK = (L1 - rest) // U * U + U
        LOOK_END = LOOK + SLOTS // (P * LOOKS)
        assert LOOK_END < L1 + DEPTH1 and J % LOOKS == 0

        def first_look(i):
            return LOOKS * (i - LOOK)

        def loaded1(n):
            return 16 * sum(S.kind(m) in NODES for m in range(n % 6, n + 1, 6))

        def rounds(i):
            return i - 2

        def stored1(n, ring, kinds=("node", "tail", "edge")):
            return 16 * sum(S.kind(m) in kinds for m in range(n % ring, n + 1, ring)) if n >= 0 else 0

        def row_of(list_, first, size):
            return list_.rearrange("(a e) -> a e", a=1)[:, bass.ds(first, size)].to_broadcast([P, size])

        with nc.Block() as block:
            @block.sync
            def _(sp):
                def body(at):
                    n = at.i
                    if S.kind(n) is not None:
                        if S.kind(n) == "edge":
                            e = (n % 6) // 3
                            k = at.value(lambda i: S.upto(i, "edge") - 1)
                            at.wait(sp, same_done, lambda i: S.upto(i, "edge") - 2)
                            if n == 2:
                                sp.dma_start(dst_row[:, e, 1:G + 1], row_of(A["dst"], 0, G)).then_inc(dst_row_in[e], 16)
                            elif n == 3 * EG - 1:
                                size = E - (EG - 1) * G + 1
                                sp.dma_start(dst_row[:, e, 0:size], row_of(A["dst"], E - size, size)).then_inc(dst_row_in[e], 16)
                            else:
                                first = at.value(lambda i: (S.upto(i, "edge") - 1) * G - 1)
                                sp.dma_start(dst_row[:, e, :], row_of(A["dst"], first, G + 1)).then_inc(dst_row_in[e], 16)
                            at.wait(sp, low_done, lambda i: S.upto(i, "edge") - 2)
                            size = E - (EG - 1) * G if n == 3 * EG - 1 else G
                            first = at.value(lambda i: (S.upto(i, "edge") - 1) * G)
                            sp.dma_start(src_row[:, e, 0:size], row_of(A["src"], first, size)).then_inc(src_row_in[e], 16)
                            at.wait(sp, ea_turned, lambda i: S.upto(i, "edge") - 2)
                            if n == 3 * EG - 1:
                                sp.dma_start(ea[0:ETAIL, e].rearrange("p j f -> p (j f)"),
                                             A["edge_attr_128"][(EG - 1) * G:E].rearrange("(p j) f -> p (j f)", j=J)).then_inc(ea_in[e], 16)
                            else:
                                sp.dma_start(ea[:, e].rearrange("p j f -> p (j f)"),
                                             A["edge_attr_128"][0:(EG - 1) * G].rearrange("(g p j) f -> g p (j f)", p=P, j=J)[k]
                                             ).then_inc(ea_in[e], 16)
                        else:
                            at.wait(sp, xb_done, lambda i: i - 5)
                            dst = xg[:, n % 6].rearrange("p j f -> p (j f)")
                            if S.kind(n) == "tail":
                                sp.dma_start(dst[0:TAIL], tail_rows(A["x"])).then_inc(x_in[n % 6], 16)
                            else:
                                k = at.value(lambda i: S.upto(i, "node") - 1)
                                sp.dma_start(dst, node_rows(A["x"], k)).then_inc(x_in[n % 6], 16)
                    n = at.i - 4
                    if S.kind(n) == "edge":
                        e = (n % 6) // 3
                        at.wait(sp, count_done, lambda i: S.upto(i - 4, "edge"))
                        g = at.value(lambda i: S.upto(i - 4, "edge") - 1)
                        sp.dma_start(count_line.rearrange("(g a) n -> g a n", a=1)[g], count[0:1, e, :]).then_inc(count_out[e], 16)
                    if at.i == LOOK + 3:
                        assert at.reg is None
                        for e in range(2):
                            sp.wait_ge(count_out[e], 16 * ((EG + 1 - e) // 2))
                        sp.dma_start(count_c[:, :, :], count_line.rearrange(by_column, j=J)).then_inc(counts_moved, 16)
                    if at.i == LOOK + 11:
                        assert at.reg is None
                        sp.wait_ge(counts_inverted, 1)
                        sp.dma_start(inv_line.rearrange(by_column, j=J), count_c[:, :, :]).then_inc(counts_moved, 16)
                    n = at.i - 8
                    if S.kind(n) is not None:
                        at.wait(sp, x1_done, lambda i: i - 7)
                        at.wait(sp, x1_out[n % 3], lambda i: stored1(i - 11, 3))
                        of = x1[:, n % 3].rearrange("p j f -> p (j f)")
                        if S.kind(n) == "tail":
                            sp.dma_start(tail_rows(x1_table), of[0:TAIL]).then_inc(x1_out[n % 3], 16)
                        elif S.kind(n) == "edge":
                            k = at.value(lambda i: S.upto(i - 8, "edge") - 1)
                            sp.dma_start(edge_rows(x1_table, k), of).then_inc(x1_out[n % 3], 16)
                        else:
                            k = at.value(lambda i: S.upto(i - 8, "node") - 1)
                            sp.dma_start(node_rows(x1_table, k), of).then_inc(x1_out[n % 3], 16)
                    n = at.i - 11
                    if S.kind(n) in NODES:
                        at.wait(sp, h1_done, lambda i: S.upto(i - 11, *NODES))
                        at.wait(sp, h1_out[n % 2], lambda i: stored1(i - 13, 2, NODES))
                        of = h1[:, n % 2].rearrange("p j f -> p (j f)")
                        if S.kind(n) == "tail":
                            sp.dma_start(tail_rows(h1_table), of[0:TAIL]).then_inc(h1_out[n % 2], 16)
                        else:
                            k = at.value(lambda i: S.upto(i - 11, "node") - 1)
                            sp.dma_start(node_rows(h1_table, k), of).then_inc(h1_out[n % 2], 16)
                run_phase(sp, S, DEPTH1 + 2, body)
                sp.wait_ge(counts_moved, 32)
                for s in range(3):
                    last = max(n for n in range(L1) if n % 3 == s)
                    sp.wait_ge(x1_out[s], stored1(last, 3))
                for s in range(2):
                    last = max(n for n in range(L1) if n % 2 == s)
                    sp.wait_ge(h1_out[s], stored1(last, 2, NODES))

            @block.tensor
            def _(pe):
                def nodes(n):
                    return S.upto(n, *NODES)

                def look_up(at, q):
                    j = first_look(at.i) % J + q
                    first = at.value(lambda i: first_look(i) // J * G)
                    hot = hot_src[:, bass.ds(first, G)].rearrange("p (i j) -> p j i", j=J)[:, j, :]
                    for part in range(2):
                        mm = pe.matmul(bank[7][:, 0:H], hot, slot_table[:, part, :], start=(part == 0), stop=(part == 1))
                    mm.then_inc(looked_up, 1)

                def body(at):
                    n = at.i - 3
                    if S.kind(n) is not None:
                        at.wait(pe, r1T_done, lambda i: i - 2)
                        at.wait(pe, z2_done, lambda i: i - 3)
                        for j in range(J):
                            mm = pe.matmul(bank[2][:, j * F:(j + 1) * F], r1T[:, n % 2, j * F:(j + 1) * F], w2c, start=True, stop=True)
                        mm.then_inc(y2_ready, 1)
                    n = at.i - 1
                    if S.kind(n) is not None:
                        edge = S.kind(n) == "edge"
                        at.wait(pe, xT_done, lambda i: i)
                        at.wait(pe, r1_done, lambda i: i - 1)
                        if edge:
                            at.wait(pe, agg_done, lambda i: S.upto(i - 1, "edge"))
                        pe.matmul(bank[1][:, :], ones3[:, :], on_all(bias_rows[:, 2]), start=True, stop=False)
                        for j in range(J):
                            to = bank[1][:, j * F:(j + 1) * F]
                            mm = pe.matmul(to, xT[:, n % 2, j * F:(j + 1) * F], w1x, start=False, stop=j == J - 1 and not edge)
                            if edge:
                                sums = aggT[:, (n % 6) // 3, :].rearrange("p (i j) -> p j i", j=J)[:, j, :]
                                mm = pe.matmul(to, sums, w1e, start=False, stop=j == J - 1)
                        mm.then_inc(y1_ready, 1)
                    if LOOK <= at.i < LOOK_END:
                        if at.i == LOOK:
                            pe.wait_ge(table_copied, 1)
                        at.wait(pe, selected, first_look)
                        look_up(at, 0)
                    n = at.i - 2
                    if S.kind(n) is not None:
                        at.wait(pe, r1_done, lambda i: i - 1)
                        at.wait(pe, r1T_done, lambda i: i - 2)
                        at.wait(pe, r2T_done, lambda i: i - 4)
                        for j in range(J):
                            mm = pe.transpose(bank[3][:, j * F:(j + 1) * F], r1[:, n % 2, j, :], identity[:, :])
                        mm.then_inc(r1_turned, 1)
                    n = at.i
                    if S.kind(n) is not None:
                        if S.kind(n) == "edge":
                            at.wait(pe, xd_in[(n % 6) // 3], lambda i: 16 * J * ((S.upto(i, "edge") + 1) // 2))
                        else:
                            at.wait(pe, x_in[n % 6], loaded1)
                        at.wait(pe, x1T_done, lambda i: nodes(i - 8))
                        at.wait(pe, xT_done, lambda i: i)
                        for j in range(J):
                            mm = pe.transpose(bank[0][:, j * F:(j + 1) * F], xg[:, n % 6, j, :], identity[:, :])
                        mm.then_inc(x_turned, 1)
                    n = at.i - 5
                    if S.kind(n) is not None:
                        at.wait(pe, r2T_done, lambda i: i - 4)
                        at.wait(pe, v3_done, lambda i: i - 5)
                        for j in range(J):
                            mm = pe.matmul(bank[4][:, j * F:(j + 1) * F], r2[:, n % 2, j * F:(j + 1) * F], w3c, start=True, stop=True)
                        mm.then_inc(y3_ready, 1)
                    n = at.i - 8
                    if S.kind(n) in NODES:
                        at.wait(pe, x1T_done, lambda i: nodes(i - 8))
                        at.wait(pe, h1_done, lambda i: nodes(i - 10))
                        pe.matmul(bank[5 + n % 2][:, :], ones3[:, :], on_all(bias_rows[:, 0]), start=True, stop=False)
                        for j in range(J):
                            mm = pe.matmul(bank[5 + n % 2][:, j * F:(j + 1) * F], x1T[:, n % 2, j * F:(j + 1) * F], wr0,
                                           start=False, stop=j == J - 1)
                        mm.then_inc(z_ready, 1)
                    if S.kind(at.i - 3) == "edge":
                        at.wait(pe, hot_ready, lambda i: S.upto(i - 3, "edge"))
                        at.wait(pe, hot_low_ready, lambda i: S.upto(i - 3, "edge"))
                        for j in range(J):
                            for part in range(2):
                                mm = pe.matmul(bank[7][:, 0:H], hot_lo[:, j, part, :], hot_hi[:, j, :],
                                               start=(at.i == 5 and j + part == 0), stop=(at.i == 3 * EG + 2 and j + part == J))
                        mm.then_inc(table_part, 1)
                    if LOOK <= at.i < LOOK_END:
                        at.wait(pe, selected, lambda i: first_look(i) + 1)
                        look_up(at, 1)
                    n = at.i - 4
                    if S.kind(n) is not None:
                        at.wait(pe, r2_done, lambda i: i - 3)
                        at.wait(pe, r1T_done, lambda i: min(i - 1, L1))
                        for j in range(J):
                            mm = pe.transpose(bank[3][:, j * F:(j + 1) * F], z2[:, n % 2, j, :], identity[:, :])
                        mm.then_inc(z2_turned, 1)
                    n = at.i
                    if S.kind(n) == "edge":
                        at.wait(pe, ea_in[(n % 6) // 3], lambda i: 16 * ((S.upto(i, "edge") + 1) // 2))
                        at.wait(pe, r1_done, lambda i: i)
                        for j in range(J):
                            mm = pe.transpose(bank[1][:, :].rearrange("p (i j) -> p j i", j=J)[:, j, :],
                                              ea[:, (n % 6) // 3, j, :], identity[:, :])
                        mm.then_inc(ea_turned, 1)
                    n = at.i - 7
                    if S.kind(n) in NODES:
                        at.wait(pe, x1_done, lambda i: i - 6)
                        at.wait(pe, xT_done, lambda i: min(i + 1, L1))
                        for j in range(J):
                            mm = pe.transpose(bank[0][:, j * F:(j + 1) * F], x1[:, n % 3, j, :], identity[:, :])
                        mm.then_inc(x1_turned, 1)
                run_phase(pe, S, DEPTH1, body)

            @block.scalar
            def _(act):
                def nodes(n):
                    return S.upto(n, *NODES)

                def body(at):
                    if at.i >= 3:
                        at.wait(act, var_done, rounds)
                        nc.scalar.activation(std[:, at.i % 2, 0:12], var[:, at.i % 2, 0:12], ACT.Sqrt, scale=1.0 / F, bias=eps[:, :])
                        nc.scalar.activation(std[:, at.i % 2, 12:16], var[:, at.i % 2, 12:16], ACT.Sqrt).then_inc(std_done, 1)
                    n = at.i - 2
                    if S.kind(n) is not None:
                        at.wait(act, r1_turned, lambda i: i - 1)
                        at.wait(act, y2_ready, lambda i: i - 3)
                        nc.scalar.copy(r1T[:, n % 2, :], bank[3][:, :]).then_inc(r1T_done, 1)
                    n = at.i
                    if S.kind(n) is not None:
                        at.wait(act, x_turned, lambda i: i + 1)
                        at.wait(act, y1_ready, lambda i: i - 1)
                        nc.scalar.copy(xT[:, n % 2, :], bank[0][:, :]).then_inc(xT_done, 1)
                    n = at.i - 1
                    if S.kind(n) is not None:
                        at.wait(act, y1_ready, lambda i: i)
                        at.wait(act, r1_turned, lambda i: i - 2)
                        at.wait(act, ln1_raw, lambda i: i - 2)
                        nc.scalar.activation(r1[:, n % 2].rearrange("p j f -> p (j f)"), bank[1][:, :], ACT.Relu).then_inc(r1_done, 1)
                    n = at.i - 9
                    if S.kind(n) in NODES:
                        at.wait(act, inv_done, rounds)
                        at.wait(act, h1_out[n % 2], lambda i: stored1(i - 11, 2, NODES))
                        for j in range(J):
                            ins = nc.scalar.activation(h1[:, n % 2, j, :], bank[5 + n % 2][:, j * F:(j + 1) * F], ACT.Relu,
                                                       scale=inv[:, at.i % 2, 12 + j:13 + j])
                        ins.then_inc(h1_done, 1)
                    n = at.i - 3
                    if S.kind(n) is not None:
                        at.wait(act, z2_done, lambda i: i - 2)
                        nc.scalar.activation(z2[:, n % 2], z2[:, n % 2], ACT.Relu).then_inc(r2_done, 1)
                    n = at.i - 4
                    if S.kind(n) is not None:
                        at.wait(act, z2_turned, lambda i: i - 3)
                        at.wait(act, y3_ready, lambda i: i - 5)
                        nc.scalar.copy(r2[:, n % 2, :], bank[3][:, :]).then_inc(r2T_done, 1)
                    n = at.i - 7
                    if S.kind(n) in NODES:
                        at.wait(act, x1_turned, lambda i: nodes(i - 7))
                        at.wait(act, z_ready, lambda i: nodes(i - 9))
                        nc.scalar.copy(x1T[:, n % 2, :], bank[0][:, :]).then_inc(x1T_done, 1)
                    n = at.i - 8
                    if S.kind(n) in NODES:
                        at.wait(act, z_ready, lambda i: nodes(i - 8))
                        at.wait(act, ssq_done, lambda i: J * nodes(i - 9))
                        at.wait(act, var_done, lambda i: rounds(i - 1))
                        for j in range(J):
                            nc.scalar.activation(junk[:, j, :], bank[5 + n % 2][:, j * F:(j + 1) * F], ACT.Square,
                                                 accum_out=ssq[:, n % 2, j:j + 1]).then_inc(ssq_done, 1)
                    if S.kind(at.i - 1) == "edge":
                        g = at.value(lambda i: S.upto(i - 1, "edge") - 1)
                        at.wait(act, hot_one, lambda i: S.upto(i - 1, "edge"))
                        at.wait(act, table_part, lambda i: S.upto(i - 1, "edge") - 1)
                        for j in range(J):
                            nc.scalar.activation(hot_lo[:, j, 0, :], hot_low[:, j, :], ACT.Copy, scale=e_high[:, g, j:j + 1])
                    if S.kind(at.i - 2) == "edge":
                        g = at.value(lambda i: S.upto(i - 2, "edge") - 1)
                        for j in range(J):
                            ins = nc.scalar.activation(hot_lo[:, j, 1, :], hot_low[:, j, :], ACT.Copy, scale=e_low[:, g, j:j + 1])
                        ins.then_inc(hot_low_ready, 1)
                run_phase(act, S, DEPTH1, body)

            @block.vector
            def _(dve):
                V = nc.vector
                lows = iota_lo[:, :].rearrange("p (a l) -> p a l", a=1).to_broadcast([P, J, P])

                links = [0]

                def link(ins):
                    links[0] += 1
                    ins.then_inc(link_s, 1)
                    dve.wait_ge(link_s, links[0])

                def select(at, q):
                    slot = first_look(at.i) + q
                    at.wait(dve, looked_up, lambda i: first_look(i) + q + 1)
                    at.wait(dve, selected, lambda i: first_look(i) + q - 1) if slot >= 2 else None
                    g, j = at.value(lambda i: first_look(i) // J), slot % J
                    V.scalar_tensor_tensor(out=entries[:, slot % 2, :], in0=iota_hi[:, :], scalar=src_hi[:, g, j:j + 1],
                                           in1=bank[7][:, 0:H], op0=ALU.is_equal, op1=ALU.mult,
                                           accum_out=found[:, g, j:j + 1]).then_inc(selected, 1)

                def row_stats(at, layer, of, done):
                    for j in range(J):
                        ins = V.bn_stats(ln_raw[:, at.i % 2, layer, j, :], of[:, j, :])
                    ins.then_inc(done, 1)

                def body(at):
                    par = at.i % 2
                    n = at.i - 2
                    if S.kind(n) is not None:
                        at.wait(dve, r1_done, lambda i: i - 1)
                        row_stats(at, 0, r1[:, n % 2], ln1_raw)
                    if at.i >= 3:
                        there = [l for l, behind in enumerate((3, 5, 6)) if S.kind(at.i - behind) is not None]
                        ins = None
                        if there:
                            at.wait(dve, ln_combined, lambda i: i - 2)
                            r = slice(there[0], there[-1] + 1)
                            ins = V.scalar_tensor_tensor(out=var[:, par, 0:12].rearrange("p (l j) -> p l j", l=3)[:, r],
                                                         in0=ln_diff2[:, 1 - par, r], scalar=F / 4.0, in1=ln_within[:, 1 - par, r],
                                                         op0=ALU.mult, op1=ALU.add)
                        if S.kind(at.i - 9) in NODES:
                            at.wait(dve, ssq_done, lambda i: J * S.upto(i - 9, *NODES))
                            ins = V.tensor_scalar(var[:, par, 12:16], ssq[:, (at.i - 9) % 2, :], NORM_EPS * NORM_EPS, None, ALU.max)
                        if ins is None:
                            ins = at.idle(dve)
                        ins.then_inc(var_done, 1)
                    n = at.i - 4
                    if S.kind(n) is not None:
                        at.wait(dve, r2_done, lambda i: i - 3)
                        row_stats(at, 1, z2[:, n % 2], ln2_raw)
                    if at.i >= 3:
                        at.wait(dve, std_done, rounds)
                        V.reciprocal(inv[:, par, :], std[:, par, :]).then_inc(inv_done, 1)
                        at.wait(dve, inv_done, rounds)
                    n = at.i - 3
                    if S.kind(n) is not None:
                        at.wait(dve, y2_ready, lambda i: i - 2)
                        at.wait(dve, z2_turned, lambda i: i - 4)
                        for j in range(J):
                            ins = V.scalar_tensor_tensor(out=z2[:, n % 2, j, :], in0=bank[2][:, j * F:(j + 1) * F],
                                                         scalar=inv[:, par, j:j + 1], in1=bias2[:, :], op0=ALU.mult, op1=ALU.add)
                        ins.then_inc(z2_done, 1)
                    if LOOK <= at.i < LOOK_END:
                        if at.i == LOOK:
                            dve.wait_ge(table_copied, 1)
                        select(at, 0)
                    n = at.i - 5
                    if S.kind(n) is not None:
                        at.wait(dve, y3_ready, lambda i: i - 4)
                        at.wait(dve, xb_done, lambda i: i - 4)
                        at.wait(dve, x1_done, lambda i: i - 6)
                        for j in range(J):
                            ins = V.scalar_tensor_tensor(out=v3[:, n % 2, j, :], in0=bank[4][:, j * F:(j + 1) * F],
                                                         scalar=inv[:, par, 4 + j:5 + j], in1=xb[:, n % 3, j, :], op0=ALU.mult, op1=ALU.add)
                        ins.then_inc(v3_done, 1)
                        at.wait(dve, v3_done, lambda i: i - 4)
                        row_stats(at, 2, v3[:, n % 2], ln3_raw)
                    if S.kind(at.i) == "edge":
                        e = (at.i % 6) // 3
                        first = at.value(lambda i: (S.upto(i, "edge") - 1) * G)
                        at.wait(dve, same_done, lambda i: S.upto(i, "edge"))
                        at.wait(dve, ea_turned, lambda i: S.upto(i, "edge"))
                        at.wait(dve, y1_ready, lambda i: i - 5)
                        at.wait(dve, agg_done, lambda i: S.upto(i, "edge") - 1)
                        V.tensor_tensor_scan(aggT[:, e, :], same[:, bass.ds(first, G)], bank[1][:, :],
                                             0.0 if at.i < 3 else aggT[:, 1 - e, G - 1:G], ALU.mult, ALU.add).then_inc(agg_done, 1)
                        g = at.value(lambda i: S.upto(i, "edge") - 1)
                        at.wait(dve, hot_low_ready, lambda i: S.upto(i, "edge") - 1)
                        V.tensor_tensor(hot_low[:, :, :], lows, dst_lo[:, g, :].rearrange("p (j a) -> p j a", a=1).to_broadcast([P, J, P]),
                                        ALU.is_equal).then_inc(hot_one, 1)
                        at.wait(dve, count_done, lambda i: S.upto(i, "edge") - 1)
                        at.wait(dve, count_out[e], lambda i: 16 * ((S.upto(i, "edge") - 1) // 2))
                        V.tensor_tensor_scan(count[:, e, :], same[:, bass.ds(first, G)], ones[:, :],
                                             0.0 if at.i < 3 else count[:, 1 - e, G - 1:G], ALU.mult, ALU.add).then_inc(count_done, 1)
                    if S.kind(at.i + 1) == "edge":
                        e = ((at.i + 1) % 6) // 3
                        at.wait(dve, dst_row_in[e], lambda i: 16 * ((S.upto(i + 1, "edge") + 1) // 2))
                        first = at.value(lambda i: (S.upto(i + 1, "edge") - 1) * G)
                        V.tensor_tensor(same[:, bass.ds(first, G)], dst_row[:, e, 1:G + 1], dst_row[:, e, 0:G],
                                        ALU.is_equal).then_inc(same_done, 1)
                    if S.kind(at.i - 2) == "edge":
                        e = ((at.i - 2) % 6) // 3
                        at.wait(dve, src_row_in[e], lambda i: 16 * ((S.upto(i - 2, "edge") + 1) // 2))
                        at.wait(dve, hot_src_done, lambda i: S.upto(i - 2, "edge") - 1)
                        V.tensor_scalar(src_low[:, :], src_row[:, e, :], P - 1, None, ALU.bitwise_and).then_inc(low_done, 1)
                        first = at.value(lambda i: (S.upto(i - 2, "edge") - 1) * G)
                        at.wait(dve, low_done, lambda i: S.upto(i - 2, "edge"))
                        V.tensor_scalar(hot_src[:, bass.ds(first, G)], src_low[:, :], iota_p[:, 0:1], None, ALU.is_equal).then_inc(hot_src_done, 1)
                    if S.kind(at.i - 1) == "edge":
                        g = at.value(lambda i: S.upto(i - 1, "edge") - 1)
                        at.wait(dve, table_part, lambda i: S.upto(i - 1, "edge") - 1)
                        for j in range(J):
                            ins = V.tensor_scalar(hot_hi[:, j, :], iota_hi[:, :], dst_hi[:, g, j:j + 1], None, ALU.is_equal)
                        ins.then_inc(hot_ready, 1)
                    if at.i == LOOK - 1:
                        assert at.reg is None
                        dve.wait_ge(table_part, EG)
                        V.tensor_copy(slot_int[:, 0, :], bank[7][:, 0:H]).then_inc(slots_split, 1)
                        dve.wait_ge(slots_split, 1)
                        V.tensor_scalar(slot_int[:, 1, :], slot_int[:, 0, :], P - 1, None, ALU.bitwise_and).then_inc(slots_split, 1)
                        dve.wait_ge(slots_split, 2)
                        V.tensor_scalar(slot_int[:, 0, :], slot_int[:, 0, :], -P, None, ALU.bitwise_and).then_inc(slots_split, 1)
                        dve.wait_ge(slots_split, 3)
                        V.tensor_copy(slot_table[:, :, :], slot_int[:, :, :]).then_inc(table_copied, 1)
                    if LOOK <= at.i < LOOK_END:
                        select(at, 1)
                    if at.i == LOOK + 5:
                        assert at.reg is None
                        dve.wait_ge(counts_moved, 16)
                        V.reciprocal(count_c[:, :, :], count_c[:, :, :]).then_inc(counts_inverted, 1)
                    if at.i == LOOK_END:
                        assert at.reg is None
                        dve.wait_ge(selected, SLOTS // P)
                        link(V.tensor_scalar(fsel[:, 0], found[:, :, :], 0.0, None, ALU.is_gt))
                        link(V.tensor_tensor(fsel[:, 1], found[:, :, :], src_f, ALU.subtract))
                        link(V.tensor_scalar(fsel[:, 1], fsel[:, 1], float(N - 1), None, ALU.add))
                        link(V.tensor_tensor(fsel[:, 1], fsel[:, 1], fsel[:, 0], ALU.mult))
                        link(V.tensor_tensor(fsel[:, 1], fsel[:, 1], src_f, ALU.add))
                        link(V.tensor_copy(row_idx[:, :, :], fsel[:, 1]))
                run_phase(dve, S, DEPTH1, body)

            @block.gpsimd
            def _(pool):
                Q = nc.gpsimd

                def on_rows(per_row):
                    return per_row.rearrange("p (j a) -> p j a", a=1).to_broadcast([P, J, F])

                def gather(n, part):
                    e = (n % 6) // 3
                    for j in (2 * part, 2 * part + 1):
                        Q.indirect_dma_start(out=xg[:, n % 6, j, :], out_offset=None, in_=A["x"],
                                             in_offset=bass.IndirectOffsetOnAxis(ap=idx_now[:, e, j:j + 1], axis=0),
                                             bounds_check=N - 1, oob_is_err=False).then_inc(xd_in[e], 16)

                def body(at):
                    n = at.i + 2
                    if S.kind(n) == "edge":
                        at.wait(pool, xb_done, lambda i: i - 3)
                        k = at.value(lambda i: S.upto(i + 2, "edge") - 1)
                        Q.tensor_copy(idx_now[:, (n % 6) // 3, :], x_idx[:, k, :]).then_inc(x_idx_now, 1)
                        at.wait(pool, x_idx_now, lambda i: S.upto(i + 2, "edge"))
                        gather(n, 0)
                    n = at.i + 1
                    if S.kind(n) == "edge":
                        gather(n, 1)
                    n = at.i - 6
                    if S.kind(n) is not None:
                        at.wait(pool, inv_done, rounds)
                        at.wait(pool, ln_combined, lambda i: i - 2)
                        at.wait(pool, x1_turned, lambda i: S.upto(i - 9, *NODES))
                        at.wait(pool, x1_out[n % 3], lambda i: stored1(i - 9, 3))
                        Q.tensor_tensor(x1[:, n % 3], v3[:, n % 2], on_rows(ln_mean[:, 1 - at.i % 2]),
                                        ALU.subtract).then_inc(x1_centred, 1)
                        at.wait(pool, x1_centred, lambda i: i - 5)
                        Q.tensor_tensor(x1[:, n % 3], x1[:, n % 3], on_rows(inv[:, at.i % 2, 8:12]), ALU.mult).then_inc(x1_done, 1)
                    now = [(l, raw, behind) for l, (raw, behind) in enumerate(((ln1_raw, 2), (ln2_raw, 4), (ln3_raw, 5)))
                           if S.kind(at.i - behind) is not None]
                    if now:
                        for l, raw, behind in now:
                            at.wait(pool, raw, lambda i: i - behind + 1)
                        if at.i >= 4:
                            at.wait(pool, var_done, lambda i: rounds(i - 1))
                        par, r = at.i % 2, slice(now[0][0], now[-1][0] + 1)
                        raw = ln_raw[:, par, r]
                        Q.tensor_tensor(ln_sum[:, par, r], raw[:, :, :, 1], raw[:, :, :, 4], ALU.add).then_inc(ln_added, 1)
                        Q.tensor_tensor(ln_diff[:, par, r], raw[:, :, :, 1], raw[:, :, :, 4], ALU.subtract).then_inc(ln_added, 1)
                        Q.tensor_tensor(ln_within[:, par, r], raw[:, :, :, 2], raw[:, :, :, 5], ALU.add)
                        at.wait(pool, ln_added, lambda i: 2 * (i - 1))
                        if now[-1][0] == 2:
                            Q.tensor_scalar(ln_mean[:, par], ln_sum[:, par, 2], 0.5, None, ALU.mult)
                        Q.tensor_tensor(ln_diff2[:, par, r], ln_diff[:, par, r], ln_diff[:, par, r], ALU.mult).then_inc(ln_combined, 1)
                    n = at.i - 3
                    if S.kind(n) is not None:
                        at.wait(pool, x_turned, lambda i: i - 2)
                        at.wait(pool, v3_done, lambda i: i - 5)
                        Q.tensor_tensor(xb[:, n % 3], xg[:, n % 6], bias3[:, :, :], ALU.add).then_inc(xb_done, 1)
                run_phase(pool, S, DEPTH1, body)

        scattered = sem("scattered")

        def sage_phase(S, name, first_node, wr_e, wl_e, bias_e, res_e):
            LS = len(S.kinds)
            table = x1_table if not res_e else h1_table
            rows_in = [sem(f"{name}_rows_in{s}") for s in range(3)]
            x1_in = [sem(f"{name}_x1_in{s}") for s in range(6)]
            counts_in = [sem(f"{name}_counts_in{s}") for s in range(2)]
            msg_in = [sem(f"{name}_messages_in{s}") for s in range(2)]
            turned, msg_turned, z_ready = sem(f"{name}_turned"), sem(f"{name}_messages_turned"), sem(f"{name}_z")
            rowsT_done, ssq_ready, std_ready = sem(f"{name}_rT"), sem(f"{name}_ssq"), sem(f"{name}_std")
            var_ready, nmean_done, sums_done, mean_done = sem(f"{name}_var"), sem(f"{name}_nmean"), sem(f"{name}_agg"), sem(f"{name}_mean")
            u_done, raw_ready, stats_ready, sum_done, normed = sem(f"{name}_u"), sem(f"{name}_raw_stats"), sem(f"{name}_stats"), sem(f"{name}_sum"), sem(f"{name}_normed")
            idx_copied = sem(f"{name}_idx_copied")
            stored = [sem(f"{name}_stored{s}") for s in range(3)]
            ALL = ("node", "tail", "edge")
            FULL = ALL if res_e else NODES

            def up(n, *k):
                return S.upto(n, *k)

            def in_slot(n, ring, kinds, w=lambda k: 16):
                return sum(w(S.kind(m)) for m in range(n % ring, n + 1, ring) if S.kind(m) in kinds) if n >= 0 else 0

            def rounds2(i):
                return i - 2

            STORED = NODES if res_e else ALL
            X1, STORE = 3, 9

            with nc.Block() as block:
                @block.sync
                def _(sp):
                    def body(at):
                        n = at.i
                        k = S.kind(n)
                        if k in ALL:
                            at.wait(sp, turned, lambda i: up(i - 3))
                            dst = rows[:, n % 3].rearrange("p j f -> p (j f)")
                            if k == "edge":
                                g = at.value(lambda i: up(i, "edge") - 1)
                                sp.dma_start(dst, edge_rows(table, g)).then_inc(rows_in[n % 3], 16)
                                e = (n % 6) // 3
                                at.wait(sp, mean_done, lambda i: up(i, "edge") - 2)
                                sp.dma_start(inv_count[:, e, :], inv_line.rearrange("(g a) n -> g a n", a=1)[g].to_broadcast([P, G])
                                             ).then_inc(counts_in[e], 16)
                            elif k == "tail":
                                sp.dma_start(dst[0:TAIL], tail_rows(h1_table)).then_inc(rows_in[n % 3], 16)
                            else:
                                g = at.value(lambda i: first_node + up(i, "node") - 1)
                                sp.dma_start(dst, node_rows(h1_table, g)).then_inc(rows_in[n % 3], 16)
                        n = at.i - X1
                        k = S.kind(n)
                        if k in FULL:
                            at.wait(sp, normed, lambda i: up(i - X1 - 6, *FULL))
                            dst = xg[:, n % 6].rearrange("p j f -> p (j f)")
                            if k == "edge":
                                g = at.value(lambda i: up(i - X1, "edge") - 1)
                                sp.dma_start(dst, edge_rows(x1_table, g)).then_inc(x1_in[n % 6], 16)
                            elif k == "tail":
                                sp.dma_start(dst[0:TAIL], tail_rows(x1_table)).then_inc(x1_in[n % 6], 16)
                            else:
                                g = at.value(lambda i: first_node + up(i - X1, "node") - 1)
                                sp.dma_start(dst, node_rows(x1_table, g)).then_inc(x1_in[n % 6], 16)
                        n = at.i - STORE
                        k = S.kind(n)
                        if k in NODES:
                            at.wait(sp, normed, lambda i: up(i - STORE, *FULL))
                            at.wait(sp, stored[n % 3], lambda i: in_slot(i - STORE - 3, 3, STORED))
                            of = x1[:, n % 3].rearrange("p j f -> p (j f)")
                            if k == "tail":
                                sp.dma_start(tail_rows(out), of[0:TAIL]).then_inc(stored[n % 3], 16)
                            else:
                                g = at.value(lambda i: first_node + up(i - STORE, "node") - 1)
                                sp.dma_start(node_rows(out, g), of).then_inc(stored[n % 3], 16)
                        elif k == "edge" and not res_e:
                            at.wait(sp, u_done, lambda i: up(i - STORE))
                            at.wait(sp, stored[n % 3], lambda i: in_slot(i - STORE - 3, 3, STORED))
                            g = at.value(lambda i: up(i - STORE, "edge") - 1)
                            sp.dma_start(edge_rows(h1_table, g), z2[:, (n % 6) // 3].rearrange("p j f -> p (j f)")).then_inc(stored[n % 3], 16)
                    run_phase(sp, S, STORE, body)
                    for s in range(3):
                        last = max(n for n in range(LS) if n % 3 == s)
                        sp.wait_ge(stored[s], in_slot(last, 3, STORED))

                @block.tensor
                def _(pe):
                    def body(at):
                        n = at.i
                        k = S.kind(n)
                        if k in ALL:
                            at.wait(pe, rows_in[n % 3], lambda i: in_slot(i, 3, ALL))
                            at.wait(pe, rowsT_done, lambda i: up(i - 1))
                            for j in range(J):
                                mm = pe.transpose(bank[0][:, j * F:(j + 1) * F], rows[:, n % 3, j, :], identity[:, :])
                            mm.then_inc(turned, 1)
                        n = at.i + 1
                        if S.kind(n) == "edge":
                            e = (n % 6) // 3
                            at.wait(pe, msg_in[e], lambda i: 16 * J * ((up(i + 1, "edge") + 1) // 2))
                            at.wait(pe, sums_done, lambda i: up(i + 1, "edge") - 1)
                            for j in range(J):
                                mm = pe.transpose(bank[1][:, :].rearrange("p (i j) -> p j i", j=J)[:, j, :], ea[:, e, j, :], identity[:, :])
                            mm.then_inc(msg_turned, 1)
                        n = at.i - 1
                        k = S.kind(n)
                        if k in ALL:
                            edge = k == "edge"
                            zb = bank[2 + n % 6]
                            at.wait(pe, rowsT_done, lambda i: up(i - 1))
                            at.wait(pe, u_done, lambda i: up(i - 7))
                            if edge:
                                at.wait(pe, mean_done, lambda i: up(i - 1, "edge"))
                            b = bias_e if edge else 1
                            pe.matmul(zb[:, :], ones3[:, :], on_all(bias_rows[:, b]), start=True, stop=False)
                            for j in range(J):
                                mm = pe.matmul(zb[:, j * F:(j + 1) * F], x1T[:, n % 2, j * F:(j + 1) * F], wr_e if edge else wr1,
                                               start=False, stop=j == J - 1 and not edge)
                                if edge:
                                    mm = pe.matmul(zb[:, j * F:(j + 1) * F], r2[:, (n % 6) // 3, j * F:(j + 1) * F], wl_e,
                                                   start=False, stop=j == J - 1)
                            mm.then_inc(z_ready, 1)
                    run_phase(pe, S, DEPTH2, body)

                @block.scalar
                def _(act):
                    def body(at):
                        if at.i >= 3:
                            at.wait(act, var_ready, rounds2)
                            nc.scalar.activation(std[:, at.i % 2, 0:8], var[:, at.i % 2, 0:8], ACT.Sqrt).then_inc(std_ready, 1)
                        n = at.i
                        if S.kind(n) in ALL:
                            at.wait(act, turned, lambda i: up(i))
                            at.wait(act, z_ready, lambda i: up(i - 2))
                            nc.scalar.copy(x1T[:, n % 2, :], bank[0][:, :]).then_inc(rowsT_done, 1)
                        n = at.i - 2
                        if S.kind(n) in ALL:
                            at.wait(act, z_ready, lambda i: up(i - 2))
                            at.wait(act, ssq_ready, lambda i: J * up(i - 3))
                            at.wait(act, var_ready, lambda i: rounds2(i - 1))
                            for j in range(J):
                                nc.scalar.activation(junk[:, j, :], bank[2 + n % 6][:, j * F:(j + 1) * F], ACT.Square,
                                                     accum_out=ssq[:, n % 2, j:j + 1]).then_inc(ssq_ready, 1)
                        n = at.i - 6
                        if S.kind(n) in FULL:
                            at.wait(act, nmean_done, rounds2)
                            at.wait(act, stored[n % 3], lambda i: in_slot(i - 9, 3, STORED))
                            to = x1[:, n % 3]
                            if S.kind(n) == "edge":
                                to = results[:, at.value(lambda i: up(i - 6, "edge") - 1)]
                            for j in range(J):
                                ins = nc.scalar.activation(to[:, j, :], xg[:, n % 6, j, :], ACT.Identity,
                                                           bias=nmean[:, at.i % 2, j:j + 1], scale=inv[:, at.i % 2, 4 + j:5 + j])
                            ins.then_inc(normed, 1)
                    run_phase(act, S, DEPTH2, body)

                @block.vector
                def _(dve):
                    V = nc.vector

                    def body(at):
                        par = at.i % 2
                        if at.i >= 3:
                            if S.kind(at.i - 6) in FULL:
                                at.wait(dve, stats_ready, lambda i: up(i - 6, *FULL))
                                V.tensor_scalar(var[:, par, 4:8], bn2[:, (at.i - 6) % 2, :, 1], LN_EPS, None, ALU.add)
                            if S.kind(at.i - 3) in ALL:
                                at.wait(dve, ssq_ready, lambda i: J * up(i - 3))
                                V.tensor_scalar(var[:, par, 0:4], ssq[:, (at.i - 3) % 2, :], NORM_EPS * NORM_EPS, None,
                                                ALU.max).then_inc(var_ready, 1)
                            else:
                                at.idle(dve).then_inc(var_ready, 1)
                        n = at.i - 4
                        if S.kind(n) in ALL:
                            full = S.kind(n) in FULL
                            u = v3[:, n % 2] if full else z2[:, (n % 6) // 3]
                            if full:
                                at.wait(dve, sum_done, lambda i: up(i - 6, *FULL))
                            else:
                                at.wait(dve, stored[n % 3], lambda i: in_slot(i - 10, 3, STORED))
                            for j in range(J):
                                ins = V.tensor_scalar(u[:, j, :], bank[2 + n % 6][:, j * F:(j + 1) * F], 0.0,
                                                      inv[:, 1 - par, j:j + 1], ALU.max, ALU.mult)
                            ins.then_inc(u_done, 1)
                        if at.i >= 3:
                            at.wait(dve, std_ready, rounds2)
                            V.reciprocal(inv[:, par, 0:8], std[:, par, 0:8]).then_inc(inv_ready, 1)
                        n = at.i - 5
                        if S.kind(n) in FULL:
                            at.wait(dve, sum_done, lambda i: up(i - 5, *FULL))
                            for j in range(J // 2):
                                V.bn_stats(bn6[:, n % 2, j, :], xg[:, n % 6, j, :])
                        if at.i >= 3:
                            dve.wait_ge(inv_ready, at.value(lambda i: i - 2 + inv_before[name]))
                            if S.kind(at.i - 6) in FULL:
                                V.scalar_tensor_tensor(out=nmean[:, par, :], in0=bn2[:, (at.i - 6) % 2, :, 0], scalar=-1.0,
                                                       in1=inv[:, par, 4:8], op0=ALU.mult, op1=ALU.mult).then_inc(nmean_done, 1)
                            else:
                                at.idle(dve).then_inc(nmean_done, 1)
                        if S.kind(n) in FULL:
                            for j in range(J // 2, J):
                                ins = V.bn_stats(bn6[:, n % 2, j, :], xg[:, n % 6, j, :])
                            ins.then_inc(raw_ready, 1)
                        if S.kind(at.i + 1) == "edge":
                            e = ((at.i + 1) % 6) // 3
                            at.wait(dve, msg_turned, lambda i: up(i + 1, "edge"))
                            at.wait(dve, mean_done, lambda i: up(i + 1, "edge") - 1)
                            first = at.value(lambda i: (up(i + 1, "edge") - 1) * G)
                            V.tensor_tensor_scan(aggT[:, e, :], same[:, bass.ds(first, G)], bank[1][:, :],
                                                 0.0 if at.i < 2 else aggT[:, 1 - e, G - 1:G], ALU.mult, ALU.add).then_inc(sums_done, 1)
                        if S.kind(n) in FULL:
                            at.wait(dve, raw_ready, lambda i: up(i - 5, *FULL), apart=True)
                            for j in range(J):
                                ins = V.bn_aggr(bn2[:, n % 2, j, :], bn6[:, n % 2, j, :])
                            ins.then_inc(stats_ready, 1)
                        if S.kind(at.i + 1) == "edge":
                            at.wait(dve, z_ready, lambda i: up(i - 5))
                            at.wait(dve, sums_done, lambda i: up(i + 1, "edge"))
                            at.wait(dve, counts_in[e], lambda i: 16 * ((up(i + 1, "edge") + 1) // 2))
                            V.tensor_tensor(r2[:, e, :].rearrange("p (j i) -> p j i", j=J),
                                            aggT[:, e, :].rearrange("p (i j) -> p j i", j=J),
                                            inv_count[:, e, :].rearrange("p (i j) -> p j i", j=J), ALU.mult).then_inc(mean_done, 1)
                    run_phase(dve, S, DEPTH2, body)

                @block.gpsimd
                def _(pool):
                    Q = nc.gpsimd

                    def indices(at, ahead):
                        e = ((at.i + ahead) % 6) // 3
                        g = at.value(lambda i: up(i + ahead, "edge") - 1)
                        at.wait(pool, msg_turned, lambda i: up(i + ahead, "edge") - 2)
                        Q.tensor_copy(idx_now[:, e, :], row_idx[:, g, :]).then_inc(idx_copied, 1)
                        at.wait(pool, idx_copied, lambda i: up(i + ahead, "edge"))

                    def gather(n, part):
                        e = (n % 6) // 3
                        for j in (2 * part, 2 * part + 1):
                            Q.indirect_dma_start(out=ea[:, e, j, :], out_offset=None, in_=table,
                                                 in_offset=bass.IndirectOffsetOnAxis(ap=idx_now[:, e, j:j + 1], axis=0),
                                                 bounds_check=ROWS - 1, oob_is_err=False).then_inc(msg_in[e], 16)

                    def body(at):
                        n = at.i - 4
                        if S.kind(n) in FULL:
                            at.wait(pool, u_done, lambda i: up(i - 4))
                            at.wait(pool, x1_in[n % 6], lambda i: in_slot(i - 4, 6, FULL))
                            Q.tensor_tensor(xg[:, n % 6], v3[:, n % 2], xg[:, n % 6], ALU.add).then_inc(sum_done, 1)
                        if at.i % 3 == 0 and S.kind(at.i + 5) == "edge":
                            indices(at, 5)
                            gather(at.i + 5, 0)
                        if at.i % 3 == 1 and S.kind(at.i + 4) == "edge":
                            gather(at.i + 4, 1)
                    indices(Place(0), 2)
                    gather(2, 0)
                    gather(2, 1)
                    run_phase(pool, S, DEPTH2, body)
                    if res_e:
                        pool.wait_ge(normed, up(LS, *FULL))
                        for s in range(3):
                            last = max(n for n in range(LS) if n % 3 == s)
                            pool.wait_ge(stored[s], in_slot(last, 3, STORED))
                        for g in range(EG):
                            for j in range(J):
                                Q.indirect_dma_start(out=out, out_offset=bass.IndirectOffsetOnAxis(ap=out_idx[:, g, j:j + 1], axis=0),
                                                     in_=results[:, g, j, :], in_offset=None,
                                                     bounds_check=N - 1, oob_is_err=False).then_inc(scattered, 16)
                        pool.wait_ge(scattered, 16 * J * EG)

        inv_ready = sem("inv_half")
        inv_before = {"p2": 0, "p3": len(phase2.kinds) + DEPTH2 - 3}
        sage_phase(phase2, "p2", 0, wr0, wl0, 0, False)
        sage_phase(phase3, "p3", half, wr1, wl1, 1, True)


_INS = ['x', 'src', 'dst', 'edge_attr_128', 'L0_gnn_u', 'L0_gnn_W1', 'L0_gnn_b1', 'L0_gnn_g1', 'L0_gnn_be1', 'L0_gnn_W2',
        'L0_gnn_b2', 'L0_gnn_g2', 'L0_gnn_be2', 'L0_gnn_W3', 'L0_gnn_b3', 'L1_gnn_W_l0', 'L1_gnn_b_l0', 'L1_gnn_W_r0',
        'L1_gnn_W_l1', 'L1_gnn_b_l1', 'L1_gnn_W_r1']


def kernel(**inputs):
    import numpy as _np
    import concourse.bacc as _bacc
    from concourse import mybir as _mybir
    from concourse.bass_utils import run_bass_kernel_spmd as _run

    nc = _bacc.Bacc("TRN2", target_bir_lowering=False, num_devices=1)
    arrays, args = {}, {}
    for name in _INS:
        a = _np.ascontiguousarray(inputs[name])
        arrays[f"in_{name}_dram"] = a
        args[name] = nc.dram_tensor(f"in_{name}_dram", a.shape, _mybir.dt.from_np(a.dtype), kind="ExternalInput").ap()
    out = nc.dram_tensor("out_0_dram", arrays["in_x_dram"].shape, _mybir.dt.float32, kind="ExternalOutput").ap()
    build(nc, args, out)
    r = _run(nc, [arrays], core_ids=[0])
    return r.results[0]["out_0_dram"]
```
